# Optimizing a Trainium2 kernel written in Bass

```python
import numpy as np
import jax
import jax.numpy as jnp

def _softmax(x, axis=-1):
    return jax.nn.softmax(x, axis=axis)

def _gelu(x):
    return jax.nn.gelu(x, approximate=True)

def _silu(x):
    return jax.nn.silu(x)

def _sigmoid(x):
    return jax.nn.sigmoid(x)

def _layernorm(x, axis=-1, eps=1e-05):
    m = jnp.mean(x, axis=axis, keepdims=True)
    v = jnp.var(x, axis=axis, keepdims=True)
    return (x - m) / jnp.sqrt(v + eps)

def _scatter_add(tgt, idx, src, axis=0):
    return tgt.at[idx].add(src)

def _segment_sum(src, seg, n):
    return jax.ops.segment_sum(src, seg, n)
kernel_name = 'mk_recurrent_d2_jaxref_r4_09f4bf'

def setup_inputs(seed: int=0):
    np.random.seed(seed)
    _w = jnp.asarray

    def _L0_attn_setup():
        import jax, jax.numpy as jnp
        import numpy as np
        from jax import lax
        NUM_LEVELS = 2
        NUM_HEADS = 16
        LN_EPS = 1e-05
        ATTN_EPS = 1e-06

        def dwconv(x, filt):
            C = x.shape[-1]
            return lax.conv_general_dilated(x, filt[:, None, :], window_strides=(1,), padding='SAME', dimension_numbers=('NWC', 'WIO', 'NWC'), feature_group_count=C)

        def linear_attention(x, num_heads):
            B, N, C = x.shape
            d = C // num_heads
            h = x.reshape(B, N, num_heads, d)
            q = jax.nn.elu(h) + 1.0
            k = q
            v = h
            kv = jnp.einsum('bnhd,bnhe->bhde', k, v)
            z = k.sum(axis=1)
            num = jnp.einsum('bnhd,bhde->bnhe', q, kv)
            den = jnp.einsum('bnhd,bhd->bnh', q, z)[..., None] + ATTN_EPS
            return (num / den).reshape(B, N, C)

        def layer_norm(x, gamma, beta):
            mu = jnp.mean(x, axis=-1, keepdims=True)
            var = jnp.mean(jnp.square(x - mu), axis=-1, keepdims=True)
            return (x - mu) * lax.rsqrt(var + LN_EPS) * gamma + beta
        key = jax.random.key(seed)
        ks = jax.random.split(key, 7)
        B, S, C, K = (8, 1024, 256, 4)
        x = jax.random.normal(ks[0], (B, S, C), dtype=jnp.float32)
        scale = 1.0 / np.sqrt(K)
        h_filter = jax.random.normal(ks[1], (K, C), dtype=jnp.float32) * scale
        g_filter = jax.random.normal(ks[2], (K, C), dtype=jnp.float32) * scale
        h_synth = jax.random.normal(ks[3], (K, C), dtype=jnp.float32) * scale
        g_synth = jax.random.normal(ks[4], (K, C), dtype=jnp.float32) * scale
        norm_gamma = jnp.ones((C,), dtype=jnp.float32)
        norm_beta = jnp.zeros((C,), dtype=jnp.float32)
        return {'x': x, 'h_filter': h_filter, 'g_filter': g_filter, 'h_synth': h_synth, 'g_synth': g_synth, 'norm_gamma': norm_gamma, 'norm_beta': norm_beta}
    _L0_attn_in = _L0_attn_setup()

    def _L0_ffn_setup():
        import jax, jax.numpy as jnp
        import numpy as np
        D_IN, D_HID = (256, 1024)

        def _ternary(key, shape):
            return jax.random.randint(key, shape, -1, 2).astype(jnp.float32)

        def _tlin(x, w, s):
            return jnp.einsum('bsi,oi->bso', x, w) * s
        key = jax.random.key(seed)
        ks = jax.random.split(key, 12)
        inv = lambda fan: 1.0 / np.sqrt(fan).astype(np.float32)
        return {'x': jax.random.normal(ks[0], (4, 512, D_IN), dtype=jnp.float32), 'w1_w': _ternary(ks[1], (D_HID, D_IN)), 'w1_s': jax.random.uniform(ks[2], (D_HID,), dtype=jnp.float32) * inv(D_IN), 'w2_w': _ternary(ks[3], (D_HID, D_IN)), 'w2_s': jax.random.uniform(ks[4], (D_HID,), dtype=jnp.float32) * inv(D_IN), 'h1_w': _ternary(ks[5], (D_HID, D_HID)), 'h1_s': jax.random.uniform(ks[6], (D_HID,), dtype=jnp.float32) * inv(D_HID), 'h2_w': _ternary(ks[7], (D_HID, D_HID)), 'h2_s': jax.random.uniform(ks[8], (D_HID,), dtype=jnp.float32) * inv(D_HID), 'w3_w': _ternary(ks[9], (D_IN, D_HID)), 'w3_s': jax.random.uniform(ks[10], (D_IN,), dtype=jnp.float32) * inv(D_HID)}
    _L0_ffn_in = _L0_ffn_setup()

    def _L1_attn_setup():
        import jax, jax.numpy as jnp
        import numpy as np
        EPS = 1e-05
        H, N, F = (256, 16, 1024)

        def layernorm(x, g, b):
            mu = jnp.mean(x, axis=-1, keepdims=True)
            var = jnp.mean(jnp.square(x - mu), axis=-1, keepdims=True)
            return (x - mu) * jax.lax.rsqrt(var + EPS) * g + b

        def _selective_ssm(xn, delta, Bm, Cm, A, D):
            Bsz = xn.shape[0]
            xs = (jnp.moveaxis(delta, 1, 0), jnp.moveaxis(Bm, 1, 0), jnp.moveaxis(Cm, 1, 0), jnp.moveaxis(xn, 1, 0))

            def step(h, t):
                d_t, b_t, c_t, x_t = t
                dA = jnp.exp(d_t[:, :, None] * A)
                dBx = d_t[:, :, None] * b_t[:, None, :] * x_t[:, :, None]
                h = dA * h + dBx
                y = jnp.einsum('bhn,bn->bh', h, c_t)
                return (h, y)
            h0 = jnp.zeros((Bsz, H, N), xn.dtype)
            _, ys = jax.lax.scan(step, h0, xs)
            y = jnp.moveaxis(ys, 0, 1)
            return y + D * xn
        key = jax.random.key(seed)
        ks = jax.random.split(key, 12)
        B, L = (2, 512)
        s = lambda fan_in: 1.0 / np.sqrt(fan_in)
        inp = {'x': jax.random.normal(ks[0], (B, L, H), jnp.float32), 'ln1_g': jnp.ones((H,), jnp.float32), 'ln1_b': jnp.zeros((H,), jnp.float32), 'Wd': jax.random.uniform(ks[1], (H, H), jnp.float32, -s(H), s(H)), 'bd': jnp.zeros((H,), jnp.float32), 'Wbc': jax.random.uniform(ks[2], (2 * N, H), jnp.float32, -s(H), s(H)), 'bbc': jnp.zeros((2 * N,), jnp.float32), 'A_log': jnp.log(jnp.tile(jnp.arange(1, N + 1, dtype=jnp.float32), (H, 1))), 'D': jnp.ones((H,), jnp.float32), 'ln2_g': jnp.ones((H,), jnp.float32), 'ln2_b': jnp.zeros((H,), jnp.float32), 'W1': jax.random.uniform(ks[3], (F, H), jnp.float32, -s(H), s(H)), 'b1': jnp.zeros((F,), jnp.float32), 'W2': jax.random.uniform(ks[4], (H, F), jnp.float32, -s(F), s(F)), 'b2': jnp.zeros((H,), jnp.float32)}
        return inp
    _L1_attn_in = _L1_attn_setup()

    def _L1_ffn_setup():
        import jax, jax.numpy as jnp
        import numpy as np
        B, S, H, I, E, K = (4, 512, 256, 256, 8, 2)
        LIMIT = 7.0
        ALPHA = 1.702
        EPS = 1e-05
        key = jax.random.key(seed)
        ks = jax.random.split(key, 5)
        x = jax.random.normal(ks[0], (B, S, H), dtype=jnp.float32)
        norm_weight = jnp.ones((H,), dtype=jnp.float32)
        gate_weight = (jax.random.normal(ks[1], (E, H), dtype=jnp.float32) / np.sqrt(H)).astype(jnp.bfloat16)
        gate_bias = jnp.zeros((E,), dtype=jnp.bfloat16)
        mlp1_weight = (jax.random.normal(ks[2], (E, 2 * I, H), dtype=jnp.float32) / np.sqrt(H)).astype(jnp.bfloat16)
        mlp1_bias = jnp.zeros((E, 2 * I), dtype=jnp.bfloat16)
        mlp2_weight = (jax.random.normal(ks[3], (E, H, I), dtype=jnp.float32) / np.sqrt(I)).astype(jnp.bfloat16)
        mlp2_bias = jnp.zeros((E, H), dtype=jnp.bfloat16)
        return {'x': x, 'norm_weight': norm_weight, 'gate_weight': gate_weight, 'gate_bias': gate_bias, 'mlp1_weight': mlp1_weight, 'mlp1_bias': mlp1_bias, 'mlp2_weight': mlp2_weight, 'mlp2_bias': mlp2_bias}
    _L1_ffn_in = _L1_ffn_setup()
    _d = {'L0_attn_x': _L0_attn_in['x'], 'L0_attn_h_filter': _L0_attn_in['h_filter'], 'L0_attn_g_filter': _L0_attn_in['g_filter'], 'L0_attn_h_synth': _L0_attn_in['h_synth'], 'L0_attn_g_synth': _L0_attn_in['g_synth'], 'L0_attn_norm_gamma': _L0_attn_in['norm_gamma'], 'L0_attn_norm_beta': _L0_attn_in['norm_beta'], 'L0_ffn_w1_w': _L0_ffn_in['w1_w'], 'L0_ffn_w1_s': _L0_ffn_in['w1_s'], 'L0_ffn_w2_w': _L0_ffn_in['w2_w'], 'L0_ffn_w2_s': _L0_ffn_in['w2_s'], 'L0_ffn_h1_w': _L0_ffn_in['h1_w'], 'L0_ffn_h1_s': _L0_ffn_in['h1_s'], 'L0_ffn_h2_w': _L0_ffn_in['h2_w'], 'L0_ffn_h2_s': _L0_ffn_in['h2_s'], 'L0_ffn_w3_w': _L0_ffn_in['w3_w'], 'L0_ffn_w3_s': _L0_ffn_in['w3_s'], 'L1_attn_ln1_g': _L1_attn_in['ln1_g'], 'L1_attn_ln1_b': _L1_attn_in['ln1_b'], 'L1_attn_Wd': _L1_attn_in['Wd'], 'L1_attn_bd': _L1_attn_in['bd'], 'L1_attn_Wbc': _L1_attn_in['Wbc'], 'L1_attn_bbc': _L1_attn_in['bbc'], 'L1_attn_A_log': _L1_attn_in['A_log'], 'L1_attn_D': _L1_attn_in['D'], 'L1_attn_ln2_g': _L1_attn_in['ln2_g'], 'L1_attn_ln2_b': _L1_attn_in['ln2_b'], 'L1_attn_W1': _L1_attn_in['W1'], 'L1_attn_b1': _L1_attn_in['b1'], 'L1_attn_W2': _L1_attn_in['W2'], 'L1_attn_b2': _L1_attn_in['b2'], 'L1_ffn_norm_weight': _L1_ffn_in['norm_weight'], 'L1_ffn_gate_weight': _L1_ffn_in['gate_weight'], 'L1_ffn_gate_bias': _L1_ffn_in['gate_bias'], 'L1_ffn_mlp1_weight': _L1_ffn_in['mlp1_weight'], 'L1_ffn_mlp1_bias': _L1_ffn_in['mlp1_bias'], 'L1_ffn_mlp2_weight': _L1_ffn_in['mlp2_weight'], 'L1_ffn_mlp2_bias': _L1_ffn_in['mlp2_bias']}
    _x0 = _d['L0_attn_x']
    _d['L0_attn_x'] = jax.random.normal(jax.random.fold_in(jax.random.key(seed), 1), (4, 1024, 256), dtype=_x0.dtype)
    del _x0
    return _d

def reference(L0_attn_x, L0_attn_h_filter, L0_attn_g_filter, L0_attn_h_synth, L0_attn_g_synth, L0_attn_norm_gamma, L0_attn_norm_beta, L0_ffn_w1_w, L0_ffn_w1_s, L0_ffn_w2_w, L0_ffn_w2_s, L0_ffn_h1_w, L0_ffn_h1_s, L0_ffn_h2_w, L0_ffn_h2_s, L0_ffn_w3_w, L0_ffn_w3_s, L1_attn_ln1_g, L1_attn_ln1_b, L1_attn_Wd, L1_attn_bd, L1_attn_Wbc, L1_attn_bbc, L1_attn_A_log, L1_attn_D, L1_attn_ln2_g, L1_attn_ln2_b, L1_attn_W1, L1_attn_b1, L1_attn_W2, L1_attn_b2, L1_ffn_norm_weight, L1_ffn_gate_weight, L1_ffn_gate_bias, L1_ffn_mlp1_weight, L1_ffn_mlp1_bias, L1_ffn_mlp2_weight, L1_ffn_mlp2_bias):

    def _L0_attn_ref(x, h_filter, g_filter, h_synth, g_synth, norm_gamma, norm_beta):
        import jax, jax.numpy as jnp
        import numpy as np
        from jax import lax
        NUM_LEVELS = 2
        NUM_HEADS = 16
        LN_EPS = 1e-05
        ATTN_EPS = 1e-06

        def dwconv(x, filt):
            C = x.shape[-1]
            return lax.conv_general_dilated(x, filt[:, None, :], window_strides=(1,), padding='SAME', dimension_numbers=('NWC', 'WIO', 'NWC'), feature_group_count=C)

        def linear_attention(x, num_heads):
            B, N, C = x.shape
            d = C // num_heads
            h = x.reshape(B, N, num_heads, d)
            q = jax.nn.elu(h) + 1.0
            k = q
            v = h
            kv = jnp.einsum('bnhd,bnhe->bhde', k, v)
            z = k.sum(axis=1)
            num = jnp.einsum('bnhd,bhde->bnhe', q, kv)
            den = jnp.einsum('bnhd,bhd->bnh', q, z)[..., None] + ATTN_EPS
            return (num / den).reshape(B, N, C)

        def layer_norm(x, gamma, beta):
            mu = jnp.mean(x, axis=-1, keepdims=True)
            var = jnp.mean(jnp.square(x - mu), axis=-1, keepdims=True)
            return (x - mu) * lax.rsqrt(var + LN_EPS) * gamma + beta
        low = x
        highs = []
        lens = []
        for _ in range(NUM_LEVELS):
            lens.append(low.shape[1])
            l = dwconv(low, h_filter)[:, ::2]
            h = dwconv(low, g_filter)[:, ::2]
            highs.append(h)
            low = l
        low = linear_attention(low, NUM_HEADS)
        for h, L in zip(reversed(highs), reversed(lens)):
            up_l = jnp.repeat(low, 2, axis=1)[:, :L]
            up_h = jnp.repeat(h, 2, axis=1)[:, :L]
            low = dwconv(up_l, h_synth) + dwconv(up_h, g_synth)
        return layer_norm(x + low, norm_gamma, norm_beta)

    def _L0_ffn_ref(x, w1_w, w1_s, w2_w, w2_s, h1_w, h1_s, h2_w, h2_s, w3_w, w3_s):
        import jax, jax.numpy as jnp
        import numpy as np
        D_IN, D_HID = (256, 1024)

        def _ternary(key, shape):
            return jax.random.randint(key, shape, -1, 2).astype(jnp.float32)

        def _tlin(x, w, s):
            return jnp.einsum('bsi,oi->bso', x, w) * s
        h = jax.nn.silu(_tlin(x, w1_w, w1_s)) * _tlin(x, w2_w, w2_s)
        h = jax.nn.gelu(_tlin(h, h1_w, h1_s), approximate=False)
        h = jax.nn.gelu(_tlin(h, h2_w, h2_s), approximate=False)
        return _tlin(h, w3_w, w3_s)

    def _L1_attn_ref(x, ln1_g, ln1_b, Wd, bd, Wbc, bbc, A_log, D, ln2_g, ln2_b, W1, b1, W2, b2):
        import jax, jax.numpy as jnp
        import numpy as np
        EPS = 1e-05
        H, N, F = (256, 16, 1024)

        def layernorm(x, g, b):
            mu = jnp.mean(x, axis=-1, keepdims=True)
            var = jnp.mean(jnp.square(x - mu), axis=-1, keepdims=True)
            return (x - mu) * jax.lax.rsqrt(var + EPS) * g + b

        def _selective_ssm(xn, delta, Bm, Cm, A, D):
            Bsz = xn.shape[0]
            xs = (jnp.moveaxis(delta, 1, 0), jnp.moveaxis(Bm, 1, 0), jnp.moveaxis(Cm, 1, 0), jnp.moveaxis(xn, 1, 0))

            def step(h, t):
                d_t, b_t, c_t, x_t = t
                dA = jnp.exp(d_t[:, :, None] * A)
                dBx = d_t[:, :, None] * b_t[:, None, :] * x_t[:, :, None]
                h = dA * h + dBx
                y = jnp.einsum('bhn,bn->bh', h, c_t)
                return (h, y)
            h0 = jnp.zeros((Bsz, H, N), xn.dtype)
            _, ys = jax.lax.scan(step, h0, xs)
            y = jnp.moveaxis(ys, 0, 1)
            return y + D * xn
        xn = layernorm(x, ln1_g, ln1_b)
        delta = jax.nn.softplus(xn @ Wd.T + bd)
        bc = xn @ Wbc.T + bbc
        Bm, Cm = (bc[..., :N], bc[..., N:])
        A = -jnp.exp(A_log)
        ssm_out = x + _selective_ssm(xn, delta, Bm, Cm, A, D)
        normed = layernorm(ssm_out, ln2_g, ln2_b)
        hff = jax.nn.gelu(normed @ W1.T + b1, approximate=False)
        ffn_out = hff @ W2.T + b2
        return ffn_out + ssm_out

    def _L1_ffn_ref(x, norm_weight, gate_weight, gate_bias, mlp1_weight, mlp1_bias, mlp2_weight, mlp2_bias):
        import jax, jax.numpy as jnp
        import numpy as np
        B, S, H, I, E, K = (4, 512, 256, 256, 8, 2)
        LIMIT = 7.0
        ALPHA = 1.702
        EPS = 1e-05
        xc = x.astype(jnp.bfloat16)
        xf = xc.astype(jnp.float32)
        rms = jnp.mean(xf * xf, axis=-1, keepdims=True)
        normed = (xf * jax.lax.rsqrt(rms + EPS) * norm_weight).astype(jnp.bfloat16)
        nf = normed.astype(jnp.float32)
        logits = (jnp.einsum('bsh,eh->bse', nf, gate_weight.astype(jnp.float32)) + gate_bias.astype(jnp.float32)).astype(jnp.bfloat16).astype(jnp.float32)
        scores, idx = jax.lax.top_k(logits, K)
        w = jax.nn.softmax(scores, axis=-1)
        combine = jnp.sum(jax.nn.one_hot(idx, E, dtype=jnp.float32) * w[..., None], axis=-2)
        p1 = jnp.einsum('bsh,eoh->bseo', nf, mlp1_weight.astype(jnp.float32)) + mlp1_bias.astype(jnp.float32)
        g = jnp.minimum(p1[..., 0::2], LIMIT)
        lin = jnp.clip(p1[..., 1::2], -LIMIT, LIMIT)
        act = g * jax.nn.sigmoid(ALPHA * g) * (lin + 1.0)
        p2 = jnp.einsum('bsei,ehi->bseh', act, mlp2_weight.astype(jnp.float32)) + mlp2_bias.astype(jnp.float32)
        combined = jnp.einsum('bseh,bse->bsh', p2, combine)
        out = (xc + combined.astype(jnp.bfloat16)).astype(x.dtype)
        return out
    x = L0_attn_x
    xn = _layernorm(x, axis=-1)
    s = _L0_attn_ref(xn, L0_attn_h_filter, L0_attn_g_filter, L0_attn_h_synth, L0_attn_g_synth, L0_attn_norm_gamma, L0_attn_norm_beta)
    g = _silu(_L0_ffn_ref(xn, L0_ffn_w1_w, L0_ffn_w1_s, L0_ffn_w2_w, L0_ffn_w2_s, L0_ffn_h1_w, L0_ffn_h1_s, L0_ffn_h2_w, L0_ffn_h2_s, L0_ffn_w3_w, L0_ffn_w3_s))
    x = x + s * g
    xn = _layernorm(x, axis=-1)
    s = _L1_attn_ref(xn, L1_attn_ln1_g, L1_attn_ln1_b, L1_attn_Wd, L1_attn_bd, L1_attn_Wbc, L1_attn_bbc, L1_attn_A_log, L1_attn_D, L1_attn_ln2_g, L1_attn_ln2_b, L1_attn_W1, L1_attn_b1, L1_attn_W2, L1_attn_b2)
    g = _silu(_L1_ffn_ref(xn, L1_ffn_norm_weight, L1_ffn_gate_weight, L1_ffn_gate_bias, L1_ffn_mlp1_weight, L1_ffn_mlp1_bias, L1_ffn_mlp2_weight, L1_ffn_mlp2_bias))
    x = x + s * g
    return x

_drawn_inputs = setup_inputs


def setup_inputs(seed=0):
    import zlib

    import numpy as np

    out = dict(_drawn_inputs(seed))
    spreads = {'L0_attn_norm_gamma': (1.0, 0.2),
     'L0_attn_norm_beta': (0.0, 0.1),
     'L1_attn_ln1_g': (1.0, 0.2),
     'L1_attn_ln1_b': (0.0, 0.1),
     'L1_attn_bd': (0.0, 0.1),
     'L1_attn_bbc': (0.0, 0.1),
     'L1_attn_D': (1.0, 0.2),
     'L1_attn_ln2_g': (1.0, 0.2),
     'L1_attn_ln2_b': (0.0, 0.1),
     'L1_attn_b1': (0.0, 0.1),
     'L1_attn_b2': (0.0, 0.1),
     'L1_ffn_norm_weight': (1.0, 0.2)}
    factors = {}
    for name, (base, spread) in spreads.items():
        noise = np.random.default_rng([zlib.crc32(name.encode()), seed]).standard_normal(out[name].shape)
        drawn = base * np.exp(spread * noise) if base else spread * noise
        out[name] = jnp.asarray(drawn.astype(out[name].dtype))
    for name, factor in factors.items():
        out[name] = (out[name] * factor).astype(out[name].dtype)
    return out
```

```python
from contextlib import ExitStack

import concourse.bass as bass
from concourse import mybir

F32 = mybir.dt.float32
F32R = mybir.dt.float32r
F16 = mybir.dt.float16
BF16 = mybir.dt.bfloat16
ALU = mybir.AluOpType
ACT = mybir.ActivationFunctionType
AX_X = mybir.AxisListType.X

P = 128
B, L, D = 4, 1024, 256
KD = D // P
F = 1024
KF = F // P
N = 512
NC = L // N
NS = 16
E = 8
HEAD = 16
LN_EPS = 1e-5
ATTN_EPS = 1e-6
LIMIT = 7.0
ALPHA = 1.702
H_UP = 128.0
G_UP = 4.0
A_UP = 1024.0

PACK = {}
_at = 0
for _name, _width in (
    ("h_filter", 8), ("g_filter", 8), ("h_synth", 8), ("g_synth", 8), ("gamma", 2), ("beta", 2),
    ("w1_s", 8), ("w2_s", 8), ("h1_s", 8), ("h2_s", 8), ("w3_s", 2), ("ln1_g", 2), ("ln1_b", 2),
    ("bd", 2), ("A_log", 32), ("D", 2), ("ln2_g", 2), ("ln2_b", 2), ("b1", 8), ("b2", 2),
    ("norm_w", 2), ("bbc", 1),
):
    PACK[_name] = (_at, _at + _width)
    _at += _width
PACKED = _at


POOL_CONST = 14
DVE_CONST = 24
LE_STEPS = 13
GATE_STEPS = 20
ATTN_AT = 4


class Signal:

    def __init__(self, sem, layer, per, unit=1):
        self.sem, self.layer, self.per, self.unit = sem, layer, per, unit

    @property
    def batch(self):
        return self.per * self.unit

    @property
    def start(self):
        return (1 + self.layer) * self.batch

    def at(self, b, k):
        return (b + 1 + self.layer) * self.batch + k * self.unit


def build(nc, a):
    ctx = ExitStack()
    with ctx:
        def sb(name, shape, dt):
            return ctx.enter_context(nc.sbuf_tensor(name, shape, dt))

        w1 = sb("w1", [P, KD, F], F16)
        w2 = sb("w2", [P, KD, F], F16)
        h1w = sb("h1w", [P, KF, F], F16)
        h2w = sb("h2w", [P, KF, F], F16)
        w3 = sb("w3", [P, KF, D], F32R)
        wd = sb("wd", [P, KD, D], F32)
        wbc = sb("wbc", [P, KD, 64], F32)
        wf1 = sb("wf1", [P, KD, F], F32)
        wf2 = sb("wf2", [P, KF, D], F32)
        xn = sb("xn", [P, KD, L + 2], F32)
        xp = sb("xp", [P, 2, KD, N], F16)
        gx = sb("gx", [P, KD, L], F32)
        x2 = sb("x2", [P, KD, L], F32)
        xb = sb("xb", [P, KD, L], BF16)
        so = sb("so", [P, KD, L], F32)
        pk = sb("pk", [P, PACKED], F32)
        ident = sb("ident", [P, P], F32)
        meanw = sb("meanw", [P, P], F32)
        headmask = sb("headmask", [P, P], F32)
        sel = sb("sel", [64, 32], F32R)
        synth = sb("synth", [P, 2, KD, 5], F32)
        aneg = sb("aneg", [P, KD, NS], F32)
        s_h = sb("s_h", [P, KF], F32)
        s_g1 = sb("s_g1", [P, KF], F32)
        s_g2 = sb("s_g2", [P, KF], F32)
        mbias16 = sb("mbias16", [P, E, 2, KD], BF16)
        mbias = sb("mbias", [P, E, 2, KD], F32)
        lin_lo = sb("lin_lo", [P, E, KD], F32)
        lin_hi = sb("lin_hi", [P, E, KD], F32)
        lin_one = sb("lin_one", [P, E, KD], F32)
        b2s = sb("b2s", [64, D], F32R)
        wgate = sb("wgate", [P, KD, E], BF16)
        gbias = sb("gbias", [1, E], BF16)
        ones16 = sb("ones16", [1, P], BF16)
        rank = sb("rank", [P, 4, E], F32)
        eps = sb("eps", [P, 1], F32)
        carry = sb("carry", [P, KD, NS], F32)
        lg16 = sb("lg16", [P, 4, E], BF16)
        lg = sb("lg", [P, 4, E], F32)
        first = sb("first", [P, 4, E], F32)
        second = sb("second", [P, 4, E], F32)
        gtmp = sb("gtmp", [P, 4, E], F32)
        gm1 = sb("gm1", [P, 4], F32)
        gm2 = sb("gm2", [P, 4], F32)
        gix = sb("gix", [P, 4], F32)
        gex = sb("gex", [P, 4], F32)
        gw1 = sb("gw1", [P, 4], F32)
        gw2 = sb("gw2", [P, 4], F32)
        comb = sb("comb", [P, 4, 64], F32)

        R1, R2 = 51200, 43008

        def region(name, size):
            base = -(-nc.sbuf_base // 32) * 32
            sb(name, [P, size // 4], F32)

            def place(name, at, shape, dt):
                return nc.alloc_sbuf_tensor_at(name, shape, dt, offset=base + at)
            return place

        r1, r2 = region("region1", R1), region("region2", R2)
        hp = r1("hp", 0, [P, 2, KF, N], F16)
        g1p = r1("g1p", 16384, [P, 2, KF, N], F16)
        g2p = r1("g2p", 32768, [P, 2, 2, N], F32R)
        sa = r1("sa", 40960, [P, 2, N], F32)
        tf = r1("tf", 45056, [P, 2, N], F32)
        sq0 = r1("sq0", 40960, [P, KD, N], F32)
        rs0 = r1("rs0", 49152, [P, N], F32)
        l1b = r1("l1b", 0, [P, KD, N + 2], F32)
        h1b = r1("h1b", 4352, [P, KD, N + 2], F32)
        l2 = r1("l2", 8704, [P, KD, N // 2], F32)
        h2b = r1("h2b", 10752, [P, KD, N // 2 + 2], F32)
        q0 = r1("q0", 12928, [P, KD, N // 2], F32)
        qe = r1("qe", 14976, [P, KD, N // 2], F32)
        low2 = r1("low2", 17024, [P, KD, N // 2 + 2], F32)
        low1 = r1("low1", 19200, [P, KD, N + 2], F32)
        qt = r1("qt", 23424, [P, 2, D], F32)
        vt = r1("vt", 25472, [P, 2, D], F32)
        kvm = r1("kvm", 27520, [P, KD, P], F32)
        zm = r1("zm", 28544, [P, KD, P], F32)
        rden = r1("rden", 29568, [P, KD, N // 2], F32)
        zs = r1("zs", 31616, [P, KD], F32)
        y0 = r1("y0", 32768, [P, KD, L], F32)
        sqb = r1("sqb", 40960, [P, KD, N], F32)
        rsb = r1("rsb", 45056, [P, N], F32)
        xr = r1("xr", 47104, [P, KD, N], F32)
        gmin = r1("gmin", 0, [P, 2, N], F32)
        sg = r1("sg", 4096, [P, 2, N], F32)
        lin = r1("lin", 8192, [P, 2, N], F32)
        sc = r1("sc", 12288, [P, 2, N], F32)
        af = r1("af", 16384, [P, 2, N], F32)
        ap2 = r1("ap2", 20480, [P, 2, 2, N], F16)
        sqm = r1("sqm", 24576, [P, KD, N], F32)
        rsm = r1("rsm", 28672, [P, N], F32)
        cs = r1("cs", 30720, [64, N], F32R)
        ct = r1("ct", 4096, [64, N], F32)
        xrms = r1("xrms", 0, [P, KD, N], F32)
        moe16 = r1("moe16", 0, [P, KD, N], BF16)
        sum16 = r1("sum16", 2048, [P, KD, N], BF16)
        gate1 = r1("gate1", 4096, [P, KD, N], F32)
        outc = r1("outc", 8192, [P, KD, N], F32)
        da = r2("da", 0, [P, 4, KD, N], F32)
        u = r2("u", 16384, [P, 4, KD, N], F32)
        delta = r2("delta", 32768, [P, KD, N], F32)
        dx = r2("dx", 36864, [P, KD, N], F32)
        bcs = r2("bcs", 40960, [64, N], F32R)
        zt = r2("zt", 0, [P, KD, N], F32)
        lt = r2("lt", 4096, [P, KD, N], F32)
        v1 = r2("v1", 8192, [P, N], F32)
        bcf = r2("bcf", 10240, [64, N], F32)
        xc = r2("xc", 16384, [P, KD, N], F32)
        sq1 = r2("sq1", 20480, [P, KD, N], F32)
        xn1 = r2("xn1", 24576, [P, KD, N], F32)
        rs1 = r2("rs1", 28672, [P, N], F32)
        rs2 = r2("rs2", 30720, [P, N], F32)
        nrm = r2("nrm", 0, [P, NC, KD, N], F32)
        sq2 = r2("sq2", 8192, [P, KD, N], F32)
        rs3 = r2("rs3", 12288, [P, N], F32)
        hff = r2("hff", 14336, [P, 2, N], F32)
        cb = r2("cb", 0, [P, E, N], F32)
        nf = r2("nf", 16384, [P, KD, N], BF16)
        mw1 = r2("mw1", 18432, [P, E, KD, 2, D], BF16)
        mw2 = r2("mw2", 34816, [P, E, KD, D], BF16)

        def ps(name):
            return ctx.enter_context(nc.psum_tensor(name, [P, 2, N], F32))

        psy, psb, psf, psg = ps("psy"), ps("psb"), ps("psf"), ps("psg")

        def col(name, k=0, w=1):
            lo, hi = PACK[name]
            return pk[:, lo + k:lo + k + w]

        def both(t):
            return t.rearrange("p (o n) -> p o n", o=1).broadcast_to([P, KD, t.shape[-1]])

        def last8(t):
            return t.rearrange("p (j o) -> p j o", o=1).broadcast_to([P, 4, E])

        signals = []
        layer = 0

        def sig(name, per, unit=1):
            s = Signal(ctx.enter_context(nc.semaphore(name)), layer, per, unit)
            signals.append(s)
            return s

        def one(name):
            return ctx.enter_context(nc.semaphore(name))

        packs_in = one("packs_in")
        w12_in = one("w12_in")
        h1_in = one("h1_in")
        h2_in = one("h2_in")
        w3_in = one("w3_in")
        wl1_in = one("wl1_in")
        b2_in = one("b2_in")
        pool_const = one("pool_const")
        dve_const = one("dve_const")
        act_const = one("act_const")
        b2s_zero = one("b2s_zero")
        x_in = [sig(f"x_in{c}", 1, 16) for c in range(NC)]
        li_mean = sig("li_mean", NC)
        li_cen = sig("li_cen", NC)
        li_sq = sig("li_sq", NC)
        li_var = sig("li_var", NC)
        li_std = sig("li_std", NC)
        li_rstd = sig("li_rstd", NC)
        li_xn = sig("li_xn", NC)
        li_hi = sig("li_hi", NC)
        li_lo = sig("li_lo", NC)
        ab_mm = sig("ab_mm", NC * KF)
        silu_a = sig("silu_a", NC * KF)
        h_f = sig("h_f", NC * KF)
        h_hi = sig("h_hi", NC * KF)
        h_lo = sig("h_lo", NC * KF)
        g1_mm = sig("g1_mm", NC * KF)
        g1_f = sig("g1_f", NC * KF)
        g1_hi = sig("g1_hi", NC * KF)
        g1_lo = sig("g1_lo", NC * KF)
        g2_mm = sig("g2_mm", NC * KF)
        g2_f = sig("g2_f", NC * KF)
        g2_hi = sig("g2_hi", NC * KF)
        g2_lo = sig("g2_lo", NC * KF)
        w3_mm = sig("w3_mm", NC * KF)
        gate0 = sig("gate0", NC)
        conv = sig("conv", 88)
        q_min = sig("q_min", 1)
        q_exp = sig("q_exp", 1)
        q_done = sig("q_done", 1)
        turned = sig("turned", 1)
        qt_done = sig("qt_done", 1)
        vt_done = sig("vt_done", 1)
        kv_mm = sig("kv_mm", 1)
        kv_masked = sig("kv_masked", 1)
        num_mm = sig("num_mm", 1)
        y_done = sig("y_done", 1)
        lb_mean = sig("lb_mean", NC)
        lb_cen = sig("lb_cen", NC)
        lb_sq = sig("lb_sq", NC)
        lb_var = sig("lb_var", NC)
        lb_std = sig("lb_std", NC)
        lb_step = sig("lb_step", 4 * NC)
        xr_in = sig("xr_in", NC, 16)
        gy = sig("gy", NC)
        x2n = sig("x2n", NC)
        layer = 1
        le_copy = sig("le_copy", NC)
        le_mean = sig("le_mean", NC)
        le_cen = sig("le_cen", NC)
        le_sq = sig("le_sq", NC)
        le_var = sig("le_var", NC)
        le_std = sig("le_std", NC)
        le_step = sig("le_step", LE_STEPS * NC)
        le_std1 = sig("le_std1", NC)
        le_xb = sig("le_xb", NC)
        dt_mm = sig("dt_mm", NC)
        bc_mm = sig("bc_mm", NC)
        z_done = sig("z_done", NC)
        z_abs = sig("z_abs", NC)
        z_exp = sig("z_exp", NC)
        z_ln = sig("z_ln", NC)
        head_done = sig("head_done", NC)
        b_mm = sig("b_mm", NC * NS)
        c_mm = sig("c_mm", NC * NS)
        da_done = sig("da_done", NC * NS)
        u_done = sig("u_done", NC * NS)
        scan_done = sig("scan_done", NC * NS)
        carried = sig("carried", NS)
        cy_done = sig("cy_done", NC * NS)
        pair_done = sig("pair_done", NC * NS // 2)
        y_acc = sig("y_acc", NC * NS // 2)
        ssm_done = sig("ssm_done", NC)
        lf_mean = sig("lf_mean", NC)
        lf_cen = sig("lf_cen", NC)
        lf_sq = sig("lf_sq", NC)
        lf_var = sig("lf_var", NC)
        lf_std = sig("lf_std", NC)
        lf_step = sig("lf_step", 3 * NC)
        f1_mm = sig("f1_mm", NC * KF)
        f1_done = sig("f1_done", NC * KF)
        f2_mm = sig("f2_mm", NC * KF)
        block_done = sig("block_done", NC)
        mw_in = sig("mw_in", 2, 16)
        m_sq = sig("m_sq", NC)
        m_ms = sig("m_ms", NC)
        m_rms = sig("m_rms", NC)
        m_step = sig("m_step", 2 * NC)
        nf_done = sig("nf_done", NC)
        gate_mm = sig("gate_mm", NC)
        gate_step = sig("gate_step", GATE_STEPS * NC)
        gate_d = sig("gate_d", NC)
        gate_e = sig("gate_e", NC)
        comb_done = sig("comb_done", NC)
        comb_t = sig("comb_t", NC)
        ct_done = sig("ct_done", 2 * NC)
        cs_done = sig("cs_done", NC)
        cb_mm = sig("cb_mm", NC * E)
        cb_done = sig("cb_done", NC * E)
        Q = NC * E * KD
        p1_mm = sig("p1_mm", Q)
        gmin_done = sig("gmin_done", Q)
        lin_done = sig("lin_done", Q)
        sg_done = sig("sg_done", Q)
        sc_done = sig("sc_done", Q)
        af_done = sig("af_done", Q)
        ahi_done = sig("ahi_done", Q)
        alo_done = sig("alo_done", Q)
        p2_mm = sig("p2_mm", Q)
        moe_r = sig("moe_r", NC)
        moe_s = sig("moe_s", NC)
        moe_g = sig("moe_g", NC)
        out_m = sig("out_m", NC)
        out_ready = sig("out_ready", NC)
        out_sent = sig("out_sent", NC, 16)

        arrived = one("arrived")
        released = {e: one(f"released_{e}") for e in ("pool", "act", "pe", "dve")}

        def next_turn(engine, name):
            engine.sem_inc(arrived, 1)
            engine.wait_ge(released[name], 1)
            engine.sem_inc(released[name], -1)

        block = ctx.enter_context(nc.Block())

        def chunk(t, c):
            return t[:, :, c * N:(c + 1) * N]

        def xn_chunk(c):
            return xn[:, :, 1 + c * N:1 + (c + 1) * N]

        def tasks(step):
            return range(step * 3 * KF // NS, (step + 1) * 3 * KF // NS)

        @block.sync
        def _(sp):
            for s in signals:
                sp.sem_inc(s.sem, s.start)

            def load_x(b, row):
                for c in range(NC):
                    sp.wait_ge(y_done.sem, y_done.at(b - 1, 1))
                    sp.dma_start(xn_chunk(c), a["x"][row][:, :, c * N:(c + 1) * N]).then_inc(x_in[c].sem, 16)

            def load_experts(b):
                sp.wait_ge(ssm_done.sem, ssm_done.at(b, NC))
                sp.dma_start(mw1[:], a["mlp1_w"]).then_inc(mw_in.sem, 16)
                sp.dma_start(mw2[:], a["mlp2_w"]).then_inc(mw_in.sem, 16)

            def load_residual(b, row):
                for c in range(NC):
                    sp.wait_ge(gate0.sem, gate0.at(b, NC))
                    sp.wait_ge(x2n.sem, x2n.at(b, c))
                    sp.dma_start(xr[:], a["x"][row][:, :, c * N:(c + 1) * N]).then_inc(xr_in.sem, 16)

            def store_out(b, row):
                for c in range(NC):
                    sp.wait_ge(out_ready.sem, out_ready.at(b, c + 1))
                    sp.dma_start(a["out"][row][:, :, c * N:(c + 1) * N], outc[:]).then_inc(out_sent.sem, 16)

            sp.dma_start(pk[:], a["pack"]).then_inc(packs_in, 16)
            load_x(0, 0)
            sp.dma_start(wf1[:], a["wf1"]).then_inc(wl1_in, 16)
            sp.dma_start(wf2[:], a["wf2"]).then_inc(wl1_in, 16)
            sp.dma_start(wd[:], a["wd"]).then_inc(wl1_in, 16)
            sp.dma_start(wbc[:], a["wbc"]).then_inc(wl1_in, 16)
            sp.dma_start(mbias16[:], a["mlp1_b"]).then_inc(packs_in, 16)
            sp.dma_start(wgate[:], a["gate_w"]).then_inc(packs_in, 16)
            sp.dma_start(gbias[:], a["gate_b"]).then_inc(packs_in, 16)

            def turn(row, last=False):
                load_experts(-1)
                load_residual(0, row)
                if not last:
                    load_x(1, row + 1)
                store_out(-1, row - 1)

            def take_down():
                sp.wait_ge(arrived, len(released))
                sp.sem_inc(arrived, -len(released))
                for s in signals:
                    sp.sem_inc(s.sem, -s.batch)
                for s in released.values():
                    sp.sem_inc(s, 1)

            load_residual(0, 0)
            load_x(1, 1)
            take_down()
            with sp.Fori(0, B - 2) as i:
                turn(i + 1)
                take_down()
            turn(B - 1, last=True)
            take_down()
            load_experts(-1)
            store_out(-1, B - 1)
            sp.wait_ge(out_sent.sem, out_sent.at(-1, NC))

        @block.gpsimd
        def _(pool):
            pool.dma_start(w1[:], a["w1"]).then_inc(w12_in, 16)
            pool.dma_start(w2[:], a["w2"]).then_inc(w12_in, 16)
            pool.dma_start(h1w[:], a["h1"]).then_inc(h1_in, 16)
            pool.dma_start(h2w[:], a["h2"]).then_inc(h2_in, 16)
            pool.dma_start(w3[:], a["w3"]).then_inc(w3_in, 16)
            pool.wait_ge(b2s_zero, 1)
            pool.dma_start(b2s[0:E, :], a["mlp2_b"]).then_inc(b2_in, 16)
            pool.dma_start(b2s[32:32 + E, :], a["mlp2_b"]).then_inc(b2_in, 16)
            k = 0

            def const(ins):
                nonlocal k
                k += 1
                ins.then_inc(pool_const, 1)
                pool.wait_ge(pool_const, k)

            const(pool.memset(ident[:], 0.0))
            const(pool.affine_select(out=ident[:], in_=ident[:], compare_op=ALU.not_equal, fill=1.0,
                                     base=0, pattern=[[-1, P]], channel_multiplier=1))
            const(pool.memset(headmask[:], 1.0))
            hm = headmask[:].rearrange("p (h d) -> p h d", d=HEAD)
            const(pool.affine_select(out=hm, in_=hm, compare_op=ALU.is_ge, fill=0.0, base=0,
                                     pattern=[[-HEAD, P // HEAD], [0, HEAD]], channel_multiplier=1))
            const(pool.affine_select(out=hm, in_=hm, compare_op=ALU.is_ge, fill=0.0, base=HEAD - 1,
                                     pattern=[[HEAD, P // HEAD], [0, HEAD]], channel_multiplier=-1))
            for e in range(E):
                const(pool.memset(rank[:, :, e:e + 1], float(E - e)))
            const(pool.memset(comb[:], 0.0))
            assert k == POOL_CONST

            def l0_low(b, c):
                pool.wait_ge(li_hi.sem, li_hi.at(b, c + 1))
                pool.tensor_tensor(xp[:, 1], xn_chunk(c), xp[:, 0], ALU.subtract).then_inc(li_lo.sem, 1)

            def ffn_task(b, c, task):
                kind, m = divmod(task, KF)
                k = c * KF + m
                if kind == 0:
                    pool.wait_ge(h_hi.sem, h_hi.at(b, k + 1))
                    pool.tensor_tensor(hp[:, 1, m], tf[:, m % 2], hp[:, 0, m], ALU.subtract)\
                        .then_inc(h_lo.sem, 1)
                elif kind == 2:
                    pool.wait_ge(g2_hi.sem, g2_hi.at(b, k + 1))
                    pool.tensor_tensor(g2p[:, m % 2, 1], tf[:, m % 2], g2p[:, m % 2, 0].bitcast(F32),
                                       ALU.subtract).then_inc(g2_lo.sem, 1)

            def state_pair(b, c, n):
                k = c * NS + n
                pool.wait_ge(cy_done.sem, cy_done.at(b, k + 2))
                pool.tensor_tensor(u[:, n % 4], u[:, n % 4], u[:, (n + 1) % 4], ALU.add)\
                    .then_inc(pair_done.sem, 1)

            def l0_out(b, c):
                pool.wait_ge(lb_step.sem, lb_step.at(b, 4 * (c + 1)))
                pool.tensor_tensor(chunk(gx, c), chunk(y0, c), chunk(gx, c), ALU.mult).then_inc(gy.sem, 1)
                pool.wait_ge(gy.sem, gy.at(b, c + 1))
                pool.wait_ge(xr_in.sem, xr_in.at(b, c + 1))
                pool.tensor_tensor(chunk(gx, c), chunk(gx, c), xr[:], ALU.add).then_inc(x2n.sem, 1)

            def expert_weighted(b, c, q):
                k = c * E * KD + q
                pool.wait_ge(sg_done.sem, sg_done.at(b, k + 1))
                pool.wait_ge(cb_done.sem, cb_done.at(b, c * E + q // KD + 1))
                pool.wait_ge(af_done.sem, af_done.at(b, k - 1))
                pool.tensor_tensor(sc[:, q % 2], sg[:, q % 2], cb[:, q // KD], ALU.mult)\
                    .then_inc(sc_done.sem, 1)

            def expert_low(b, c, q):
                k = c * E * KD + q
                pool.wait_ge(ahi_done.sem, ahi_done.at(b, k + 1))
                pool.tensor_tensor(ap2[:, q % 2, 1], af[:, q % 2], ap2[:, q % 2, 0], ALU.subtract)\
                    .then_inc(alo_done.sem, 1)

            def expert_out(b, c):
                pool.wait_ge(moe_g.sem, moe_g.at(b, c + 1))
                pool.wait_ge(block_done.sem, block_done.at(b, c + 1))
                pool.wait_ge(out_sent.sem, out_sent.at(b, c))
                pool.tensor_tensor(outc[:], chunk(so, c), gate1[:], ALU.mult).then_inc(out_m.sem, 1)
                pool.wait_ge(out_m.sem, out_m.at(b, c + 1))
                pool.tensor_tensor(outc[:], outc[:], chunk(x2, c), ALU.add).then_inc(out_ready.sem, 1)

            def batch(b0, b1):
                for c in range(NC):
                    if b0 is not None:
                        l0_low(b0, c)
                    for n in range(NS):
                        if b0 is not None:
                            for task in tasks(n):
                                ffn_task(b0, c, task)
                        if b1 is not None and n % 2 == 1:
                            state_pair(b1, c, n - 1)
                if b0 is not None:
                    for c in range(NC):
                        l0_out(b0, c)
                if b1 is not None:
                    for c in range(NC):
                        for q in range(E * KD + 1):
                            if q < E * KD:
                                expert_weighted(b1, c, q)
                            if q >= 1:
                                expert_low(b1, c, q - 1)
                        expert_out(b1, c)

            batch(0, None)
            next_turn(pool, "pool")
            with pool.Fori(0, B - 1):
                batch(0, -1)
                next_turn(pool, "pool")
            batch(None, -1)

        @block.scalar
        def _(act):
            act.wait_ge(packs_in, 16 * 4)
            lo, hi = PACK["A_log"]
            act.activation(aneg[:], pk[:, lo:hi].rearrange("p (t n) -> p t n", t=KD), ACT.Exp)\
                .then_inc(act_const, 1)

            def split_input(b, c):
                act.wait_ge(li_xn.sem, li_xn.at(b, c + 1))
                act.wait_ge(ab_mm.sem, ab_mm.at(b, c * KF))
                act.activation(xp[:, 0], xn_chunk(c), ACT.Copy).then_inc(li_hi.sem, 1)

            def l0_square(b, c):
                act.wait_ge(li_cen.sem, li_cen.at(b, c + 1))
                if c == 0:
                    act.wait_ge(lb_var.sem, lb_var.at(b - 1, NC))
                    act.wait_ge(x2n.sem, x2n.at(b - 1, NC))
                else:
                    act.wait_ge(h_f.sem, h_f.at(b, c * KF))
                    act.wait_ge(g2_lo.sem, g2_lo.at(b, c * KF))
                act.activation(sq0[:], xn_chunk(c), ACT.Square).then_inc(li_sq.sem, 1)

            def l0_std(b, c):
                act.wait_ge(li_var.sem, li_var.at(b, c + 1))
                act.activation(rs0[:], psf[:, 1], ACT.Sqrt, bias=eps[:]).then_inc(li_std.sem, 1)

            def ffn_task(b, c, task):
                kind, m = divmod(task, KF)
                k = c * KF + m
                if kind == 0:
                    bank = psf if m % 2 == 0 else psg
                    act.wait_ge(ab_mm.sem, ab_mm.at(b, k + 1))
                    act.wait_ge(h_f.sem, h_f.at(b, k - 1))
                    act.activation(sa[:, m % 2], bank[:, 0], ACT.Silu, scale=col("w1_s", m))\
                        .then_inc(silu_a.sem, 1)
                    act.wait_ge(h_f.sem, h_f.at(b, k + 1))
                    if m == 0:
                        act.wait_ge(g1_mm.sem, g1_mm.at(b, c * KF))
                        act.wait_ge(out_sent.sem, out_sent.at(b - 2, NC))
                    act.activation(hp[:, 0, m], tf[:, m % 2], ACT.Copy).then_inc(h_hi.sem, 1)
                elif kind == 1:
                    act.wait_ge(g1_mm.sem, g1_mm.at(b, k + 1))
                    if m < 2:
                        act.wait_ge(h_lo.sem, h_lo.at(b, c * KF + KF))
                    else:
                        act.wait_ge(g1_lo.sem, g1_lo.at(b, k - 1))
                    act.activation(tf[:, m % 2], psf[:, m % 2], ACT.Gelu, scale=s_g1[:, m:m + 1])\
                        .then_inc(g1_f.sem, 1)
                    act.wait_ge(g1_f.sem, g1_f.at(b, k + 1))
                    if m == 0:
                        act.wait_ge(g2_mm.sem, g2_mm.at(b, c * KF))
                    act.activation(g1p[:, 0, m], tf[:, m % 2], ACT.Copy, scale=G_UP).then_inc(g1_hi.sem, 1)
                else:
                    act.wait_ge(g2_mm.sem, g2_mm.at(b, k + 1))
                    if m < 2:
                        act.wait_ge(g1_lo.sem, g1_lo.at(b, c * KF + KF))
                    else:
                        act.wait_ge(g2_lo.sem, g2_lo.at(b, k - 1))
                    act.activation(tf[:, m % 2], psf[:, m % 2], ACT.Gelu, scale=s_g2[:, m:m + 1])\
                        .then_inc(g2_f.sem, 1)
                    act.wait_ge(g2_f.sem, g2_f.at(b, k + 1))
                    act.wait_ge(w3_mm.sem, w3_mm.at(b, k - 1))
                    act.activation(g2p[:, m % 2, 0], tf[:, m % 2], ACT.Copy).then_inc(g2_hi.sem, 1)

            def l0_gate(b, c):
                act.wait_ge(w3_mm.sem, w3_mm.at(b, (c + 1) * KF))
                act.wait_ge(le_mean.sem, le_mean.at(b - 1, c + 1))
                act.wait_ge(le_cen.sem, le_cen.at(b - 1, c + 1))
                for t in range(KD):
                    last = act.activation(gx[:, t, c * N:(c + 1) * N], psg[:, t], ACT.Silu,
                                          scale=col("w3_s", t))
                last.then_inc(gate0.sem, 1)

            def q_expo(b):
                act.wait_ge(q_min.sem, q_min.at(b, 1))
                act.activation(qe[:], qe[:], ACT.Exp).then_inc(q_exp.sem, 1)

            def turn_copy(b):
                act.wait_ge(turned.sem, turned.at(b, 1))
                act.activation(qt[:], psf[:, 0].rearrange("p (j c) -> p j c", j=2), ACT.Copy)\
                    .then_inc(qt_done.sem, 1)
                act.activation(vt[:], psf[:, 1].rearrange("p (j c) -> p j c", j=2), ACT.Copy)\
                    .then_inc(vt_done.sem, 1)

            def lb_square(b, c):
                act.wait_ge(lb_cen.sem, lb_cen.at(b, c + 1))
                act.wait_ge(lb_var.sem, lb_var.at(b, c))
                act.activation(sqb[:], chunk(y0, c), ACT.Square).then_inc(lb_sq.sem, 1)

            def lb_root(b, c):
                act.wait_ge(lb_var.sem, lb_var.at(b, c + 1))
                act.wait_ge(lb_step.sem, lb_step.at(b, 4 * c))
                act.activation(rsb[:], psf[:, 1], ACT.Sqrt, bias=eps[:]).then_inc(lb_std.sem, 1)

            def head_copy(b, c):
                act.wait_ge(x2n.sem, x2n.at(b, c + 1))
                act.wait_ge(out_ready.sem, out_ready.at(b - 1, c + 1))
                act.activation(chunk(x2, c), chunk(gx, c), ACT.Copy).then_inc(le_copy.sem, 1)

            def head_square(b, c):
                act.wait_ge(le_cen.sem, le_cen.at(b, c + 1))
                act.activation(sq1[:], xc[:], ACT.Square).then_inc(le_sq.sem, 1)

            def head_root(b, c):
                act.wait_ge(le_var.sem, le_var.at(b, c + 1))
                act.activation(rs1[:], psy[:, 1], ACT.Sqrt, bias=eps[:]).then_inc(le_std.sem, 1)

            def head_root1(b, c):
                act.wait_ge(le_step.sem, le_step.at(b, LE_STEPS * c + 3))
                act.activation(rs2[:], v1[:], ACT.Sqrt, bias=eps[:]).then_inc(le_std1.sem, 1)

            def head_b16(b, c):
                act.wait_ge(le_step.sem, le_step.at(b, LE_STEPS * c + 4))
                act.activation(chunk(xb, c), xc[:], ACT.Copy).then_inc(le_xb.sem, 1)

            def softplus(b, c):
                act.wait_ge(z_done.sem, z_done.at(b, c + 1))
                act.activation(lt[:], zt[:], ACT.Abs).then_inc(z_abs.sem, 1)
                act.wait_ge(z_abs.sem, z_abs.at(b, c + 1))
                act.activation(lt[:], lt[:], ACT.Exp, scale=-1.0).then_inc(z_exp.sem, 1)
                act.wait_ge(z_exp.sem, z_exp.at(b, c + 1))
                act.activation(lt[:], lt[:], ACT.Ln, bias=1.0).then_inc(z_ln.sem, 1)

            def decay(b, c, n):
                k = c * NS + n
                if n == 0:
                    act.wait_ge(head_done.sem, head_done.at(b, c + 1))
                act.wait_ge(scan_done.sem, scan_done.at(b, k - 3))
                for t in range(KD):
                    last = act.activation(da[:, n % 4, t], delta[:, t], ACT.Exp, scale=aneg[:, t, n:n + 1])
                last.then_inc(da_done.sem, 1)

            def lf_square(b, c):
                act.wait_ge(lf_cen.sem, lf_cen.at(b, c + 1))
                act.wait_ge(lf_var.sem, lf_var.at(b, c))
                act.activation(sq2[:], nrm[:, c], ACT.Square).then_inc(lf_sq.sem, 1)

            def lf_root(b, c):
                act.wait_ge(lf_var.sem, lf_var.at(b, c + 1))
                act.wait_ge(lf_step.sem, lf_step.at(b, 3 * c))
                act.activation(rs3[:], psb[:, 1], ACT.Sqrt, bias=eps[:]).then_inc(lf_std.sem, 1)

            def hidden1(b, c, m):
                k = c * KF + m
                act.wait_ge(f1_mm.sem, f1_mm.at(b, k + 1))
                act.wait_ge(f2_mm.sem, f2_mm.at(b, k - 1))
                act.activation(hff[:, m % 2], psy[:, m % 2], ACT.Gelu, bias=col("b1", m))\
                    .then_inc(f1_done.sem, 1)

            def expert_square(b, c):
                if c == 0:
                    act.wait_ge(le_xb.sem, le_xb.at(b, NC))
                act.activation(sqm[:], chunk(xb, c), ACT.Square).then_inc(m_sq.sem, 1)

            def expert_root(b, c):
                act.wait_ge(m_ms.sem, m_ms.at(b, c + 1))
                act.activation(rsm[:], psy[:, 0], ACT.Sqrt, bias=eps[:]).then_inc(m_rms.sem, 1)

            def gate_exp(b, c):
                act.wait_ge(gate_d.sem, gate_d.at(b, c + 1))
                act.activation(gex[:], gex[:], ACT.Exp).then_inc(gate_e.sem, 1)

            def gate_copy(b, c, e):
                k = c * E + e
                act.wait_ge(cb_mm.sem, cb_mm.at(b, k + 1))
                act.activation(cb[:, e], psy[:, e % 2], ACT.Copy, scale=1.0 / ALPHA).then_inc(cb_done.sem, 1)

            def expert_silu(b, c, q):
                k = c * E * KD + q
                act.wait_ge(gmin_done.sem, gmin_done.at(b, k + 1))
                act.wait_ge(sc_done.sem, sc_done.at(b, k - 1))
                act.activation(sg[:, q % 2], gmin[:, q % 2], ACT.Silu, scale=ALPHA).then_inc(sg_done.sem, 1)

            def expert_high(b, c, q):
                k = c * E * KD + q
                act.wait_ge(af_done.sem, af_done.at(b, k + 1))
                act.wait_ge(p2_mm.sem, p2_mm.at(b, k - 1))
                act.activation(ap2[:, q % 2, 0], af[:, q % 2], ACT.Copy).then_inc(ahi_done.sem, 1)

            def expert_gate(b, c):
                act.wait_ge(moe_s.sem, moe_s.at(b, c + 1))
                act.activation(gate1[:], sum16[:], ACT.Silu).then_inc(moe_g.sem, 1)

            def batch(b0, b1):
                for c in range(NC):
                    if b1 is not None:
                        head_copy(b1, c)
                    if b0 is not None:
                        l0_square(b0, c)
                    if b1 is not None:
                        head_square(b1, c)
                    if b0 is not None:
                        l0_std(b0, c)
                    if b1 is not None:
                        head_root(b1, c)
                        head_root1(b1, c)
                    if b0 is not None:
                        split_input(b0, c)
                    if b1 is not None:
                        head_b16(b1, c)
                        softplus(b1, c)
                        decay(b1, c, 0)
                        decay(b1, c, 1)
                    for n in range(NS):
                        if b1 is not None and n % 2 == 0 and n + 2 < NS:
                            decay(b1, c, n + 2)
                            decay(b1, c, n + 3)
                        if b0 is not None:
                            for task in tasks(n):
                                ffn_task(b0, c, task)
                    if b0 is not None:
                        l0_gate(b0, c)
                if b1 is not None:
                    for c in range(NC):
                        lf_square(b1, c)
                        lf_root(b1, c)
                if b1 is None:
                    q_expo(b0)
                    turn_copy(b0)
                else:
                    for c in range(NC):
                        for m in range(KF):
                            hidden1(b1, c, m)
                            if b0 is not None and c == 0 and m == ATTN_AT:
                                q_expo(b0)
                                turn_copy(b0)
                if b0 is not None:
                    for c in range(NC):
                        lb_square(b0, c)
                        lb_root(b0, c)
                if b1 is not None:
                    for c in range(NC):
                        expert_square(b1, c)
                        expert_root(b1, c)
                        gate_exp(b1, c)
                        for e in range(E):
                            gate_copy(b1, c, e)
                        for q in range(E * KD + 1):
                            if q < E * KD:
                                expert_silu(b1, c, q)
                            if q >= 1:
                                expert_high(b1, c, q - 1)
                        expert_gate(b1, c)

            act.wait_ge(dve_const, DVE_CONST)
            batch(0, None)
            next_turn(act, "act")
            with act.Fori(0, B - 1):
                batch(0, -1)
                next_turn(act, "act")
            batch(None, -1)

        @block.tensor
        def _(pe):
            def average(out, rhs):
                for k in range(KD):
                    last = pe.matmul(out, meanw[:], rhs[:, k], start=(k == 0), stop=(k == KD - 1))
                return last

            def l0_mean(b, c):
                pe.wait_ge(x_in[c].sem, x_in[c].at(b, 1))
                if c == 0:
                    pe.wait_ge(lb_cen.sem, lb_cen.at(b - 1, NC))
                else:
                    pe.wait_ge(g2_f.sem, g2_f.at(b, c * KF))
                average(psf[:, 0], xn_chunk(c)).then_inc(li_mean.sem, 1)

            def l0_var(b, c):
                pe.wait_ge(li_sq.sem, li_sq.at(b, c + 1))
                if c == 0:
                    pe.wait_ge(lb_std.sem, lb_std.at(b - 1, NC))
                average(psf[:, 1], sq0).then_inc(li_var.sem, 1)

            def ffn_task(b, c, task):
                kind, m = divmod(task, KF)
                k = c * KF + m
                cols = slice(m * P, (m + 1) * P)
                if kind == 0:
                    bank = psf if m % 2 == 0 else psg
                    if m == 0:
                        pe.wait_ge(li_lo.sem, li_lo.at(b, c + 1))
                        pe.wait_ge(li_std.sem, li_std.at(b, c + 1))
                    elif m == 1 and c == 0:
                        pe.wait_ge(lin_done.sem, lin_done.at(b - 2, Q))
                        pe.wait_ge(gate0.sem, gate0.at(b - 1, NC))
                        pe.wait_ge(kv_masked.sem, kv_masked.at(b - 1, 1))
                    elif m == 1:
                        pe.wait_ge(gate0.sem, gate0.at(b, c))
                    if m >= 2:
                        pe.wait_ge(silu_a.sem, silu_a.at(b, k - 1))
                        pe.wait_ge(h_f.sem, h_f.at(b, k - 1))
                    for half, w in enumerate((w1, w2)):
                        for t in range(KD):
                            for part in range(2):
                                last = pe.matmul(bank[:, half], w[:, t, cols], xp[:, part, t],
                                                 start=(t == 0 and part == 0),
                                                 stop=(t == KD - 1 and part == 1))
                    last.then_inc(ab_mm.sem, 1)
                    return
                if kind == 1:
                    src, w, mm, free = hp, h1w, g1_mm, g1_f
                    if m == 0:
                        pe.wait_ge(h_hi.sem, h_hi.at(b, (c + 1) * KF))
                        pe.wait_ge(h_lo.sem, h_lo.at(b, (c + 1) * KF))
                else:
                    src, w, mm, free = g1p, h2w, g2_mm, g2_f
                    if m == 0:
                        pe.wait_ge(g1_hi.sem, g1_hi.at(b, (c + 1) * KF))
                        pe.wait_ge(g1_lo.sem, g1_lo.at(b, (c + 1) * KF))
                if m >= 2:
                    pe.wait_ge(free.sem, free.at(b, k - 1))
                for t in range(KF):
                    for part in range(2):
                        last = pe.matmul(psf[:, m % 2], w[:, t, cols], src[:, part, t],
                                         start=(t == 0 and part == 0), stop=(t == KF - 1 and part == 1))
                last.then_inc(mm.sem, 1)
                if kind == 2 and m >= 1:
                    project(b, c, m - 1)

            def project(b, c, m):
                k = c * KF + m
                pe.wait_ge(g2_hi.sem, g2_hi.at(b, k + 1))
                pe.wait_ge(g2_lo.sem, g2_lo.at(b, k + 1))
                for t in range(KD):
                    for part in range(2):
                        last = pe.matmul(psg[:, t], w3[:, m, t * P:(t + 1) * P], g2p[:, m % 2, part],
                                         start=(m == 0 and part == 0), stop=(m == KF - 1 and part == 1))
                last.then_inc(w3_mm.sem, 1)

            def attention_turn(b):
                pe.wait_ge(q_done.sem, q_done.at(b, 1))
                pe.wait_ge(g2_f.sem, g2_f.at(b, NC * KF))
                for half, src in enumerate((q0, l2)):
                    for j in range(2):
                        for t in range(KD):
                            last = pe.transpose(psf[:, half, (j * KD + t) * P:(j * KD + t + 1) * P],
                                                src[:, t, j * P:(j + 1) * P], ident[:])
                last.then_inc(turned.sem, 1)

            def attention_kv(b):
                pe.wait_ge(qt_done.sem, qt_done.at(b, 1))
                pe.wait_ge(vt_done.sem, vt_done.at(b, 1))
                pe.wait_ge(gate0.sem, gate0.at(b, NC))
                for t in range(KD):
                    for j in range(2):
                        last = pe.matmul(psg[:, 0, t * P:(t + 1) * P], qt[:, j, t * P:(t + 1) * P],
                                         vt[:, j, t * P:(t + 1) * P], start=(j == 0), stop=(j == 1))
                last.then_inc(kv_mm.sem, 1)

            def attention_num(b):
                pe.wait_ge(kv_masked.sem, kv_masked.at(b, 1))
                for half, w in enumerate((kvm, zm)):
                    for t in range(KD):
                        last = pe.matmul(psf[:, half, t * N // 2:(t + 1) * N // 2], w[:, t], q0[:, t],
                                         start=True, stop=True)
                last.then_inc(num_mm.sem, 1)

            def lb_average(b, c):
                pe.wait_ge(y_done.sem, y_done.at(b, 1))
                pe.wait_ge(lb_cen.sem, lb_cen.at(b, c))
                average(psf[:, 0], chunk(y0, c)).then_inc(lb_mean.sem, 1)

            def lb_variance(b, c):
                pe.wait_ge(lb_sq.sem, lb_sq.at(b, c + 1))
                pe.wait_ge(lb_std.sem, lb_std.at(b, c))
                average(psf[:, 1], sqb).then_inc(lb_var.sem, 1)

            def head_mean(b, c):
                pe.wait_ge(x2n.sem, x2n.at(b, c + 1))
                if c == 0:
                    pe.wait_ge(lin_done.sem, lin_done.at(b - 1, Q))
                else:
                    pe.wait_ge(ssm_done.sem, ssm_done.at(b, c))
                average(psy[:, 0], chunk(gx, c)).then_inc(le_mean.sem, 1)

            def head_var(b, c):
                pe.wait_ge(le_sq.sem, le_sq.at(b, c + 1))
                average(psy[:, 1], sq1).then_inc(le_var.sem, 1)

            def head_project(b, c):
                pe.wait_ge(le_step.sem, le_step.at(b, LE_STEPS * c + 8))
                for t in range(KD):
                    for k in range(KD):
                        last = pe.matmul(psy[:, t], wd[:, k, t * P:(t + 1) * P], xn1[:, k],
                                         start=(k == 0), stop=(k == KD - 1))
                last.then_inc(dt_mm.sem, 1)
                if c == 0:
                    pe.wait_ge(moe_r.sem, moe_r.at(b - 1, NC))
                else:
                    pe.wait_ge(u_done.sem, u_done.at(b, c * NS))
                for k in range(KD):
                    last = pe.matmul(psb[0:64, 0], wbc[:, k], xn1[:, k], start=(k == 0), stop=(k == KD - 1))
                last.then_inc(bc_mm.sem, 1)

            def spread_bc(b, c, n):
                k = c * NS + n
                if n == 0:
                    pe.wait_ge(head_done.sem, head_done.at(b, c + 1))
                else:
                    pe.wait_ge(u_done.sem, u_done.at(b, k))
                pe.matmul(psb[:, 0], sel[:, n:n + 1].broadcast_to([64, P]), bcs[:], start=True, stop=True)\
                    .then_inc(b_mm.sem, 1)
                if n == 0 and c == 0:
                    pe.wait_ge(moe_r.sem, moe_r.at(b - 1, NC))
                else:
                    pe.wait_ge(cy_done.sem, cy_done.at(b, k))
                pe.matmul(psb[:, 1], sel[:, NS + n:NS + n + 1].broadcast_to([64, P]), bcs[:],
                          start=True, stop=True).then_inc(c_mm.sem, 1)

            def sum_states(b, c, n):
                k = c * NS + n
                pe.wait_ge(pair_done.sem, pair_done.at(b, k // 2 + 1))
                for t in range(KD):
                    last = pe.matmul(psy[:, t], ident[:], u[:, n % 4, t], start=(n == 0), stop=(n == NS - 2))
                last.then_inc(y_acc.sem, 1)

            def lf_average(b, c):
                if c == 0:
                    pe.wait_ge(ssm_done.sem, ssm_done.at(b, NC))
                else:
                    pe.wait_ge(lf_cen.sem, lf_cen.at(b, c))
                average(psb[:, 0], chunk(so, c)).then_inc(lf_mean.sem, 1)

            def lf_variance(b, c):
                pe.wait_ge(lf_sq.sem, lf_sq.at(b, c + 1))
                if c == 1:
                    pe.wait_ge(lf_std.sem, lf_std.at(b, c))
                average(psb[:, 1], sq2).then_inc(lf_var.sem, 1)

            def hidden1(b, c, m):
                k = c * KF + m
                if m == 0:
                    pe.wait_ge(lf_step.sem, lf_step.at(b, 3 * NC))
                if k >= 2:
                    pe.wait_ge(f1_done.sem, f1_done.at(b, k - 1))
                for t in range(KD):
                    last = pe.matmul(psy[:, m % 2], wf1[:, t, m * P:(m + 1) * P], nrm[:, c, t],
                                     start=(t == 0), stop=(t == KD - 1))
                last.then_inc(f1_mm.sem, 1)

            def hidden2(b, c, m):
                k = c * KF + m
                pe.wait_ge(f1_done.sem, f1_done.at(b, k + 1))
                if m == 0:
                    pe.wait_ge(lf_std.sem, lf_std.at(b, NC))
                    pe.wait_ge(block_done.sem, block_done.at(b, c))
                for t in range(KD):
                    last = pe.matmul(psb[:, t], wf2[:, m, t * P:(t + 1) * P], hff[:, m % 2],
                                     start=(m == 0), stop=(m == KF - 1))
                last.then_inc(f2_mm.sem, 1)

            def expert_mean(b, c):
                pe.wait_ge(m_sq.sem, m_sq.at(b, c + 1))
                if c == 0:
                    pe.wait_ge(f1_done.sem, f1_done.at(b, NC * KF))
                else:
                    pe.wait_ge(lin_done.sem, lin_done.at(b, c * E * KD))
                average(psy[:, 0], sqm).then_inc(m_ms.sem, 1)

            def expert_logits(b, c):
                pe.wait_ge(nf_done.sem, nf_done.at(b, c + 1))
                for j in range(4):
                    out = psy[:, 1, j * E:(j + 1) * E]
                    for t in range(KD):
                        pe.matmul(out, nf[:, t, j * P:(j + 1) * P], wgate[:, t], start=(t == 0), stop=False)
                    last = pe.matmul(out, ones16[:], gbias[:], start=False, stop=True)
                last.then_inc(gate_mm.sem, 1)

            def expert_turn(b, c):
                pe.wait_ge(comb_done.sem, comb_done.at(b, c + 1))
                for j in range(4):
                    last = pe.transpose(psy[0:64, 0, j * P:(j + 1) * P], comb[:, j], ident[:])
                last.then_inc(comb_t.sem, 1)

            def expert_spread(b, c):
                pe.wait_ge(cs_done.sem, cs_done.at(b, c + 1))
                pe.wait_ge(block_done.sem, block_done.at(b, NC))
                if c == 1:
                    pe.wait_ge(moe_r.sem, moe_r.at(b, c))
                for t in range(KD):
                    pe.matmul(psb[:, t], b2s[:, t * P:(t + 1) * P], cs[:], start=True, stop=False)
                for e in range(E):
                    k = c * E + e
                    if e >= 2:
                        pe.wait_ge(cb_done.sem, cb_done.at(b, k - 1))
                    pe.matmul(psy[:, e % 2], sel[:, e:e + 1].broadcast_to([64, P]), cs[:],
                              start=True, stop=True).then_inc(cb_mm.sem, 1)

            def expert_up(b, c, q, beside):
                k = c * E * KD + q
                e, t = divmod(q, KD)
                bank = psy if q % 2 == 0 else psg
                if q == 0:
                    pe.wait_ge(cb_done.sem, cb_done.at(b, (c + 1) * E))
                    pe.wait_ge(mw_in.sem, mw_in.at(b, 2))
                elif q == 1 and c == 0:
                    ahead = b + 1 if beside else b
                    pe.wait_ge(gate0.sem, gate0.at(ahead, NC))
                    pe.wait_ge(kv_masked.sem, kv_masked.at(ahead, 1))
                else:
                    pe.wait_ge(lin_done.sem, lin_done.at(b, k - 1))
                for half in range(2):
                    for kk in range(KD):
                        last = pe.matmul(bank[:, half], mw1[:, e, kk, half, t * P:(t + 1) * P], nf[:, kk],
                                         start=(kk == 0), stop=(kk == KD - 1))
                last.then_inc(p1_mm.sem, 1)

            def expert_down(b, c, q):
                k = c * E * KD + q
                e, t = divmod(q, KD)
                pe.wait_ge(alo_done.sem, alo_done.at(b, k + 1))
                for h in range(KD):
                    for part in range(2):
                        last = pe.matmul(psb[:, h], mw2[:, e, t, h * P:(h + 1) * P], ap2[:, q % 2, part],
                                         start=False, stop=(q == E * KD - 1 and part == 1))
                last.then_inc(p2_mm.sem, 1)

            def batch(b0, b1):
                for c in range(NC):
                    if b0 is not None:
                        l0_mean(b0, c)
                    if b1 is not None:
                        head_mean(b1, c)
                    if b0 is not None:
                        l0_var(b0, c)
                    if b1 is not None:
                        head_var(b1, c)
                        head_project(b1, c)
                    for n in range(NS):
                        if b1 is not None:
                            spread_bc(b1, c, n)
                        if b0 is not None:
                            for task in tasks(n):
                                ffn_task(b0, c, task)
                        if b1 is not None and n % 2 == 1 and n >= 3:
                            sum_states(b1, c, n - 3)
                    if b1 is not None:
                        sum_states(b1, c, NS - 2)
                    if b0 is not None:
                        project(b0, c, KF - 1)
                if b1 is not None:
                    for c in range(NC):
                        lf_average(b1, c)
                        lf_variance(b1, c)
                    for c in range(NC):
                        for m in range(KF + 1):
                            if m < KF:
                                hidden1(b1, c, m)
                            if m >= 1:
                                hidden2(b1, c, m - 1)
                            if b0 is not None and c == 0 and m == ATTN_AT:
                                attention_turn(b0)
                                attention_kv(b0)
                            if b0 is not None and c == 0 and m == ATTN_AT + 1:
                                attention_num(b0)
                elif b0 is not None:
                    attention_turn(b0)
                    attention_kv(b0)
                    attention_num(b0)
                if b0 is not None:
                    for c in range(NC):
                        lb_average(b0, c)
                        lb_variance(b0, c)
                if b1 is not None:
                    for c in range(NC):
                        expert_mean(b1, c)
                        expert_logits(b1, c)
                        expert_turn(b1, c)
                        expert_spread(b1, c)
                        for q in range(E * KD + 1):
                            if q < E * KD:
                                expert_up(b1, c, q, b0 is not None)
                            if q >= 1:
                                expert_down(b1, c, q - 1)

            pe.wait_ge(dve_const, DVE_CONST)
            pe.wait_ge(pool_const, POOL_CONST)
            pe.wait_ge(w12_in, 32)
            pe.wait_ge(h1_in, 16)
            pe.wait_ge(h2_in, 16)
            pe.wait_ge(w3_in, 16)
            batch(0, None)
            pe.wait_ge(wl1_in, 64)
            pe.wait_ge(packs_in, 64)
            pe.wait_ge(b2_in, 32)
            next_turn(pe, "pe")
            with pe.Fori(0, B - 1):
                batch(0, -1)
                next_turn(pe, "pe")
            batch(None, -1)

        @block.vector
        def _(dve):
            k = 0

            def const(ins):
                nonlocal k
                k += 1
                ins.then_inc(dve_const, 1)

            dve.memset(b2s[:].bitcast(F32), 0.0).then_inc(b2s_zero, 1)
            const(dve.memset(meanw[:], 1.0 / D))
            const(dve.memset(eps[:], LN_EPS))
            const(dve.memset(ones16[:], 1.0))
            for side in (0, L + 1):
                const(dve.memset(xn[:, :, side:side + 1], 0.0))
            dve.wait_ge(pool_const, POOL_CONST)
            const(dve.tensor_tensor(sel[:], ident[0:64, 0:32], ident[0:64, 32:64], ALU.add))
            dve.wait_ge(packs_in, 64)
            for j, name in enumerate(("h_synth", "g_synth")):
                lo, hi = PACK[name]
                f = pk[:, lo:hi].rearrange("p (t k) -> p t k", k=4)
                const(dve.tensor_copy(synth[:, j, :, 0:1], f[:, :, 0:1]))
                const(dve.tensor_tensor(synth[:, j, :, 1:2], f[:, :, 1:2], f[:, :, 2:3], ALU.add))
                const(dve.tensor_copy(synth[:, j, :, 2:3], f[:, :, 3:4]))
                const(dve.tensor_tensor(synth[:, j, :, 3:4], f[:, :, 0:1], f[:, :, 1:2], ALU.add))
                const(dve.tensor_tensor(synth[:, j, :, 4:5], f[:, :, 2:3], f[:, :, 3:4], ALU.add))
            const(dve.tensor_scalar(s_h[:], col("w2_s", 0, KF), H_UP, None, ALU.mult))
            const(dve.tensor_scalar(s_g1[:], col("h1_s", 0, KF), 1.0 / H_UP, None, ALU.mult))
            const(dve.tensor_scalar(s_g2[:], col("h2_s", 0, KF), 1.0 / G_UP, None, ALU.mult))
            const(dve.tensor_copy(mbias[:], mbias16[:]))
            dve.wait_ge(dve_const, k)
            blin = mbias[:, :, 1]
            const(dve.tensor_scalar(lin_lo[:], blin, -1.0, -LIMIT, ALU.mult, ALU.add))
            const(dve.tensor_scalar(lin_hi[:], blin, -1.0, LIMIT, ALU.mult, ALU.add))
            const(dve.tensor_scalar(lin_one[:], blin, 1.0, None, ALU.add))
            dve.wait_ge(act_const, 1)
            const(dve.tensor_scalar(aneg[:], aneg[:], -1.0, None, ALU.mult))
            dve.wait_ge(dve_const, k)
            assert k == DVE_CONST

            def l0_center(b, c):
                dve.wait_ge(li_mean.sem, li_mean.at(b, c + 1))
                dve.tensor_tensor(xn_chunk(c), xn_chunk(c), both(psf[:, 0]), ALU.subtract)\
                    .then_inc(li_cen.sem, 1)

            def l0_scale(b, c):
                dve.wait_ge(li_std.sem, li_std.at(b, c + 1))
                dve.reciprocal(rs0[:], rs0[:]).then_inc(li_rstd.sem, 1)
                dve.wait_ge(li_rstd.sem, li_rstd.at(b, c + 1))
                dve.tensor_tensor(xn_chunk(c), xn_chunk(c), both(rs0[:]), ALU.mult).then_inc(li_xn.sem, 1)

            def ffn_task(b, c, task):
                kind, m = divmod(task, KF)
                k = c * KF + m
                if kind == 0:
                    bank = psf if m % 2 == 0 else psg
                    dve.wait_ge(silu_a.sem, silu_a.at(b, k + 1))
                    if m >= 2:
                        dve.wait_ge(h_lo.sem, h_lo.at(b, k - 1))
                    elif c >= 1:
                        dve.wait_ge(g2_lo.sem, g2_lo.at(b, c * KF))
                    else:
                        dve.wait_ge(x2n.sem, x2n.at(b - 1, NC))
                    dve.scalar_tensor_tensor(tf[:, m % 2], bank[:, 1], s_h[:, m:m + 1], sa[:, m % 2],
                                             ALU.mult, ALU.mult).then_inc(h_f.sem, 1)
                elif kind == 1:
                    dve.wait_ge(g1_hi.sem, g1_hi.at(b, k + 1))
                    dve.scalar_tensor_tensor(g1p[:, 1, m], tf[:, m % 2], G_UP, g1p[:, 0, m],
                                             ALU.mult, ALU.subtract).then_inc(g1_lo.sem, 1)

            def wavelets_and_attention(b, b1):
                n = 0

                def step(ins):
                    nonlocal n
                    n += 1
                    ins.then_inc(conv.sem, 1)

                def settle(back):
                    dve.wait_ge(conv.sem, conv.at(b, n - back))

                def filters(terms, lag):
                    depth = max(len(t) for _, t, _ in terms)
                    for j in range(depth):
                        for out, views, base in terms:
                            if j >= len(views):
                                continue
                            view, scalar = views[j]
                            if n:
                                settle(0 if len(terms) < 2 else lag)
                            if j == 0 and base is None:
                                step(dve.tensor_scalar(out, view, scalar, None, ALU.mult))
                            else:
                                step(dve.scalar_tensor_tensor(out, view, scalar, out if j else base,
                                                              ALU.mult, ALU.add))

                def taps(name, t):
                    lo, _ = PACK[name]
                    return [pk[:, lo + 4 * t + j:lo + 4 * t + j + 1] for j in range(4)]

                def analysis(src, width, low, high):
                    terms = []
                    for t in range(KD):
                        for name, out in (("h_filter", low), ("g_filter", high)):
                            f = taps(name, t)
                            views = [(src[:, t, j:j + width - 1:2], f[j]) for j in range(4)]
                            terms.append((out(t), views, None))
                    filters(terms, 3)

                dve.wait_ge(gate0.sem, gate0.at(b, NC))
                half, quarter = L // 2, L // 4
                for buf, width in ((l1b, half), (h1b, half), (h2b, quarter), (low2, quarter), (low1, half)):
                    for side in (0, width + 1):
                        step(dve.memset(buf[:, :, side:side + 1], 0.0))
                analysis(xn, L, lambda t: l1b[:, t, 1:half + 1], lambda t: h1b[:, t, 1:half + 1])
                settle(0)
                analysis(l1b, half, lambda t: l2[:, t, :], lambda t: h2b[:, t, 1:quarter + 1])
                settle(0)
                dve.tensor_scalar(qe[:], l2[:], 0.0, None, ALU.min).then_inc(q_min.sem, 1)
                dve.wait_ge(q_exp.sem, q_exp.at(b, 1))
                dve.scalar_tensor_tensor(q0[:], l2[:], 0.0, qe[:], ALU.max, ALU.add).then_inc(q_done.sem, 1)
                dve.wait_ge(q_done.sem, q_done.at(b, 1))
                step(dve.tensor_reduce(zs[:], q0[:], AX_X, ALU.add))
                settle(0)
                for t in range(KD):
                    step(dve.tensor_scalar(zm[:, t], headmask[:], zs[:, t:t + 1], None, ALU.mult))
                dve.wait_ge(kv_mm.sem, kv_mm.at(b, 1))
                settle(0)
                dve.tensor_tensor(kvm[:], psg[:, 0, 0:KD * P].rearrange("p (t n) -> p t n", t=KD),
                                  headmask[:].rearrange("p (o n) -> p o n", o=1).broadcast_to([P, KD, P]),
                                  ALU.mult).then_inc(kv_masked.sem, 1)
                dve.wait_ge(num_mm.sem, num_mm.at(b, 1))
                step(dve.tensor_scalar(rden[:], psf[:, 1].rearrange("p (t n) -> p t n", t=KD), ATTN_EPS,
                                       None, ALU.add))
                settle(0)
                step(dve.reciprocal(rden[:], rden[:]))
                settle(0)
                step(dve.tensor_tensor(low2[:, :, 1:quarter + 1],
                                       psf[:, 0].rearrange("p (t n) -> p t n", t=KD), rden[:], ALU.mult))
                settle(0)

                def synthesis(low, high, width, out, base):
                    terms = []
                    for t in range(KD):
                        for odd in range(2):
                            views = []
                            for j, src in enumerate((low, high)):
                                f = [synth[:, j, t, i:i + 1] for i in range(5)]
                                if odd:
                                    views += [(src[:, t, 1:width + 1], f[3]), (src[:, t, 2:width + 2], f[4])]
                                else:
                                    views += [(src[:, t, i:width + i], f[i]) for i in range(3)]
                            terms.append((out(t, odd), views, base(t, odd) if base else None))
                    filters(terms, 1)

                if b1 is not None:
                    block_out(b1, 0)
                synthesis(low2, h2b, quarter, lambda t, odd: low1[:, t, 1 + odd:half + odd:2], None)
                settle(0)
                synthesis(low1, h1b, half, lambda t, odd: y0[:, t, odd:L - 1 + odd:2],
                          lambda t, odd: xn[:, t, 1 + odd:L + odd:2])
                assert n == conv.per
                settle(0)
                dve.memset(zs[:], 0.0).then_inc(y_done.sem, 1)

            def lb_center(b, c):
                dve.wait_ge(lb_mean.sem, lb_mean.at(b, c + 1))
                dve.tensor_tensor(chunk(y0, c), chunk(y0, c), both(psf[:, 0]), ALU.subtract)\
                    .then_inc(lb_cen.sem, 1)

            def lb_scale(b, c):
                dve.wait_ge(lb_std.sem, lb_std.at(b, c + 1))
                dve.reciprocal(rsb[:], rsb[:]).then_inc(lb_step.sem, 1)
                dve.wait_ge(lb_step.sem, lb_step.at(b, 4 * c + 1))
                dve.tensor_tensor(chunk(y0, c), chunk(y0, c), both(rsb[:]), ALU.mult).then_inc(lb_step.sem, 1)
                dve.wait_ge(lb_step.sem, lb_step.at(b, 4 * c + 2))
                for t in range(KD):
                    part = y0[:, t, c * N:(c + 1) * N]
                    dve.tensor_scalar(part, part, col("gamma", t), col("beta", t), ALU.mult, ALU.add)\
                        .then_inc(lb_step.sem, 1)

            def head_center(b, c):
                dve.wait_ge(le_mean.sem, le_mean.at(b, c + 1))
                if c == 0:
                    dve.wait_ge(p2_mm.sem, p2_mm.at(b - 1, Q))
                    dve.wait_ge(out_m.sem, out_m.at(b - 1, NC))
                dve.tensor_tensor(xc[:], chunk(gx, c), both(psy[:, 0]), ALU.subtract).then_inc(le_cen.sem, 1)

            def head_norm(b, c):
                at = LE_STEPS * c

                def step(ins):
                    nonlocal at
                    at += 1
                    ins.then_inc(le_step.sem, 1)
                    dve.wait_ge(le_step.sem, le_step.at(b, at))

                dve.wait_ge(le_std.sem, le_std.at(b, c + 1))
                step(dve.reciprocal(rs1[:], rs1[:]))
                step(dve.tensor_tensor(v1[:], psy[:, 1], rs1[:], ALU.mult))
                step(dve.tensor_tensor(v1[:], v1[:], rs1[:], ALU.mult))
                step(dve.tensor_tensor(xc[:], xc[:], both(rs1[:]), ALU.mult))
                dve.wait_ge(le_std1.sem, le_std1.at(b, c + 1))
                step(dve.reciprocal(rs2[:], rs2[:]))
                step(dve.tensor_tensor(xn1[:], xc[:], both(rs2[:]), ALU.mult))
                for t in range(KD):
                    step(dve.tensor_scalar(xn1[:, t], xn1[:, t], col("ln1_g", t), col("ln1_b", t),
                                           ALU.mult, ALU.add))

            def head_rest(b, c):
                for t in range(KD):
                    if t == 0:
                        dve.wait_ge(dt_mm.sem, dt_mm.at(b, c + 1))
                    last = dve.tensor_scalar(zt[:, t], psy[:, t], col("bd", t), None, ALU.add)
                last.then_inc(z_done.sem, 1)
                at = LE_STEPS * c + 8

                def step(ins):
                    nonlocal at
                    at += 1
                    ins.then_inc(le_step.sem, 1)
                    dve.wait_ge(le_step.sem, le_step.at(b, at))

                dve.wait_ge(bc_mm.sem, bc_mm.at(b, c + 1))
                step(dve.tensor_scalar(bcf[:], psb[0:64, 0], col("bbc")[0:64], None, ALU.add))
                step(dve.tensor_copy(bcs[:], bcf[:]))
                step(dve.tensor_tensor(bcs[32:64], bcf[32:64], bcs[32:64].bitcast(F32), ALU.subtract))
                for t in range(KD):
                    last = dve.scalar_tensor_tensor(so[:, t, c * N:(c + 1) * N], xn1[:, t], col("D", t),
                                                    xc[:, t], ALU.mult, ALU.add)
                step(last)
                dve.wait_ge(z_ln.sem, z_ln.at(b, c + 1))
                step(dve.scalar_tensor_tensor(delta[:], zt[:], 0.0, lt[:], ALU.max, ALU.add))
                assert at == LE_STEPS * (c + 1)
                dve.tensor_tensor(dx[:], delta[:], xn1[:], ALU.mult).then_inc(head_done.sem, 1)

            def state(b, c, n):
                k = c * NS + n
                s = n % 4
                dve.wait_ge(b_mm.sem, b_mm.at(b, k + 1))
                if n >= 4:
                    dve.wait_ge(y_acc.sem, y_acc.at(b, (k - 4) // 2 + 1))
                dve.tensor_tensor(u[:, s], dx[:], both(psb[:, 0]), ALU.mult).then_inc(u_done.sem, 1)
                dve.wait_ge(u_done.sem, u_done.at(b, k + 1))
                dve.wait_ge(da_done.sem, da_done.at(b, k + 1))
                for t in range(KD):
                    last = dve.tensor_tensor_scan(u[:, s, t], da[:, s, t], u[:, s, t],
                                                  0.0 if c == 0 else carry[:, t, n:n + 1],
                                                  ALU.mult, ALU.add)
                last.then_inc(scan_done.sem, 1)
                dve.wait_ge(scan_done.sem, scan_done.at(b, k + 1))
                if c + 1 < NC:
                    dve.tensor_copy(carry[:, :, n:n + 1], u[:, s, :, N - 1:N]).then_inc(carried.sem, 1)
                    dve.wait_ge(carried.sem, carried.at(b, n + 1))
                dve.wait_ge(c_mm.sem, c_mm.at(b, k + 1))
                dve.tensor_tensor(u[:, s], u[:, s], both(psb[:, 1]), ALU.mult).then_inc(cy_done.sem, 1)

            def states_add(b, c):
                dve.wait_ge(y_acc.sem, y_acc.at(b, (c + 1) * NS // 2))
                dve.tensor_tensor(chunk(so, c), chunk(so, c), psy[:], ALU.add).then_inc(ssm_done.sem, 1)

            def lf_center(b, c):
                dve.wait_ge(lf_mean.sem, lf_mean.at(b, c + 1))
                dve.tensor_tensor(nrm[:, c], chunk(so, c), both(psb[:, 0]), ALU.subtract)\
                    .then_inc(lf_cen.sem, 1)

            def lf_scale(b, c):
                dve.wait_ge(lf_std.sem, lf_std.at(b, c + 1))
                dve.reciprocal(rs3[:], rs3[:]).then_inc(lf_step.sem, 1)
                dve.wait_ge(lf_step.sem, lf_step.at(b, 3 * c + 1))
                dve.tensor_tensor(nrm[:, c], nrm[:, c], both(rs3[:]), ALU.mult).then_inc(lf_step.sem, 1)
                dve.wait_ge(lf_step.sem, lf_step.at(b, 3 * c + 2))
                for t in range(KD):
                    last = dve.tensor_scalar(nrm[:, c, t], nrm[:, c, t], col("ln2_g", t), col("ln2_b", t),
                                             ALU.mult, ALU.add)
                last.then_inc(lf_step.sem, 1)

            def block_out(b, c):
                dve.wait_ge(f2_mm.sem, f2_mm.at(b, (c + 1) * KF))
                for t in range(KD):
                    part = so[:, t, c * N:(c + 1) * N]
                    last = dve.scalar_tensor_tensor(part, psb[:, t], col("b2", t), part, ALU.add, ALU.add)
                last.then_inc(block_done.sem, 1)

            def expert_norm(b, c):
                dve.wait_ge(m_rms.sem, m_rms.at(b, c + 1))
                dve.wait_ge(out_m.sem, out_m.at(b, c))
                dve.reciprocal(rsm[:], rsm[:]).then_inc(m_step.sem, 1)
                dve.wait_ge(m_step.sem, m_step.at(b, 2 * c + 1))
                dve.tensor_tensor(xrms[:], chunk(xb, c), both(rsm[:]), ALU.mult).then_inc(m_step.sem, 1)
                dve.wait_ge(m_step.sem, m_step.at(b, 2 * c + 2))
                for t in range(KD):
                    last = dve.tensor_scalar(nf[:, t], xrms[:, t], col("norm_w", t), None, ALU.mult)
                last.then_inc(nf_done.sem, 1)
                dve.wait_ge(nf_done.sem, nf_done.at(b, c + 1))

            def expert_gate(b, c):
                at = GATE_STEPS * c

                def step(ins):
                    nonlocal at
                    at += 1
                    ins.then_inc(gate_step.sem, 1)
                    dve.wait_ge(gate_step.sem, gate_step.at(b, at))

                dve.wait_ge(gate_mm.sem, gate_mm.at(b, c + 1))
                step(dve.tensor_copy(lg16[:], psy[:, 1, 0:4 * E].rearrange("p (j e) -> p j e", e=E)))
                step(dve.tensor_copy(lg[:], lg16[:]))
                for largest, chosen in ((gm1, first), (gm2, second)):
                    step(dve.tensor_reduce(largest[:], lg[:], AX_X, ALU.max))
                    step(dve.tensor_tensor(gtmp[:], lg[:], last8(largest[:]), ALU.is_equal))
                    step(dve.tensor_tensor(gtmp[:], gtmp[:], rank[:], ALU.mult))
                    step(dve.tensor_reduce(gix[:], gtmp[:], AX_X, ALU.max))
                    step(dve.tensor_tensor(chosen[:], gtmp[:], last8(gix[:]), ALU.is_equal))
                    if chosen is first:
                        step(dve.scalar_tensor_tensor(lg[:], first[:], -3e38, lg[:], ALU.mult, ALU.add))
                dve.tensor_tensor(gex[:], gm2[:], gm1[:], ALU.subtract).then_inc(gate_d.sem, 1)
                dve.wait_ge(gate_e.sem, gate_e.at(b, c + 1))
                step(dve.tensor_scalar(gw1[:], gex[:], 1.0, None, ALU.add))
                step(dve.reciprocal(gw1[:], gw1[:]))
                step(dve.tensor_scalar(gw1[:], gw1[:], A_UP, None, ALU.mult))
                step(dve.tensor_tensor(gw2[:], gex[:], gw1[:], ALU.mult))
                step(dve.tensor_tensor(first[:], first[:], last8(gw1[:]), ALU.mult))
                step(dve.tensor_tensor(second[:], second[:], last8(gw2[:]), ALU.mult))
                step(dve.tensor_tensor(comb[:, :, 0:E], first[:], second[:], ALU.add))
                assert at == GATE_STEPS * (c + 1)
                dve.tensor_copy(comb[:, :, 32:32 + E], comb[:, :, 0:E]).then_inc(comb_done.sem, 1)

            def expert_parts(b, c):
                dve.wait_ge(comb_t.sem, comb_t.at(b, c + 1))
                dve.tensor_copy(ct[:], psy[0:64, 0]).then_inc(ct_done.sem, 1)
                dve.wait_ge(ct_done.sem, ct_done.at(b, 2 * c + 1))
                dve.tensor_copy(cs[:], ct[:]).then_inc(ct_done.sem, 1)
                dve.wait_ge(ct_done.sem, ct_done.at(b, 2 * c + 2))
                dve.tensor_tensor(cs[32:64], ct[32:64], cs[32:64].bitcast(F32), ALU.subtract)\
                    .then_inc(cs_done.sem, 1)

            def expert_clip(b, c, q):
                k = c * E * KD + q
                e, t = divmod(q, KD)
                bank = psy if q % 2 == 0 else psg
                dve.wait_ge(p1_mm.sem, p1_mm.at(b, k + 1))
                if q >= 2:
                    dve.wait_ge(sg_done.sem, sg_done.at(b, k - 1))
                elif q == 0 and c >= 1:
                    dve.wait_ge(out_sent.sem, out_sent.at(b, c))
                dve.tensor_scalar(gmin[:, q % 2], bank[:, 0], mbias[:, e, 0, t:t + 1], LIMIT, ALU.add, ALU.min)\
                    .then_inc(gmin_done.sem, 1)
                dve.tensor_scalar(lin[:, q % 2], bank[:, 1], lin_lo[:, e, t:t + 1], lin_hi[:, e, t:t + 1],
                                  ALU.max, ALU.min).then_inc(lin_done.sem, 1)

            def expert_product(b, c, q):
                k = c * E * KD + q
                e, t = divmod(q, KD)
                dve.wait_ge(sc_done.sem, sc_done.at(b, k + 1))
                dve.wait_ge(lin_done.sem, lin_done.at(b, k + 1))
                if q >= 2:
                    dve.wait_ge(alo_done.sem, alo_done.at(b, k - 1))
                dve.scalar_tensor_tensor(af[:, q % 2], lin[:, q % 2], lin_one[:, e, t:t + 1], sc[:, q % 2],
                                         ALU.add, ALU.mult).then_inc(af_done.sem, 1)

            def expert_sum(b, c):
                dve.wait_ge(p2_mm.sem, p2_mm.at(b, (c + 1) * E * KD))
                dve.tensor_scalar(moe16[:], psb[:], 1.0 / A_UP, None, ALU.mult).then_inc(moe_r.sem, 1)
                dve.wait_ge(moe_r.sem, moe_r.at(b, c + 1))
                dve.tensor_tensor(sum16[:], chunk(xb, c), moe16[:], ALU.add).then_inc(moe_s.sem, 1)

            def batch(b0, b1):
                for c in range(NC):
                    if b0 is not None:
                        l0_center(b0, c)
                    if b1 is not None:
                        head_center(b1, c)
                    if b0 is not None:
                        l0_scale(b0, c)
                    if b1 is not None:
                        head_norm(b1, c)
                        head_rest(b1, c)
                    for n in range(NS):
                        if b1 is not None:
                            state(b1, c, n)
                        if b0 is not None:
                            for task in tasks(n):
                                ffn_task(b0, c, task)
                    if b1 is not None:
                        states_add(b1, c)
                if b1 is not None:
                    for c in range(NC):
                        lf_center(b1, c)
                        lf_scale(b1, c)
                if b0 is not None:
                    wavelets_and_attention(b0, b1)
                elif b1 is not None:
                    block_out(b1, 0)
                if b1 is not None:
                    block_out(b1, 1)
                if b0 is not None:
                    for c in range(NC):
                        lb_center(b0, c)
                        lb_scale(b0, c)
                if b1 is not None:
                    for c in range(NC):
                        expert_norm(b1, c)
                        expert_gate(b1, c)
                        expert_parts(b1, c)
                        for q in range(E * KD + 1):
                            if q < E * KD:
                                expert_clip(b1, c, q)
                            if q >= 1:
                                expert_product(b1, c, q - 1)
                        expert_sum(b1, c)

            batch(0, None)
            next_turn(dve, "dve")
            with dve.Fori(0, B - 1):
                batch(0, -1)
                next_turn(dve, "dve")
            batch(None, -1)


_NAMES = ("x", "pack", "w1", "w2", "h1", "h2", "w3", "wd", "wbc", "wf1", "wf2", "mlp1_w", "mlp1_b", "mlp2_w",
          "mlp2_b", "gate_w", "gate_b")


def kernel(**inputs):
    import numpy as _np
    import concourse.bacc as _bacc
    from concourse import mybir as _mybir
    from concourse.bass_utils import run_bass_kernel_spmd as _run

    g = {k: _np.asarray(v) for k, v in inputs.items()}

    def columns(v):
        v = v.reshape(v.shape[0] // P, P, -1)
        return v.transpose(1, 0, 2).reshape(P, -1)

    def stationary(w):
        return w.T.reshape(-1, P, w.shape[0]).transpose(1, 0, 2)

    vectors = {
        "h_filter": g["L0_attn_h_filter"].T, "g_filter": g["L0_attn_g_filter"].T,
        "h_synth": g["L0_attn_h_synth"].T, "g_synth": g["L0_attn_g_synth"].T,
        "gamma": g["L0_attn_norm_gamma"], "beta": g["L0_attn_norm_beta"],
        "w1_s": g["L0_ffn_w1_s"], "w2_s": g["L0_ffn_w2_s"], "h1_s": g["L0_ffn_h1_s"],
        "h2_s": g["L0_ffn_h2_s"], "w3_s": g["L0_ffn_w3_s"], "ln1_g": g["L1_attn_ln1_g"],
        "ln1_b": g["L1_attn_ln1_b"], "bd": g["L1_attn_bd"], "A_log": g["L1_attn_A_log"],
        "D": g["L1_attn_D"], "ln2_g": g["L1_attn_ln2_g"], "ln2_b": g["L1_attn_ln2_b"],
        "b1": g["L1_attn_b1"], "b2": g["L1_attn_b2"], "norm_w": g["L1_ffn_norm_weight"],
        "bbc": _np.concatenate([g["L1_attn_bbc"]] * (P // 32)),
    }
    wbc = g["L1_attn_Wbc"]
    mlp1 = g["L1_ffn_mlp1_weight"].reshape(E, D, 2, KD, P)
    mlp2 = g["L1_ffn_mlp2_weight"].reshape(E, D, KD, P)
    arrays = {
        "x": g["L0_attn_x"].reshape(B, L, KD, P).transpose(0, 3, 2, 1),
        "pack": _np.concatenate([columns(vectors[k]) for k in PACK], axis=1),
        "w1": stationary(g["L0_ffn_w1_w"]), "w2": stationary(g["L0_ffn_w2_w"]),
        "h1": stationary(g["L0_ffn_h1_w"]), "h2": stationary(g["L0_ffn_h2_w"]),
        "w3": stationary(g["L0_ffn_w3_w"]), "wd": stationary(g["L1_attn_Wd"]),
        "wbc": stationary(_np.concatenate([wbc, wbc])),
        "wf1": stationary(g["L1_attn_W1"]), "wf2": stationary(g["L1_attn_W2"]),
        "mlp1_w": mlp1.transpose(4, 0, 3, 2, 1),
        "mlp1_b": g["L1_ffn_mlp1_bias"].reshape(E, KD, P, 2).transpose(2, 0, 3, 1),
        "mlp2_w": mlp2.transpose(3, 0, 2, 1),
        "mlp2_b": g["L1_ffn_mlp2_bias"],
        "gate_w": g["L1_ffn_gate_weight"].reshape(E, KD, P).transpose(2, 1, 0),
        "gate_b": g["L1_ffn_gate_bias"].reshape(1, E),
    }
    nc = _bacc.Bacc("TRN2", target_bir_lowering=False, num_devices=1)
    aps, feed = {}, {}
    for name in _NAMES:
        v = _np.ascontiguousarray(arrays[name])
        feed[f"in_{name}"] = v
        aps[name] = nc.dram_tensor(f"in_{name}", v.shape, _mybir.dt.from_np(v.dtype), kind="ExternalInput").ap()
    aps["out"] = nc.dram_tensor("out_0", (B, P, KD, L), F32, kind="ExternalOutput").ap()
    build(nc, aps)
    r = _run(nc, [feed], core_ids=[0])
    out = r.results[0]["out_0"]
    return out.transpose(0, 3, 2, 1).reshape(B, L, D)
```

```python
from contextlib import ExitStack

import concourse.bass as bass
from concourse import mybir

F32 = mybir.dt.float32
F32R = mybir.dt.float32r
F16 = mybir.dt.float16
BF16 = mybir.dt.bfloat16
ALU = mybir.AluOpType
ACT = mybir.ActivationFunctionType
AX_X = mybir.AxisListType.X

P = 128
B, L, D = 4, 1024, 256
KD = D // P
F = 1024
KF = F // P
N = 512
NC = L // N
NS = 16
E = 8
HEAD = 16
LN_EPS = 1e-5
ATTN_EPS = 1e-6
LIMIT = 7.0
ALPHA = 1.702
H_UP = 128.0
G_UP = 4.0
A_UP = 1024.0

PACK = {}
_at = 0
for _name, _width in (
    ("h_filter", 8), ("g_filter", 8), ("h_synth", 8), ("g_synth", 8), ("gamma", 2), ("beta", 2),
    ("w1_s", 8), ("w2_s", 8), ("h1_s", 8), ("h2_s", 8), ("w3_s", 2), ("ln1_g", 2), ("ln1_b", 2),
    ("bd", 2), ("A_log", 32), ("D", 2), ("ln2_g", 2), ("ln2_b", 2), ("b1", 8), ("b2", 2),
    ("norm_w", 2), ("bbc", 1),
):
    PACK[_name] = (_at, _at + _width)
    _at += _width
PACKED = _at


POOL_CONST = 14
DVE_CONST = 24
LB_STEPS = 3
LE_STEPS = 9
HEAD_STEPS = 4
GATE_STEPS = 20
NJ = L // P
NQ = E * KD
NB = 4
LAG = 1
LAG_DOWN = 3
OUT_LAG = 6
RMS_AT, RMS1_AT, LOGITS_AT, ATTN_AT, NUM_AT, TURN_AT, TURN1_AT = 1, 2, 5, 6, 7, 10, 13


class Signal:

    def __init__(self, sem, layer, per, unit=1):
        self.sem, self.layer, self.per, self.unit = sem, layer, per, unit

    @property
    def batch(self):
        return self.per * self.unit

    @property
    def start(self):
        return (1 + self.layer) * self.batch

    def at(self, b, k):
        return (b + 1 + self.layer) * self.batch + k * self.unit


def build(nc, a):
    ctx = ExitStack()
    with ctx:
        def sb(name, shape, dt):
            return ctx.enter_context(nc.sbuf_tensor(name, shape, dt))

        w1 = sb("w1", [P, KD, F], F16)
        w2 = sb("w2", [P, KD, F], F16)
        h1w = sb("h1w", [P, KF, F], F16)
        h2w = sb("h2w", [P, KF, F], F16)
        w3 = sb("w3", [P, KF, D], F32R)
        wd = sb("wd", [P, KD, D], F32)
        wbc = sb("wbc", [P, KD, 64], F32)
        wf1 = sb("wf1", [P, KD, F], F32)
        wf2 = sb("wf2", [P, KF, D], F32)
        xn = sb("xn", [P, KD, L + 2], F32)
        xp = sb("xp", [P, 2, KD, N], F16)
        gx = sb("gx", [P, KD, L], F32)
        x2 = sb("x2", [P, KD, L], F32)
        xb = sb("xb", [P, KD, L], BF16)
        so = sb("so", [P, KD, L], F32)
        pk = sb("pk", [P, PACKED], F32)
        ident = sb("ident", [P, P], F32)
        meanw = sb("meanw", [P, P], F32)
        headmask = sb("headmask", [P, P], F32)
        sel = sb("sel", [64, 32], F32R)
        synth = sb("synth", [P, 2, KD, 5], F32)
        aneg = sb("aneg", [P, KD, NS], F32)
        s_h = sb("s_h", [P, KF], F32)
        s_g1 = sb("s_g1", [P, KF], F32)
        s_g2 = sb("s_g2", [P, KF], F32)
        mbias16 = sb("mbias16", [P, E, 2, KD], BF16)
        mbias = sb("mbias", [P, E, 2, KD], F32)
        lin_lo = sb("lin_lo", [P, E, KD], F32)
        lin_hi = sb("lin_hi", [P, E, KD], F32)
        lin_one = sb("lin_one", [P, E, KD], F32)
        b2s = sb("b2s", [64, D], F32R)
        wgate = sb("wgate", [P, KD, E], BF16)
        gbias = sb("gbias", [1, E], BF16)
        ones16 = sb("ones16", [1, P], BF16)
        rank = sb("rank", [P, NJ, E], F32)
        eps = sb("eps", [P, 1], F32)
        carry = sb("carry", [P, KD, NS], F32)
        lg16 = sb("lg16", [P, NJ, E], BF16)
        lg = sb("lg", [P, NJ, E], F32)
        first = sb("first", [P, NJ, E], F32)
        second = sb("second", [P, NJ, E], F32)
        gtmp = sb("gtmp", [P, NJ, E], F32)
        gm1 = sb("gm1", [P, NJ], F32)
        gm2 = sb("gm2", [P, NJ], F32)
        gix = sb("gix", [P, NJ], F32)
        gex = sb("gex", [P, NJ], F32)
        gw1 = sb("gw1", [P, NJ], F32)
        gw2 = sb("gw2", [P, NJ], F32)
        comb = sb("comb", [P, NJ, 64], F32)

        R1, R2 = 51200, 43008

        def region(name, size):
            base = -(-nc.sbuf_base // 32) * 32
            sb(name, [P, size // 4], F32)

            def place(name, at, shape, dt):
                return nc.alloc_sbuf_tensor_at(name, shape, dt, offset=base + at)
            return place

        r1, r2 = region("region1", R1), region("region2", R2)
        hp = r1("hp", 0, [P, 2, KF, N], F16)
        g1p = r1("g1p", 16384, [P, 2, KF, N], F16)
        g2p = r1("g2p", 32768, [P, 2, 2, N], F32R)
        sa = r1("sa", 40960, [P, 2, N], F32)
        tf = r1("tf", 45056, [P, 2, N], F32)
        sq0 = r1("sq0", 40960, [P, KD, N], F32)
        rs0 = r1("rs0", 49152, [P, N], F32)
        l1b = r1("l1b", 0, [P, KD, N + 2], F32)
        h1b = r1("h1b", 4352, [P, KD, N + 2], F32)
        l2 = r1("l2", 8704, [P, KD, N // 2], F32)
        h2b = r1("h2b", 10752, [P, KD, N // 2 + 2], F32)
        q0 = r1("q0", 12928, [P, KD, N // 2], F32)
        qe = r1("qe", 14976, [P, KD, N // 2], F32)
        low2 = r1("low2", 17024, [P, KD, N // 2 + 2], F32)
        low1 = r1("low1", 19200, [P, KD, N + 2], F32)
        qt = r1("qt", 23424, [P, 2, D], F32)
        vt = r1("vt", 25472, [P, 2, D], F32)
        kvm = r1("kvm", 27520, [P, KD, P], F32)
        zm = r1("zm", 28544, [P, KD, P], F32)
        rden = r1("rden", 29568, [P, KD, N // 2], F32)
        zs = r1("zs", 31616, [P, KD], F32)
        y0 = r1("y0", 32768, [P, KD, L], F32)
        sqb = r1("sqb", 40960, [P, KD, N], F32)
        rsb = r1("rsb", 45056, [P, N], F32)
        xr = r1("xr", 47104, [P, KD, N], F32)
        gate = r1("gate", 0, [P, NB, N], F32)
        lin = r1("lin", 8192, [P, NB, N], F32)
        sum16 = r1("sum16", 16384, [P, KD, N], BF16)
        gate1 = r1("gate1", 18432, [P, KD, N], F32)
        cs = r1("cs", 23424, [64, NC, N], F32R)
        af = r1("af", 27520, [P, NB, N], F32)
        ap2 = r1("ap2", 35712, [P, NB, 2, N], F16)
        outc = r1("outc", 43904, [P, KD, N], F32)
        sqm = r1("sqm", 40960, [P, KD, N], F32)
        rsm = r1("rsm", 45056, [P, N], F32)
        xrms = r1("xrms", 47104, [P, KD, N], F32)
        ct = r1("ct", 45056, [64, N], F32)
        sq2 = r1("sq2", 40960, [P, KD, N], F32)
        da = r2("da", 0, [P, 4, KD, N], F32)
        u = r2("u", 16384, [P, 4, KD, N], F32)
        delta = r2("delta", 32768, [P, KD, N], F32)
        dx = r2("dx", 36864, [P, KD, N], F32)
        bcs = r2("bcs", 40960, [64, N], F32R)
        zt = r2("zt", 0, [P, KD, N], F32)
        lt = r2("lt", 4096, [P, KD, N], F32)
        v1 = r2("v1", 8192, [P, N], F32)
        bcf = r2("bcf", 10240, [64, N], F32)
        xc = r2("xc", 16384, [P, KD, N], F32)
        sq1 = r2("sq1", 20480, [P, KD, N], F32)
        xn1 = r2("xn1", 24576, [P, KD, N], F32)
        rs1 = r2("rs1", 28672, [P, N], F32)
        rs2 = r2("rs2", 30720, [P, N], F32)
        nrm = r2("nrm", 0, [P, NC, KD, N], F32)
        hff = r2("hff", 8192, [P, 2, N], F32)
        rs3 = r2("rs3", 12288, [P, N], F32)
        cb = r2("cb", 0, [P, NB, N], F32)
        nf = r2("nf", 14336, [P, NC, KD, N], BF16)
        mw1 = r2("mw1", 18432, [P, E, KD, 2, D], BF16)
        mw2 = r2("mw2", 34816, [P, E, KD, D], BF16)

        def ps(name):
            return ctx.enter_context(nc.psum_tensor(name, [P, 2, N], F32))

        psy, psb, psf, psg = ps("psy"), ps("psb"), ps("psf"), ps("psg")

        def col(name, k=0, w=1):
            lo, hi = PACK[name]
            return pk[:, lo + k:lo + k + w]

        def both(t):
            return t.rearrange("p (o n) -> p o n", o=1).broadcast_to([P, KD, t.shape[-1]])

        def last8(t):
            return t.rearrange("p (j o) -> p j o", o=1).broadcast_to([P, NJ, E])

        signals = []
        layer = 0

        def sig(name, per, unit=1):
            s = Signal(ctx.enter_context(nc.semaphore(name)), layer, per, unit)
            signals.append(s)
            return s

        def one(name):
            return ctx.enter_context(nc.semaphore(name))

        packs_in = one("packs_in")
        w12_in = one("w12_in")
        h1_in = one("h1_in")
        h2_in = one("h2_in")
        w3_in = one("w3_in")
        wl1_in = one("wl1_in")
        b2_in = one("b2_in")
        pool_const = one("pool_const")
        dve_const = one("dve_const")
        act_const = one("act_const")
        b2s_zero = one("b2s_zero")
        x_in = [sig(f"x_in{c}", 1, 16) for c in range(NC)]
        li_mean = sig("li_mean", NC)
        li_cen = sig("li_cen", NC)
        li_sq = sig("li_sq", NC)
        li_var = sig("li_var", NC)
        li_ln = sig("li_ln", NC)
        li_rstd = sig("li_rstd", NC)
        li_xn = sig("li_xn", NC)
        li_hi = sig("li_hi", NC)
        li_lo = sig("li_lo", NC)
        ab_mm = sig("ab_mm", NC * KF)
        silu_a = sig("silu_a", NC * KF)
        h_f = sig("h_f", NC * KF)
        h_hi = sig("h_hi", NC * KF)
        h_lo = sig("h_lo", NC * KF)
        g1_mm = sig("g1_mm", NC * KF)
        g1_f = sig("g1_f", NC * KF)
        g1_hi = sig("g1_hi", NC * KF)
        g1_lo = sig("g1_lo", NC * KF)
        g2_mm = sig("g2_mm", NC * KF)
        g2_f = sig("g2_f", NC * KF)
        g2_hi = sig("g2_hi", NC * KF)
        g2_lo = sig("g2_lo", NC * KF)
        w3_mm = sig("w3_mm", NC * KF)
        gate0 = sig("gate0", NC)
        conv = sig("conv", 88)
        q_min = sig("q_min", 1)
        q_exp = sig("q_exp", 1)
        q_done = sig("q_done", 1)
        turned = sig("turned", 1)
        qt_done = sig("qt_done", 1)
        vt_done = sig("vt_done", 1)
        kv_mm = sig("kv_mm", 1)
        kv_masked = sig("kv_masked", 1)
        num_mm = sig("num_mm", 1)
        y_done = sig("y_done", 1)
        lb_mean = sig("lb_mean", NC)
        lb_cen = sig("lb_cen", NC)
        lb_sq = sig("lb_sq", NC)
        lb_var = sig("lb_var", NC)
        lb_ln = sig("lb_ln", NC)
        lb_rstd = sig("lb_rstd", NC)
        lb_step = sig("lb_step", LB_STEPS * NC)
        xr_in = sig("xr_in", NC, 16)
        gy = sig("gy", NC)
        x2n = sig("x2n", NC)
        layer = 1
        le_copy = sig("le_copy", NC)
        le_mean = sig("le_mean", NC)
        le_cen = sig("le_cen", NC)
        le_sq = sig("le_sq", NC)
        le_var = sig("le_var", NC)
        le_ln = sig("le_ln", 2 * NC)
        le_rstd = sig("le_rstd", NC)
        le_step = sig("le_step", LE_STEPS * NC)
        le_rstd1 = sig("le_rstd1", NC)
        le_xb = sig("le_xb", NC)
        dt_mm = sig("dt_mm", NC)
        bc_mm = sig("bc_mm", NC)
        z_done = sig("z_done", NC)
        z_abs = sig("z_abs", NC)
        z_exp = sig("z_exp", NC)
        z_ln = sig("z_ln", NC)
        head_done = sig("head_done", NC)
        b_mm = sig("b_mm", NC * NS)
        c_mm = sig("c_mm", NC * NS)
        da_done = sig("da_done", NC * NS)
        u_done = sig("u_done", NC * NS)
        scan_done = sig("scan_done", NC * NS)
        carried = sig("carried", NS)
        cy_done = sig("cy_done", NC * NS)
        pair_done = sig("pair_done", NC * NS // 2)
        y_acc = sig("y_acc", NC * NS // 2)
        ssm_done = sig("ssm_done", NC)
        lf_mean = sig("lf_mean", NC)
        lf_cen = sig("lf_cen", NC)
        lf_sq = sig("lf_sq", NC)
        lf_var = sig("lf_var", NC)
        lf_ln = sig("lf_ln", NC)
        lf_rstd = sig("lf_rstd", NC)
        lf_step = sig("lf_step", 2 * NC)
        f1_mm = sig("f1_mm", NC * KF)
        f1_done = sig("f1_done", NC * KF)
        f2_mm = sig("f2_mm", NC * KF)
        block_done = sig("block_done", NC)
        mw_in = sig("mw_in", 2, 16)
        m_sq = sig("m_sq", NC)
        m_ms = sig("m_ms", NC)
        m_rms = sig("m_rms", NC)
        m_ln = sig("m_ln", NC)
        m_step = sig("m_step", NC)
        nf_done = sig("nf_done", NC)
        gate_mm = sig("gate_mm", 1)
        gate_step = sig("gate_step", GATE_STEPS)
        gate_d = sig("gate_d", 1)
        gate_e = sig("gate_e", 1)
        comb_done = sig("comb_done", 1)
        comb_t = sig("comb_t", NC)
        ct_done = sig("ct_done", 2 * NC)
        cs_done = sig("cs_done", NC)
        cb_mm = sig("cb_mm", NC * E)
        cb_done = sig("cb_done", NC * E)
        Q = NC * NQ
        p1_mm = sig("p1_mm", Q)
        gmin_done = sig("gmin_done", Q)
        lin_done = sig("lin_done", Q)
        sg_done = sig("sg_done", Q)
        sc_done = sig("sc_done", Q)
        af_done = sig("af_done", Q)
        ahi_done = sig("ahi_done", Q)
        alo_done = sig("alo_done", Q)
        p2_mm = sig("p2_mm", Q)
        moe_r = sig("moe_r", NC)
        moe_s = sig("moe_s", NC)
        moe_g = sig("moe_g", NC)
        out_m = sig("out_m", NC)
        out_ready = sig("out_ready", NC)
        out_sent = sig("out_sent", NC, 16)

        arrived = one("arrived")
        released = {e: one(f"released_{e}") for e in ("pool", "act", "pe", "dve")}

        def next_turn(engine, name):
            engine.sem_inc(arrived, 1)
            engine.wait_ge(released[name], 1)
            engine.sem_inc(released[name], -1)

        block = ctx.enter_context(nc.Block())

        def chunk(t, c):
            return t[:, :, c * N:(c + 1) * N]

        def xn_chunk(c):
            return xn[:, :, 1 + c * N:1 + (c + 1) * N]

        def tasks(step):
            return range(step * 3 * KF // NS, (step + 1) * 3 * KF // NS)

        @block.sync
        def _(sp):
            for s in signals:
                sp.sem_inc(s.sem, s.start)

            def load_x(b, row):
                for c in range(NC):
                    sp.wait_ge(y_done.sem, y_done.at(b - 1, 1))
                    sp.dma_start(xn_chunk(c), a["x"][row][:, :, c * N:(c + 1) * N]).then_inc(x_in[c].sem, 16)

            def load_experts(b):
                sp.wait_ge(ssm_done.sem, ssm_done.at(b, NC))
                sp.dma_start(mw1[:], a["mlp1_w"]).then_inc(mw_in.sem, 16)
                sp.dma_start(mw2[:], a["mlp2_w"]).then_inc(mw_in.sem, 16)

            def load_residual(b, row):
                for c in range(NC):
                    sp.wait_ge(gate0.sem, gate0.at(b, NC))
                    sp.wait_ge(nf_done.sem, nf_done.at(b - 1, NC))
                    sp.wait_ge(x2n.sem, x2n.at(b, c))
                    sp.dma_start(xr[:], a["x"][row][:, :, c * N:(c + 1) * N]).then_inc(xr_in.sem, 16)

            def store_out(b, row):
                for c in range(NC):
                    sp.wait_ge(out_ready.sem, out_ready.at(b, c + 1))
                    sp.dma_start(a["out"][row][:, :, c * N:(c + 1) * N], outc[:]).then_inc(out_sent.sem, 16)

            sp.dma_start(pk[:], a["pack"]).then_inc(packs_in, 16)
            load_x(0, 0)
            sp.dma_start(wf1[:], a["wf1"]).then_inc(wl1_in, 16)
            sp.dma_start(wf2[:], a["wf2"]).then_inc(wl1_in, 16)
            sp.dma_start(wd[:], a["wd"]).then_inc(wl1_in, 16)
            sp.dma_start(wbc[:], a["wbc"]).then_inc(wl1_in, 16)
            sp.dma_start(mbias16[:], a["mlp1_b"]).then_inc(packs_in, 16)
            sp.dma_start(wgate[:], a["gate_w"]).then_inc(packs_in, 16)
            sp.dma_start(gbias[:], a["gate_b"]).then_inc(packs_in, 16)

            def turn(row, last=False):
                load_experts(-1)
                load_residual(0, row)
                if not last:
                    load_x(1, row + 1)
                store_out(-1, row - 1)

            def take_down():
                sp.wait_ge(arrived, len(released))
                sp.sem_inc(arrived, -len(released))
                for s in signals:
                    sp.sem_inc(s.sem, -s.batch)
                for s in released.values():
                    sp.sem_inc(s, 1)

            load_residual(0, 0)
            load_x(1, 1)
            take_down()
            with sp.Fori(0, B - 2) as i:
                turn(i + 1)
                take_down()
            turn(B - 1, last=True)
            take_down()
            load_experts(-1)
            store_out(-1, B - 1)
            sp.wait_ge(out_sent.sem, out_sent.at(-1, NC))

        @block.gpsimd
        def _(pool):
            pool.dma_start(w1[:], a["w1"]).then_inc(w12_in, 16)
            pool.dma_start(w2[:], a["w2"]).then_inc(w12_in, 16)
            pool.dma_start(h1w[:], a["h1"]).then_inc(h1_in, 16)
            pool.dma_start(h2w[:], a["h2"]).then_inc(h2_in, 16)
            pool.dma_start(w3[:], a["w3"]).then_inc(w3_in, 16)
            pool.wait_ge(b2s_zero, 1)
            pool.dma_start(b2s[0:E, :], a["mlp2_b"]).then_inc(b2_in, 16)
            pool.dma_start(b2s[32:32 + E, :], a["mlp2_b"]).then_inc(b2_in, 16)
            k = 0

            def const(ins):
                nonlocal k
                k += 1
                ins.then_inc(pool_const, 1)
                pool.wait_ge(pool_const, k)

            const(pool.memset(ident[:], 0.0))
            const(pool.affine_select(out=ident[:], in_=ident[:], compare_op=ALU.not_equal, fill=1.0,
                                     base=0, pattern=[[-1, P]], channel_multiplier=1))
            const(pool.memset(headmask[:], 1.0))
            hm = headmask[:].rearrange("p (h d) -> p h d", d=HEAD)
            const(pool.affine_select(out=hm, in_=hm, compare_op=ALU.is_ge, fill=0.0, base=0,
                                     pattern=[[-HEAD, P // HEAD], [0, HEAD]], channel_multiplier=1))
            const(pool.affine_select(out=hm, in_=hm, compare_op=ALU.is_ge, fill=0.0, base=HEAD - 1,
                                     pattern=[[HEAD, P // HEAD], [0, HEAD]], channel_multiplier=-1))
            for e in range(E):
                const(pool.memset(rank[:, :, e:e + 1], float(E - e)))
            const(pool.memset(comb[:], 0.0))
            assert k == POOL_CONST

            def l0_low(b, c):
                pool.wait_ge(li_hi.sem, li_hi.at(b, c + 1))
                pool.tensor_tensor(xp[:, 1], xn_chunk(c), xp[:, 0], ALU.subtract).then_inc(li_lo.sem, 1)

            def ffn_task(b, c, task):
                kind, m = divmod(task, KF)
                k = c * KF + m
                if kind == 0:
                    pool.wait_ge(h_hi.sem, h_hi.at(b, k + 1))
                    pool.tensor_tensor(hp[:, 1, m], tf[:, m % 2], hp[:, 0, m], ALU.subtract)\
                        .then_inc(h_lo.sem, 1)
                elif kind == 2:
                    pool.wait_ge(g2_hi.sem, g2_hi.at(b, k + 1))
                    pool.tensor_tensor(g2p[:, m % 2, 1], tf[:, m % 2], g2p[:, m % 2, 0].bitcast(F32),
                                       ALU.subtract).then_inc(g2_lo.sem, 1)

            def state_pair(b, c, n):
                k = c * NS + n
                pool.wait_ge(cy_done.sem, cy_done.at(b, k + 2))
                pool.tensor_tensor(u[:, n % 4], u[:, n % 4], u[:, (n + 1) % 4], ALU.add)\
                    .then_inc(pair_done.sem, 1)

            def l0_out(b, c):
                pool.wait_ge(lb_step.sem, lb_step.at(b, LB_STEPS * (c + 1)))
                pool.tensor_tensor(chunk(gx, c), chunk(y0, c), chunk(gx, c), ALU.mult).then_inc(gy.sem, 1)
                pool.wait_ge(gy.sem, gy.at(b, c + 1))
                pool.wait_ge(xr_in.sem, xr_in.at(b, c + 1))
                pool.tensor_tensor(chunk(gx, c), chunk(gx, c), xr[:], ALU.add).then_inc(x2n.sem, 1)

            def expert_weighted(b, r):
                pool.wait_ge(sg_done.sem, sg_done.at(b, r + 1))
                pool.wait_ge(cb_done.sem, cb_done.at(b, r // KD + 1))
                pool.tensor_tensor(gate[:, r % NB], gate[:, r % NB], cb[:, r // KD % NB], ALU.mult)\
                    .then_inc(sc_done.sem, 1)

            def expert_low(b, r):
                pool.wait_ge(ahi_done.sem, ahi_done.at(b, r + 1))
                pool.tensor_tensor(ap2[:, r % NB, 1], af[:, r % NB], ap2[:, r % NB, 0], ALU.subtract)\
                    .then_inc(alo_done.sem, 1)

            def expert_out(b, c, ahead):
                pool.wait_ge(moe_g.sem, moe_g.at(b, c + 1))
                pool.wait_ge(block_done.sem, block_done.at(b, c + 1))
                pool.wait_ge(x2n.sem, x2n.at(ahead, NC))
                pool.wait_ge(out_sent.sem, out_sent.at(b, c))
                pool.tensor_tensor(outc[:], chunk(so, c), gate1[:], ALU.mult).then_inc(out_m.sem, 1)
                pool.wait_ge(out_m.sem, out_m.at(b, c + 1))
                pool.tensor_tensor(outc[:], outc[:], chunk(x2, c), ALU.add).then_inc(out_ready.sem, 1)

            def batch(b0, b1):
                for c in range(NC):
                    if b0 is not None:
                        l0_low(b0, c)
                    for n in range(NS):
                        if b0 is not None:
                            for task in tasks(n):
                                ffn_task(b0, c, task)
                        if b1 is not None and n % 2 == 1:
                            state_pair(b1, c, n - 1)
                if b0 is not None:
                    for c in range(NC):
                        l0_out(b0, c)
                if b1 is not None:
                    ahead = 0 if b0 is not None else b1
                    for r in range(Q + LAG):
                        if r < Q:
                            expert_weighted(b1, r)
                        if r >= LAG:
                            expert_low(b1, r - LAG)
                        if r == NQ + OUT_LAG:
                            expert_out(b1, 0, ahead)
                    expert_out(b1, 1, ahead)

            batch(0, None)
            next_turn(pool, "pool")
            with pool.Fori(0, B - 1):
                batch(0, -1)
                next_turn(pool, "pool")
            batch(None, -1)

        @block.scalar
        def _(act):
            act.wait_ge(packs_in, 16 * 4)
            lo, hi = PACK["A_log"]
            act.activation(aneg[:], pk[:, lo:hi].rearrange("p (t n) -> p t n", t=KD), ACT.Exp)\
                .then_inc(act_const, 1)

            def split_input(b, c):
                act.wait_ge(li_xn.sem, li_xn.at(b, c + 1))
                act.wait_ge(ab_mm.sem, ab_mm.at(b, c * KF))
                act.activation(xp[:, 0], xn_chunk(c), ACT.Copy).then_inc(li_hi.sem, 1)

            def l0_square(b, c):
                act.wait_ge(li_cen.sem, li_cen.at(b, c + 1))
                if c == 0:
                    act.wait_ge(lb_var.sem, lb_var.at(b - 1, NC))
                    act.wait_ge(x2n.sem, x2n.at(b - 1, NC))
                    act.wait_ge(p2_mm.sem, p2_mm.at(b - 2, Q))
                    act.wait_ge(out_sent.sem, out_sent.at(b - 2, NC))
                else:
                    act.wait_ge(h_f.sem, h_f.at(b, c * KF))
                    act.wait_ge(g2_lo.sem, g2_lo.at(b, c * KF))
                act.activation(sq0[:], xn_chunk(c), ACT.Square).then_inc(li_sq.sem, 1)

            def l0_std(b, c):
                act.wait_ge(li_var.sem, li_var.at(b, c + 1))
                act.activation(rs0[:], psf[:, 1], ACT.Ln, bias=eps[:]).then_inc(li_ln.sem, 1)
                act.wait_ge(li_ln.sem, li_ln.at(b, c + 1))
                act.activation(rs0[:], rs0[:], ACT.Exp, scale=-0.5).then_inc(li_rstd.sem, 1)

            def ffn_task(b, c, task):
                kind, m = divmod(task, KF)
                k = c * KF + m
                if kind == 0:
                    bank = psf if m % 2 == 0 else psg
                    act.wait_ge(ab_mm.sem, ab_mm.at(b, k + 1))
                    act.wait_ge(h_f.sem, h_f.at(b, k - 1))
                    act.activation(sa[:, m % 2], bank[:, 0], ACT.Silu, scale=col("w1_s", m))\
                        .then_inc(silu_a.sem, 1)
                    act.wait_ge(h_f.sem, h_f.at(b, k + 1))
                    if m == 0:
                        act.wait_ge(g1_mm.sem, g1_mm.at(b, c * KF))
                    act.activation(hp[:, 0, m], tf[:, m % 2], ACT.Copy).then_inc(h_hi.sem, 1)
                elif kind == 1:
                    act.wait_ge(g1_mm.sem, g1_mm.at(b, k + 1))
                    if m < 2:
                        act.wait_ge(h_lo.sem, h_lo.at(b, c * KF + KF))
                    else:
                        act.wait_ge(g1_lo.sem, g1_lo.at(b, k - 1))
                    act.activation(tf[:, m % 2], psf[:, m % 2], ACT.Gelu, scale=s_g1[:, m:m + 1])\
                        .then_inc(g1_f.sem, 1)
                    act.wait_ge(g1_f.sem, g1_f.at(b, k + 1))
                    if m == 0:
                        act.wait_ge(g2_mm.sem, g2_mm.at(b, c * KF))
                    act.activation(g1p[:, 0, m], tf[:, m % 2], ACT.Copy, scale=G_UP).then_inc(g1_hi.sem, 1)
                else:
                    act.wait_ge(g2_mm.sem, g2_mm.at(b, k + 1))
                    if m < 2:
                        act.wait_ge(g1_lo.sem, g1_lo.at(b, c * KF + KF))
                    else:
                        act.wait_ge(g2_lo.sem, g2_lo.at(b, k - 1))
                    act.activation(tf[:, m % 2], psf[:, m % 2], ACT.Gelu, scale=s_g2[:, m:m + 1])\
                        .then_inc(g2_f.sem, 1)
                    act.wait_ge(g2_f.sem, g2_f.at(b, k + 1))
                    act.wait_ge(w3_mm.sem, w3_mm.at(b, k - 1))
                    act.activation(g2p[:, m % 2, 0], tf[:, m % 2], ACT.Copy).then_inc(g2_hi.sem, 1)

            def l0_gate(b, c):
                act.wait_ge(w3_mm.sem, w3_mm.at(b, (c + 1) * KF))
                act.wait_ge(le_mean.sem, le_mean.at(b - 1, c + 1))
                act.wait_ge(le_cen.sem, le_cen.at(b - 1, c + 1))
                for t in range(KD):
                    last = act.activation(gx[:, t, c * N:(c + 1) * N], psg[:, t], ACT.Silu,
                                          scale=col("w3_s", t))
                last.then_inc(gate0.sem, 1)

            def q_expo(b):
                act.wait_ge(q_min.sem, q_min.at(b, 1))
                act.activation(qe[:], qe[:], ACT.Exp).then_inc(q_exp.sem, 1)

            def turn_copy(b):
                act.wait_ge(turned.sem, turned.at(b, 1))
                act.activation(qt[:], psf[:, 0].rearrange("p (j c) -> p j c", j=2), ACT.Copy)\
                    .then_inc(qt_done.sem, 1)
                act.activation(vt[:], psf[:, 1].rearrange("p (j c) -> p j c", j=2), ACT.Copy)\
                    .then_inc(vt_done.sem, 1)

            def lb_square(b, c):
                act.wait_ge(lb_cen.sem, lb_cen.at(b, c + 1))
                act.wait_ge(lb_var.sem, lb_var.at(b, c))
                act.activation(sqb[:], chunk(y0, c), ACT.Square).then_inc(lb_sq.sem, 1)

            def lb_root(b, c):
                act.wait_ge(lb_var.sem, lb_var.at(b, c + 1))
                act.wait_ge(lb_step.sem, lb_step.at(b, LB_STEPS * c))
                act.activation(rsb[:], psf[:, 1], ACT.Ln, bias=eps[:]).then_inc(lb_ln.sem, 1)
                act.wait_ge(lb_ln.sem, lb_ln.at(b, c + 1))
                act.activation(rsb[:], rsb[:], ACT.Exp, scale=-0.5).then_inc(lb_rstd.sem, 1)

            def head_copy(b, c):
                act.wait_ge(x2n.sem, x2n.at(b, c + 1))
                act.wait_ge(out_ready.sem, out_ready.at(b - 1, c + 1))
                act.activation(chunk(x2, c), chunk(gx, c), ACT.Copy).then_inc(le_copy.sem, 1)

            def head_square(b, c):
                act.wait_ge(le_cen.sem, le_cen.at(b, c + 1))
                act.activation(sq1[:], xc[:], ACT.Square).then_inc(le_sq.sem, 1)

            def head_root(b, c):
                act.wait_ge(le_var.sem, le_var.at(b, c + 1))
                act.activation(v1[:], psy[:, 1], ACT.Ln, bias=eps[:]).then_inc(le_ln.sem, 1)
                act.wait_ge(le_ln.sem, le_ln.at(b, 2 * c + 1))
                act.activation(rs1[:], v1[:], ACT.Exp, scale=-0.5)
                act.activation(v1[:], v1[:], ACT.Exp, scale=-1.0).then_inc(le_rstd.sem, 1)

            def head_root1(b, c):
                act.wait_ge(le_step.sem, le_step.at(b, LE_STEPS * c + 1))
                act.activation(rs2[:], v1[:], ACT.Ln, bias=eps[:]).then_inc(le_ln.sem, 1)
                act.wait_ge(le_ln.sem, le_ln.at(b, 2 * c + 2))
                act.activation(rs2[:], rs2[:], ACT.Exp, scale=-0.5).then_inc(le_rstd1.sem, 1)

            def head_b16(b, c):
                act.wait_ge(le_step.sem, le_step.at(b, LE_STEPS * c + 2))
                act.activation(chunk(xb, c), xc[:], ACT.Copy).then_inc(le_xb.sem, 1)

            def softplus(b, c):
                act.wait_ge(z_done.sem, z_done.at(b, c + 1))
                act.activation(lt[:], zt[:], ACT.Abs).then_inc(z_abs.sem, 1)
                act.wait_ge(z_abs.sem, z_abs.at(b, c + 1))
                act.activation(lt[:], lt[:], ACT.Exp, scale=-1.0).then_inc(z_exp.sem, 1)
                act.wait_ge(z_exp.sem, z_exp.at(b, c + 1))
                act.activation(lt[:], lt[:], ACT.Ln, bias=1.0).then_inc(z_ln.sem, 1)

            def decay(b, c, n):
                k = c * NS + n
                if n == 0:
                    act.wait_ge(head_done.sem, head_done.at(b, c + 1))
                act.wait_ge(scan_done.sem, scan_done.at(b, k - 3))
                for t in range(KD):
                    last = act.activation(da[:, n % 4, t], delta[:, t], ACT.Exp, scale=aneg[:, t, n:n + 1])
                last.then_inc(da_done.sem, 1)

            def lf_square(b, c):
                act.wait_ge(lf_cen.sem, lf_cen.at(b, c + 1))
                act.wait_ge(lf_var.sem, lf_var.at(b, c))
                act.wait_ge(out_sent.sem, out_sent.at(b - 1, NC))
                act.activation(sq2[:], nrm[:, c], ACT.Square).then_inc(lf_sq.sem, 1)

            def lf_root(b, c):
                act.wait_ge(lf_var.sem, lf_var.at(b, c + 1))
                act.wait_ge(lf_step.sem, lf_step.at(b, 2 * c))
                act.activation(rs3[:], psb[:, 1], ACT.Ln, bias=eps[:]).then_inc(lf_ln.sem, 1)
                act.wait_ge(lf_ln.sem, lf_ln.at(b, c + 1))
                act.activation(rs3[:], rs3[:], ACT.Exp, scale=-0.5).then_inc(lf_rstd.sem, 1)

            def hidden1(b, c, m):
                k = c * KF + m
                act.wait_ge(f1_mm.sem, f1_mm.at(b, k + 1))
                act.wait_ge(f2_mm.sem, f2_mm.at(b, k - 1))
                act.activation(hff[:, m % 2], psy[:, m % 2], ACT.Gelu, bias=col("b1", m))\
                    .then_inc(f1_done.sem, 1)

            def expert_square(b, c):
                if c == 0:
                    act.wait_ge(le_xb.sem, le_xb.at(b, NC))
                    act.wait_ge(lf_var.sem, lf_var.at(b, NC))
                else:
                    act.wait_ge(m_ms.sem, m_ms.at(b, c))
                act.activation(sqm[:], chunk(xb, c), ACT.Square).then_inc(m_sq.sem, 1)

            def expert_root(b, c):
                act.wait_ge(m_ms.sem, m_ms.at(b, c + 1))
                act.wait_ge(m_step.sem, m_step.at(b, c))
                act.activation(rsm[:], psg[:, 1], ACT.Ln, bias=eps[:]).then_inc(m_ln.sem, 1)
                act.wait_ge(m_ln.sem, m_ln.at(b, c + 1))
                act.activation(rsm[:], rsm[:], ACT.Exp, scale=-0.5).then_inc(m_rms.sem, 1)

            def gate_exp(b):
                act.wait_ge(gate_d.sem, gate_d.at(b, 1))
                act.activation(gex[:], gex[:], ACT.Exp).then_inc(gate_e.sem, 1)

            def gate_copy(b, k):
                act.wait_ge(cb_mm.sem, cb_mm.at(b, k + 1))
                if k >= NB:
                    act.wait_ge(sc_done.sem, sc_done.at(b, (k - NB + 1) * KD))
                act.activation(cb[:, k % NB], psf[:, k % 2], ACT.Copy, scale=1.0 / ALPHA)\
                    .then_inc(cb_done.sem, 1)

            def expert_silu(b, r):
                act.wait_ge(gmin_done.sem, gmin_done.at(b, r + 1))
                act.activation(gate[:, r % NB], gate[:, r % NB], ACT.Silu, scale=ALPHA)\
                    .then_inc(sg_done.sem, 1)

            def expert_high(b, r):
                act.wait_ge(af_done.sem, af_done.at(b, r + 1))
                if r >= NB:
                    act.wait_ge(p2_mm.sem, p2_mm.at(b, r - NB + 1))
                act.activation(ap2[:, r % NB, 0], af[:, r % NB], ACT.Copy).then_inc(ahi_done.sem, 1)

            def expert_gate(b, c):
                act.wait_ge(moe_s.sem, moe_s.at(b, c + 1))
                if c >= 1:
                    act.wait_ge(out_m.sem, out_m.at(b, c))
                act.activation(gate1[:], sum16[:], ACT.Silu).then_inc(moe_g.sem, 1)

            def batch(b0, b1):
                for c in range(NC):
                    if b1 is not None:
                        head_copy(b1, c)
                    if b0 is not None:
                        l0_square(b0, c)
                    if b1 is not None:
                        head_square(b1, c)
                    if b0 is not None:
                        l0_std(b0, c)
                    if b1 is not None:
                        head_root(b1, c)
                        head_root1(b1, c)
                    if b0 is not None:
                        split_input(b0, c)
                    if b1 is not None:
                        head_b16(b1, c)
                        softplus(b1, c)
                        decay(b1, c, 0)
                        decay(b1, c, 1)
                    for n in range(NS):
                        if b1 is not None and n % 2 == 0 and n + 2 < NS:
                            decay(b1, c, n + 2)
                            decay(b1, c, n + 3)
                        if b0 is not None:
                            for task in tasks(n):
                                ffn_task(b0, c, task)
                    if b0 is not None:
                        l0_gate(b0, c)
                if b1 is not None:
                    for c in range(NC):
                        lf_square(b1, c)
                        lf_root(b1, c)
                if b1 is None:
                    q_expo(b0)
                    turn_copy(b0)
                else:
                    expert_square(b1, 0)
                    for k in range(NC * KF):
                        if k == RMS_AT:
                            expert_root(b1, 0)
                            expert_square(b1, 1)
                        if k == RMS1_AT:
                            expert_root(b1, 1)
                        if b0 is not None and k == ATTN_AT:
                            q_expo(b0)
                            turn_copy(b0)
                        if k == NUM_AT:
                            gate_exp(b1)
                        hidden1(b1, *divmod(k, KF))
                if b0 is not None:
                    for c in range(NC):
                        lb_square(b0, c)
                        lb_root(b0, c)
                if b1 is not None:
                    gate_copy(b1, 0)
                    for r in range(Q + LAG):
                        if r < Q:
                            expert_silu(b1, r)
                        if r >= LAG:
                            expert_high(b1, r - LAG)
                        if r % KD == 0 and r // KD + 1 < NC * E:
                            gate_copy(b1, r // KD + 1)
                        if r == NQ + LAG_DOWN + 1:
                            expert_gate(b1, 0)
                    expert_gate(b1, 1)

            act.wait_ge(dve_const, DVE_CONST)
            batch(0, None)
            next_turn(act, "act")
            with act.Fori(0, B - 1):
                batch(0, -1)
                next_turn(act, "act")
            batch(None, -1)

        @block.tensor
        def _(pe):
            def average(out, rhs):
                for k in range(KD):
                    last = pe.matmul(out, meanw[:], rhs[:, k], start=(k == 0), stop=(k == KD - 1))
                return last

            def l0_mean(b, c):
                pe.wait_ge(x_in[c].sem, x_in[c].at(b, 1))
                if c == 0:
                    pe.wait_ge(lb_cen.sem, lb_cen.at(b - 1, NC))
                else:
                    pe.wait_ge(g2_f.sem, g2_f.at(b, c * KF))
                average(psf[:, 0], xn_chunk(c)).then_inc(li_mean.sem, 1)

            def l0_var(b, c):
                pe.wait_ge(li_sq.sem, li_sq.at(b, c + 1))
                if c == 0:
                    pe.wait_ge(lb_ln.sem, lb_ln.at(b - 1, NC))
                average(psf[:, 1], sq0).then_inc(li_var.sem, 1)

            def ffn_task(b, c, task):
                kind, m = divmod(task, KF)
                k = c * KF + m
                cols = slice(m * P, (m + 1) * P)
                if kind == 0:
                    bank = psf if m % 2 == 0 else psg
                    if m == 0:
                        pe.wait_ge(li_lo.sem, li_lo.at(b, c + 1))
                        pe.wait_ge(li_ln.sem, li_ln.at(b, c + 1))
                    elif m == 1 and c == 0:
                        pe.wait_ge(lin_done.sem, lin_done.at(b - 2, Q))
                        pe.wait_ge(gate0.sem, gate0.at(b - 1, NC))
                        pe.wait_ge(kv_masked.sem, kv_masked.at(b - 1, 1))
                    elif m == 1:
                        pe.wait_ge(gate0.sem, gate0.at(b, c))
                    if m >= 2:
                        pe.wait_ge(silu_a.sem, silu_a.at(b, k - 1))
                        pe.wait_ge(h_f.sem, h_f.at(b, k - 1))
                    for half, w in enumerate((w1, w2)):
                        for t in range(KD):
                            for part in range(2):
                                last = pe.matmul(bank[:, half], w[:, t, cols], xp[:, part, t],
                                                 start=(t == 0 and part == 0),
                                                 stop=(t == KD - 1 and part == 1))
                    last.then_inc(ab_mm.sem, 1)
                    return
                if kind == 1:
                    src, w, mm, free = hp, h1w, g1_mm, g1_f
                    if m == 0:
                        pe.wait_ge(h_hi.sem, h_hi.at(b, (c + 1) * KF))
                        pe.wait_ge(h_lo.sem, h_lo.at(b, (c + 1) * KF))
                else:
                    src, w, mm, free = g1p, h2w, g2_mm, g2_f
                    if m == 0:
                        pe.wait_ge(g1_hi.sem, g1_hi.at(b, (c + 1) * KF))
                        pe.wait_ge(g1_lo.sem, g1_lo.at(b, (c + 1) * KF))
                if m >= 2:
                    pe.wait_ge(free.sem, free.at(b, k - 1))
                for t in range(KF):
                    for part in range(2):
                        last = pe.matmul(psf[:, m % 2], w[:, t, cols], src[:, part, t],
                                         start=(t == 0 and part == 0), stop=(t == KF - 1 and part == 1))
                last.then_inc(mm.sem, 1)
                if kind == 2 and m >= 1:
                    project(b, c, m - 1)

            def project(b, c, m):
                k = c * KF + m
                pe.wait_ge(g2_hi.sem, g2_hi.at(b, k + 1))
                pe.wait_ge(g2_lo.sem, g2_lo.at(b, k + 1))
                for t in range(KD):
                    for part in range(2):
                        last = pe.matmul(psg[:, t], w3[:, m, t * P:(t + 1) * P], g2p[:, m % 2, part],
                                         start=(m == 0 and part == 0), stop=(m == KF - 1 and part == 1))
                last.then_inc(w3_mm.sem, 1)

            def attention_turn(b):
                pe.wait_ge(q_done.sem, q_done.at(b, 1))
                pe.wait_ge(g2_f.sem, g2_f.at(b, NC * KF))
                for half, src in enumerate((q0, l2)):
                    for j in range(2):
                        for t in range(KD):
                            last = pe.transpose(psf[:, half, (j * KD + t) * P:(j * KD + t + 1) * P],
                                                src[:, t, j * P:(j + 1) * P], ident[:])
                last.then_inc(turned.sem, 1)

            def attention_kv(b):
                pe.wait_ge(qt_done.sem, qt_done.at(b, 1))
                pe.wait_ge(vt_done.sem, vt_done.at(b, 1))
                pe.wait_ge(gate0.sem, gate0.at(b, NC))
                for t in range(KD):
                    for j in range(2):
                        last = pe.matmul(psg[:, 0, t * P:(t + 1) * P], qt[:, j, t * P:(t + 1) * P],
                                         vt[:, j, t * P:(t + 1) * P], start=(j == 0), stop=(j == 1))
                last.then_inc(kv_mm.sem, 1)

            def attention_num(b):
                pe.wait_ge(kv_masked.sem, kv_masked.at(b, 1))
                for half, w in enumerate((kvm, zm)):
                    for t in range(KD):
                        last = pe.matmul(psf[:, half, t * N // 2:(t + 1) * N // 2], w[:, t], q0[:, t],
                                         start=True, stop=True)
                last.then_inc(num_mm.sem, 1)

            def lb_average(b, c):
                pe.wait_ge(y_done.sem, y_done.at(b, 1))
                pe.wait_ge(lb_cen.sem, lb_cen.at(b, c))
                average(psf[:, 0], chunk(y0, c)).then_inc(lb_mean.sem, 1)

            def lb_variance(b, c):
                pe.wait_ge(lb_sq.sem, lb_sq.at(b, c + 1))
                pe.wait_ge(lb_ln.sem, lb_ln.at(b, c))
                average(psf[:, 1], sqb).then_inc(lb_var.sem, 1)

            def head_mean(b, c):
                pe.wait_ge(x2n.sem, x2n.at(b, c + 1))
                if c == 0:
                    pe.wait_ge(lin_done.sem, lin_done.at(b - 1, Q))
                else:
                    pe.wait_ge(ssm_done.sem, ssm_done.at(b, c))
                average(psy[:, 0], chunk(gx, c)).then_inc(le_mean.sem, 1)

            def head_var(b, c):
                pe.wait_ge(le_sq.sem, le_sq.at(b, c + 1))
                average(psy[:, 1], sq1).then_inc(le_var.sem, 1)

            def head_project(b, c):
                pe.wait_ge(le_step.sem, le_step.at(b, LE_STEPS * c + HEAD_STEPS))
                for t in range(KD):
                    for k in range(KD):
                        last = pe.matmul(psy[:, t], wd[:, k, t * P:(t + 1) * P], xn1[:, k],
                                         start=(k == 0), stop=(k == KD - 1))
                last.then_inc(dt_mm.sem, 1)
                if c == 0:
                    pe.wait_ge(moe_r.sem, moe_r.at(b - 1, NC))
                else:
                    pe.wait_ge(u_done.sem, u_done.at(b, c * NS))
                for k in range(KD):
                    last = pe.matmul(psb[0:64, 0], wbc[:, k], xn1[:, k], start=(k == 0), stop=(k == KD - 1))
                last.then_inc(bc_mm.sem, 1)

            def spread_bc(b, c, n):
                k = c * NS + n
                if n == 0:
                    pe.wait_ge(head_done.sem, head_done.at(b, c + 1))
                else:
                    pe.wait_ge(u_done.sem, u_done.at(b, k))
                pe.matmul(psb[:, 0], sel[:, n:n + 1].broadcast_to([64, P]), bcs[:], start=True, stop=True)\
                    .then_inc(b_mm.sem, 1)
                if n == 0 and c == 0:
                    pe.wait_ge(moe_r.sem, moe_r.at(b - 1, NC))
                else:
                    pe.wait_ge(cy_done.sem, cy_done.at(b, k))
                pe.matmul(psb[:, 1], sel[:, NS + n:NS + n + 1].broadcast_to([64, P]), bcs[:],
                          start=True, stop=True).then_inc(c_mm.sem, 1)

            def sum_states(b, c, n):
                k = c * NS + n
                pe.wait_ge(pair_done.sem, pair_done.at(b, k // 2 + 1))
                for t in range(KD):
                    last = pe.matmul(psy[:, t], ident[:], u[:, n % 4, t], start=(n == 0), stop=(n == NS - 2))
                last.then_inc(y_acc.sem, 1)

            def lf_average(b, c):
                if c == 0:
                    pe.wait_ge(ssm_done.sem, ssm_done.at(b, NC))
                else:
                    pe.wait_ge(lf_cen.sem, lf_cen.at(b, c))
                average(psb[:, 0], chunk(so, c)).then_inc(lf_mean.sem, 1)

            def lf_variance(b, c):
                pe.wait_ge(lf_sq.sem, lf_sq.at(b, c + 1))
                if c == 1:
                    pe.wait_ge(lf_ln.sem, lf_ln.at(b, c))
                average(psb[:, 1], sq2).then_inc(lf_var.sem, 1)

            def hidden1(b, c, m):
                k = c * KF + m
                if m == 0:
                    pe.wait_ge(lf_step.sem, lf_step.at(b, 2 * NC))
                if k >= 2:
                    pe.wait_ge(f1_done.sem, f1_done.at(b, k - 1))
                for t in range(KD):
                    last = pe.matmul(psy[:, m % 2], wf1[:, t, m * P:(m + 1) * P], nrm[:, c, t],
                                     start=(t == 0), stop=(t == KD - 1))
                last.then_inc(f1_mm.sem, 1)

            def hidden2(b, c, m):
                k = c * KF + m
                pe.wait_ge(f1_done.sem, f1_done.at(b, k + 1))
                if m == 0:
                    pe.wait_ge(lf_ln.sem, lf_ln.at(b, NC))
                    pe.wait_ge(block_done.sem, block_done.at(b, c))
                for t in range(KD):
                    last = pe.matmul(psb[:, t], wf2[:, m, t * P:(t + 1) * P], hff[:, m % 2],
                                     start=(m == 0), stop=(m == KF - 1))
                last.then_inc(f2_mm.sem, 1)

            def expert_mean(b, c, ahead):
                pe.wait_ge(m_sq.sem, m_sq.at(b, c + 1))
                if c == 0:
                    pe.wait_ge(gate0.sem, gate0.at(ahead, NC))
                else:
                    pe.wait_ge(m_ln.sem, m_ln.at(b, c))
                average(psg[:, 1], sqm).then_inc(m_ms.sem, 1)

            def expert_logits(b):
                pe.wait_ge(m_ln.sem, m_ln.at(b, NC))
                pe.wait_ge(nf_done.sem, nf_done.at(b, NC))
                for j in range(NJ):
                    out = psg[:, 1, j * E:(j + 1) * E]
                    c, at = divmod(j * P, N)
                    for t in range(KD):
                        pe.matmul(out, nf[:, c, t, at:at + P], wgate[:, t], start=(t == 0), stop=False)
                    last = pe.matmul(out, ones16[:], gbias[:], start=False, stop=True)
                last.then_inc(gate_mm.sem, 1)

            def expert_turn(b, c):
                pe.wait_ge(comb_done.sem, comb_done.at(b, 1))
                if c >= 1:
                    pe.wait_ge(ct_done.sem, ct_done.at(b, 2 * c - 1))
                for j in range(N // P):
                    last = pe.transpose(psg[0:64, 1, j * P:(j + 1) * P], comb[:, c * N // P + j], ident[:])
                last.then_inc(comb_t.sem, 1)

            def expert_spread(b, k, ahead):
                if k < 2:
                    pe.wait_ge(cs_done.sem, cs_done.at(b, NC))
                    pe.wait_ge(lb_cen.sem, lb_cen.at(ahead, NC))
                    pe.wait_ge(lb_ln.sem, lb_ln.at(ahead, NC))
                else:
                    pe.wait_ge(cb_done.sem, cb_done.at(b, k - 1))
                c, e = divmod(k, E)
                pe.matmul(psf[:, k % 2], sel[:, e:e + 1].broadcast_to([64, P]), cs[:, c],
                          start=True, stop=True).then_inc(cb_mm.sem, 1)

            def expert_up(b, r, ahead):
                c, q = divmod(r, NQ)
                e, t = divmod(q, KD)
                bank = psy if r % 2 == 0 else psg
                if r == 0:
                    pe.wait_ge(mw_in.sem, mw_in.at(b, 2))
                    pe.wait_ge(f1_done.sem, f1_done.at(b, NC * KF))
                elif r == 1:
                    pe.wait_ge(kv_masked.sem, kv_masked.at(ahead, 1))
                    pe.wait_ge(ct_done.sem, ct_done.at(b, 2 * NC))
                else:
                    pe.wait_ge(lin_done.sem, lin_done.at(b, r - 1))
                for half in range(2):
                    for kk in range(KD):
                        last = pe.matmul(bank[:, half], mw1[:, e, kk, half, t * P:(t + 1) * P], nf[:, c, kk],
                                         start=(kk == 0), stop=(kk == KD - 1))
                last.then_inc(p1_mm.sem, 1)

            def expert_down(b, r):
                c, q = divmod(r, NQ)
                e, t = divmod(q, KD)
                if q == 0:
                    if c == 0:
                        pe.wait_ge(block_done.sem, block_done.at(b, NC))
                    else:
                        pe.wait_ge(moe_r.sem, moe_r.at(b, c))
                    for h in range(KD):
                        pe.matmul(psb[:, h], b2s[:, h * P:(h + 1) * P], cs[:, c], start=True, stop=False)
                pe.wait_ge(alo_done.sem, alo_done.at(b, r + 1))
                for h in range(KD):
                    for part in range(2):
                        last = pe.matmul(psb[:, h], mw2[:, e, t, h * P:(h + 1) * P], ap2[:, r % NB, part],
                                         start=False, stop=(q == NQ - 1 and part == 1))
                last.then_inc(p2_mm.sem, 1)

            def batch(b0, b1):
                for c in range(NC):
                    if b0 is not None:
                        l0_mean(b0, c)
                    if b1 is not None:
                        head_mean(b1, c)
                    if b0 is not None:
                        l0_var(b0, c)
                    if b1 is not None:
                        head_var(b1, c)
                        head_project(b1, c)
                    for n in range(NS):
                        if b1 is not None:
                            spread_bc(b1, c, n)
                        if b0 is not None:
                            for task in tasks(n):
                                ffn_task(b0, c, task)
                        if b1 is not None and n % 2 == 1 and n >= 3:
                            sum_states(b1, c, n - 3)
                    if b1 is not None:
                        sum_states(b1, c, NS - 2)
                    if b0 is not None:
                        project(b0, c, KF - 1)
                ahead = 0 if b0 is not None else b1
                if b1 is not None:
                    for c in range(NC):
                        lf_average(b1, c)
                        lf_variance(b1, c)
                    for k in range(NC * KF + 1):
                        if k == RMS_AT:
                            expert_mean(b1, 0, ahead)
                        if k == RMS1_AT:
                            expert_mean(b1, 1, ahead)
                        if k == LOGITS_AT:
                            expert_logits(b1)
                        if b0 is not None and k == ATTN_AT:
                            attention_turn(b0)
                            attention_kv(b0)
                        if b0 is not None and k == NUM_AT:
                            attention_num(b0)
                        if k == TURN_AT:
                            expert_turn(b1, 0)
                        if k == TURN1_AT:
                            expert_turn(b1, 1)
                        if k < NC * KF:
                            hidden1(b1, *divmod(k, KF))
                        if k >= 1:
                            hidden2(b1, *divmod(k - 1, KF))
                elif b0 is not None:
                    attention_turn(b0)
                    attention_kv(b0)
                    attention_num(b0)
                if b0 is not None:
                    for c in range(NC):
                        lb_average(b0, c)
                        lb_variance(b0, c)
                if b1 is not None:
                    expert_spread(b1, 0, ahead)
                    for r in range(Q + LAG_DOWN):
                        if r < Q:
                            expert_up(b1, r, ahead)
                        if r % KD == 0 and r // KD + 1 < NC * E:
                            expert_spread(b1, r // KD + 1, ahead)
                        if r >= LAG_DOWN:
                            expert_down(b1, r - LAG_DOWN)

            pe.wait_ge(dve_const, DVE_CONST)
            pe.wait_ge(pool_const, POOL_CONST)
            pe.wait_ge(w12_in, 32)
            pe.wait_ge(h1_in, 16)
            pe.wait_ge(h2_in, 16)
            pe.wait_ge(w3_in, 16)
            batch(0, None)
            pe.wait_ge(wl1_in, 64)
            pe.wait_ge(packs_in, 64)
            pe.wait_ge(b2_in, 32)
            next_turn(pe, "pe")
            with pe.Fori(0, B - 1):
                batch(0, -1)
                next_turn(pe, "pe")
            batch(None, -1)

        @block.vector
        def _(dve):
            k = 0

            def const(ins):
                nonlocal k
                k += 1
                ins.then_inc(dve_const, 1)

            dve.memset(b2s[:].bitcast(F32), 0.0).then_inc(b2s_zero, 1)
            const(dve.memset(meanw[:], 1.0 / D))
            const(dve.memset(eps[:], LN_EPS))
            const(dve.memset(ones16[:], 1.0))
            for side in (0, L + 1):
                const(dve.memset(xn[:, :, side:side + 1], 0.0))
            dve.wait_ge(pool_const, POOL_CONST)
            const(dve.tensor_tensor(sel[:], ident[0:64, 0:32], ident[0:64, 32:64], ALU.add))
            dve.wait_ge(packs_in, 64)
            for j, name in enumerate(("h_synth", "g_synth")):
                lo, hi = PACK[name]
                f = pk[:, lo:hi].rearrange("p (t k) -> p t k", k=4)
                const(dve.tensor_copy(synth[:, j, :, 0:1], f[:, :, 0:1]))
                const(dve.tensor_tensor(synth[:, j, :, 1:2], f[:, :, 1:2], f[:, :, 2:3], ALU.add))
                const(dve.tensor_copy(synth[:, j, :, 2:3], f[:, :, 3:4]))
                const(dve.tensor_tensor(synth[:, j, :, 3:4], f[:, :, 0:1], f[:, :, 1:2], ALU.add))
                const(dve.tensor_tensor(synth[:, j, :, 4:5], f[:, :, 2:3], f[:, :, 3:4], ALU.add))
            const(dve.tensor_scalar(s_h[:], col("w2_s", 0, KF), H_UP, None, ALU.mult))
            const(dve.tensor_scalar(s_g1[:], col("h1_s", 0, KF), 1.0 / H_UP, None, ALU.mult))
            const(dve.tensor_scalar(s_g2[:], col("h2_s", 0, KF), 1.0 / G_UP, None, ALU.mult))
            const(dve.tensor_copy(mbias[:], mbias16[:]))
            dve.wait_ge(dve_const, k)
            blin = mbias[:, :, 1]
            const(dve.tensor_scalar(lin_lo[:], blin, -1.0, -LIMIT, ALU.mult, ALU.add))
            const(dve.tensor_scalar(lin_hi[:], blin, -1.0, LIMIT, ALU.mult, ALU.add))
            const(dve.tensor_scalar(lin_one[:], blin, 1.0, None, ALU.add))
            dve.wait_ge(act_const, 1)
            const(dve.tensor_scalar(aneg[:], aneg[:], -1.0, None, ALU.mult))
            dve.wait_ge(dve_const, k)
            assert k == DVE_CONST

            def l0_center(b, c):
                dve.wait_ge(li_mean.sem, li_mean.at(b, c + 1))
                dve.tensor_tensor(xn_chunk(c), xn_chunk(c), both(psf[:, 0]), ALU.subtract)\
                    .then_inc(li_cen.sem, 1)

            def l0_scale(b, c):
                dve.wait_ge(li_rstd.sem, li_rstd.at(b, c + 1))
                dve.tensor_tensor(xn_chunk(c), xn_chunk(c), both(rs0[:]), ALU.mult).then_inc(li_xn.sem, 1)

            def ffn_task(b, c, task):
                kind, m = divmod(task, KF)
                k = c * KF + m
                if kind == 0:
                    bank = psf if m % 2 == 0 else psg
                    dve.wait_ge(silu_a.sem, silu_a.at(b, k + 1))
                    if m >= 2:
                        dve.wait_ge(h_lo.sem, h_lo.at(b, k - 1))
                    elif c >= 1:
                        dve.wait_ge(g2_lo.sem, g2_lo.at(b, c * KF))
                    else:
                        dve.wait_ge(x2n.sem, x2n.at(b - 1, NC))
                    dve.scalar_tensor_tensor(tf[:, m % 2], bank[:, 1], s_h[:, m:m + 1], sa[:, m % 2],
                                             ALU.mult, ALU.mult).then_inc(h_f.sem, 1)
                elif kind == 1:
                    dve.wait_ge(g1_hi.sem, g1_hi.at(b, k + 1))
                    dve.scalar_tensor_tensor(g1p[:, 1, m], tf[:, m % 2], G_UP, g1p[:, 0, m],
                                             ALU.mult, ALU.subtract).then_inc(g1_lo.sem, 1)

            def wavelets_and_attention(b, b1):
                n = 0

                def step(ins):
                    nonlocal n
                    n += 1
                    ins.then_inc(conv.sem, 1)

                def settle(back):
                    dve.wait_ge(conv.sem, conv.at(b, n - back))

                def filters(terms, lag):
                    depth = max(len(t) for _, t, _ in terms)
                    for j in range(depth):
                        for out, views, base in terms:
                            if j >= len(views):
                                continue
                            view, scalar = views[j]
                            if n:
                                settle(0 if len(terms) < 2 else lag)
                            if j == 0 and base is None:
                                step(dve.tensor_scalar(out, view, scalar, None, ALU.mult))
                            else:
                                step(dve.scalar_tensor_tensor(out, view, scalar, out if j else base,
                                                              ALU.mult, ALU.add))

                def taps(name, t):
                    lo, _ = PACK[name]
                    return [pk[:, lo + 4 * t + j:lo + 4 * t + j + 1] for j in range(4)]

                def analysis(src, width, low, high):
                    terms = []
                    for t in range(KD):
                        for name, out in (("h_filter", low), ("g_filter", high)):
                            f = taps(name, t)
                            views = [(src[:, t, j:j + width - 1:2], f[j]) for j in range(4)]
                            terms.append((out(t), views, None))
                    filters(terms, 3)

                dve.wait_ge(gate0.sem, gate0.at(b, NC))
                half, quarter = L // 2, L // 4
                for buf, width in ((l1b, half), (h1b, half), (h2b, quarter), (low2, quarter), (low1, half)):
                    for side in (0, width + 1):
                        step(dve.memset(buf[:, :, side:side + 1], 0.0))
                analysis(xn, L, lambda t: l1b[:, t, 1:half + 1], lambda t: h1b[:, t, 1:half + 1])
                if b1 is not None:
                    expert_norm(b1, 0)
                    expert_norm(b1, 1)
                settle(0)
                analysis(l1b, half, lambda t: l2[:, t, :], lambda t: h2b[:, t, 1:quarter + 1])
                settle(0)
                dve.tensor_scalar(qe[:], l2[:], 0.0, None, ALU.min).then_inc(q_min.sem, 1)
                dve.wait_ge(q_exp.sem, q_exp.at(b, 1))
                dve.scalar_tensor_tensor(q0[:], l2[:], 0.0, qe[:], ALU.max, ALU.add).then_inc(q_done.sem, 1)
                dve.wait_ge(q_done.sem, q_done.at(b, 1))
                step(dve.tensor_reduce(zs[:], q0[:], AX_X, ALU.add))
                settle(0)
                for t in range(KD):
                    step(dve.tensor_scalar(zm[:, t], headmask[:], zs[:, t:t + 1], None, ALU.mult))
                if b1 is not None:
                    expert_gate(b1)
                dve.wait_ge(kv_mm.sem, kv_mm.at(b, 1))
                settle(0)
                dve.tensor_tensor(kvm[:], psg[:, 0, 0:KD * P].rearrange("p (t n) -> p t n", t=KD),
                                  headmask[:].rearrange("p (o n) -> p o n", o=1).broadcast_to([P, KD, P]),
                                  ALU.mult).then_inc(kv_masked.sem, 1)
                dve.wait_ge(num_mm.sem, num_mm.at(b, 1))
                step(dve.tensor_scalar(rden[:], psf[:, 1].rearrange("p (t n) -> p t n", t=KD), ATTN_EPS,
                                       None, ALU.add))
                settle(0)
                step(dve.reciprocal(rden[:], rden[:]))
                settle(0)
                step(dve.tensor_tensor(low2[:, :, 1:quarter + 1],
                                       psf[:, 0].rearrange("p (t n) -> p t n", t=KD), rden[:], ALU.mult))
                settle(0)

                def synthesis(low, high, width, out, base):
                    terms = []
                    for t in range(KD):
                        for odd in range(2):
                            views = []
                            for j, src in enumerate((low, high)):
                                f = [synth[:, j, t, i:i + 1] for i in range(5)]
                                if odd:
                                    views += [(src[:, t, 1:width + 1], f[3]), (src[:, t, 2:width + 2], f[4])]
                                else:
                                    views += [(src[:, t, i:width + i], f[i]) for i in range(3)]
                            terms.append((out(t, odd), views, base(t, odd) if base else None))
                    filters(terms, 1)

                if b1 is not None:
                    block_out(b1, 0)
                synthesis(low2, h2b, quarter, lambda t, odd: low1[:, t, 1 + odd:half + odd:2], None)
                settle(0)
                if b1 is not None:
                    expert_parts(b1, 0)
                    expert_parts(b1, 1)
                synthesis(low1, h1b, half, lambda t, odd: y0[:, t, odd:L - 1 + odd:2],
                          lambda t, odd: xn[:, t, 1 + odd:L + odd:2])
                assert n == conv.per
                settle(0)
                dve.memset(zs[:], 0.0).then_inc(y_done.sem, 1)

            def lb_center(b, c):
                dve.wait_ge(lb_mean.sem, lb_mean.at(b, c + 1))
                dve.tensor_tensor(chunk(y0, c), chunk(y0, c), both(psf[:, 0]), ALU.subtract)\
                    .then_inc(lb_cen.sem, 1)

            def lb_scale(b, c):
                dve.wait_ge(lb_rstd.sem, lb_rstd.at(b, c + 1))
                dve.tensor_tensor(chunk(y0, c), chunk(y0, c), both(rsb[:]), ALU.mult).then_inc(lb_step.sem, 1)
                dve.wait_ge(lb_step.sem, lb_step.at(b, LB_STEPS * c + 1))
                for t in range(KD):
                    part = y0[:, t, c * N:(c + 1) * N]
                    dve.tensor_scalar(part, part, col("gamma", t), col("beta", t), ALU.mult, ALU.add)\
                        .then_inc(lb_step.sem, 1)

            def head_center(b, c):
                dve.wait_ge(le_mean.sem, le_mean.at(b, c + 1))
                if c == 0:
                    dve.wait_ge(p2_mm.sem, p2_mm.at(b - 1, Q))
                    dve.wait_ge(out_m.sem, out_m.at(b - 1, NC))
                dve.tensor_tensor(xc[:], chunk(gx, c), both(psy[:, 0]), ALU.subtract).then_inc(le_cen.sem, 1)

            def head_norm(b, c):
                at = LE_STEPS * c

                def step(ins):
                    nonlocal at
                    at += 1
                    ins.then_inc(le_step.sem, 1)
                    dve.wait_ge(le_step.sem, le_step.at(b, at))

                dve.wait_ge(le_rstd.sem, le_rstd.at(b, c + 1))
                step(dve.tensor_tensor(v1[:], psy[:, 1], v1[:], ALU.mult))
                step(dve.tensor_tensor(xc[:], xc[:], both(rs1[:]), ALU.mult))
                dve.wait_ge(le_rstd1.sem, le_rstd1.at(b, c + 1))
                step(dve.tensor_tensor(xn1[:], xc[:], both(rs2[:]), ALU.mult))
                last = [dve.tensor_scalar(xn1[:, t], xn1[:, t], col("ln1_g", t), col("ln1_b", t),
                                          ALU.mult, ALU.add) for t in range(KD)][-1]
                step(last)

            def head_rest(b, c):
                for t in range(KD):
                    if t == 0:
                        dve.wait_ge(dt_mm.sem, dt_mm.at(b, c + 1))
                    last = dve.tensor_scalar(zt[:, t], psy[:, t], col("bd", t), None, ALU.add)
                last.then_inc(z_done.sem, 1)
                at = LE_STEPS * c + HEAD_STEPS

                def step(ins):
                    nonlocal at
                    at += 1
                    ins.then_inc(le_step.sem, 1)
                    dve.wait_ge(le_step.sem, le_step.at(b, at))

                dve.wait_ge(bc_mm.sem, bc_mm.at(b, c + 1))
                step(dve.tensor_scalar(bcf[:], psb[0:64, 0], col("bbc")[0:64], None, ALU.add))
                step(dve.tensor_copy(bcs[:], bcf[:]))
                step(dve.tensor_tensor(bcs[32:64], bcf[32:64], bcs[32:64].bitcast(F32), ALU.subtract))
                for t in range(KD):
                    last = dve.scalar_tensor_tensor(so[:, t, c * N:(c + 1) * N], xn1[:, t], col("D", t),
                                                    xc[:, t], ALU.mult, ALU.add)
                step(last)
                dve.wait_ge(z_ln.sem, z_ln.at(b, c + 1))
                step(dve.scalar_tensor_tensor(delta[:], zt[:], 0.0, lt[:], ALU.max, ALU.add))
                assert at == LE_STEPS * (c + 1)
                dve.tensor_tensor(dx[:], delta[:], xn1[:], ALU.mult).then_inc(head_done.sem, 1)

            def state(b, c, n):
                k = c * NS + n
                s = n % 4
                dve.wait_ge(b_mm.sem, b_mm.at(b, k + 1))
                if n >= 4:
                    dve.wait_ge(y_acc.sem, y_acc.at(b, (k - 4) // 2 + 1))
                dve.tensor_tensor(u[:, s], dx[:], both(psb[:, 0]), ALU.mult).then_inc(u_done.sem, 1)
                dve.wait_ge(u_done.sem, u_done.at(b, k + 1))
                dve.wait_ge(da_done.sem, da_done.at(b, k + 1))
                for t in range(KD):
                    last = dve.tensor_tensor_scan(u[:, s, t], da[:, s, t], u[:, s, t],
                                                  0.0 if c == 0 else carry[:, t, n:n + 1],
                                                  ALU.mult, ALU.add)
                last.then_inc(scan_done.sem, 1)
                dve.wait_ge(scan_done.sem, scan_done.at(b, k + 1))
                if c + 1 < NC:
                    dve.tensor_copy(carry[:, :, n:n + 1], u[:, s, :, N - 1:N]).then_inc(carried.sem, 1)
                    dve.wait_ge(carried.sem, carried.at(b, n + 1))
                dve.wait_ge(c_mm.sem, c_mm.at(b, k + 1))
                dve.tensor_tensor(u[:, s], u[:, s], both(psb[:, 1]), ALU.mult).then_inc(cy_done.sem, 1)

            def states_add(b, c):
                dve.wait_ge(y_acc.sem, y_acc.at(b, (c + 1) * NS // 2))
                dve.tensor_tensor(chunk(so, c), chunk(so, c), psy[:], ALU.add).then_inc(ssm_done.sem, 1)

            def lf_center(b, c):
                dve.wait_ge(lf_mean.sem, lf_mean.at(b, c + 1))
                dve.tensor_tensor(nrm[:, c], chunk(so, c), both(psb[:, 0]), ALU.subtract)\
                    .then_inc(lf_cen.sem, 1)

            def lf_scale(b, c):
                dve.wait_ge(lf_rstd.sem, lf_rstd.at(b, c + 1))
                dve.tensor_tensor(nrm[:, c], nrm[:, c], both(rs3[:]), ALU.mult).then_inc(lf_step.sem, 1)
                dve.wait_ge(lf_step.sem, lf_step.at(b, 2 * c + 1))
                for t in range(KD):
                    last = dve.tensor_scalar(nrm[:, c, t], nrm[:, c, t], col("ln2_g", t), col("ln2_b", t),
                                             ALU.mult, ALU.add)
                last.then_inc(lf_step.sem, 1)

            def block_out(b, c):
                dve.wait_ge(f2_mm.sem, f2_mm.at(b, (c + 1) * KF))
                for t in range(KD):
                    part = so[:, t, c * N:(c + 1) * N]
                    last = dve.scalar_tensor_tensor(part, psb[:, t], col("b2", t), part, ALU.add, ALU.add)
                last.then_inc(block_done.sem, 1)

            def expert_norm(b, c):
                dve.wait_ge(m_rms.sem, m_rms.at(b, c + 1))
                dve.wait_ge(nf_done.sem, nf_done.at(b, c))
                dve.tensor_tensor(xrms[:], chunk(xb, c), both(rsm[:]), ALU.mult).then_inc(m_step.sem, 1)
                dve.wait_ge(m_step.sem, m_step.at(b, c + 1))
                for t in range(KD):
                    last = dve.tensor_scalar(nf[:, c, t], xrms[:, t], col("norm_w", t), None, ALU.mult)
                last.then_inc(nf_done.sem, 1)

            def expert_gate(b):
                at = 0

                def step(ins):
                    nonlocal at
                    at += 1
                    ins.then_inc(gate_step.sem, 1)
                    dve.wait_ge(gate_step.sem, gate_step.at(b, at))

                dve.wait_ge(gate_mm.sem, gate_mm.at(b, 1))
                step(dve.tensor_copy(lg16[:], psg[:, 1, 0:NJ * E].rearrange("p (j e) -> p j e", e=E)))
                step(dve.tensor_copy(lg[:], lg16[:]))
                for largest, chosen in ((gm1, first), (gm2, second)):
                    step(dve.tensor_reduce(largest[:], lg[:], AX_X, ALU.max))
                    step(dve.tensor_tensor(gtmp[:], lg[:], last8(largest[:]), ALU.is_equal))
                    step(dve.tensor_tensor(gtmp[:], gtmp[:], rank[:], ALU.mult))
                    step(dve.tensor_reduce(gix[:], gtmp[:], AX_X, ALU.max))
                    step(dve.tensor_tensor(chosen[:], gtmp[:], last8(gix[:]), ALU.is_equal))
                    if chosen is first:
                        step(dve.scalar_tensor_tensor(lg[:], first[:], -3e38, lg[:], ALU.mult, ALU.add))
                dve.tensor_tensor(gex[:], gm2[:], gm1[:], ALU.subtract).then_inc(gate_d.sem, 1)
                dve.wait_ge(gate_e.sem, gate_e.at(b, 1))
                step(dve.tensor_scalar(gw1[:], gex[:], 1.0, None, ALU.add))
                step(dve.reciprocal(gw1[:], gw1[:]))
                step(dve.tensor_scalar(gw1[:], gw1[:], A_UP, None, ALU.mult))
                step(dve.tensor_tensor(gw2[:], gex[:], gw1[:], ALU.mult))
                step(dve.tensor_tensor(first[:], first[:], last8(gw1[:]), ALU.mult))
                step(dve.tensor_tensor(second[:], second[:], last8(gw2[:]), ALU.mult))
                step(dve.tensor_tensor(comb[:, :, 0:E], first[:], second[:], ALU.add))
                assert at == GATE_STEPS
                dve.tensor_copy(comb[:, :, 32:32 + E], comb[:, :, 0:E]).then_inc(comb_done.sem, 1)

            def expert_parts(b, c):
                dve.wait_ge(comb_t.sem, comb_t.at(b, c + 1))
                dve.wait_ge(cs_done.sem, cs_done.at(b, c))
                dve.tensor_copy(ct[:], psg[0:64, 1]).then_inc(ct_done.sem, 1)
                dve.wait_ge(ct_done.sem, ct_done.at(b, 2 * c + 1))
                dve.tensor_copy(cs[:, c], ct[:]).then_inc(ct_done.sem, 1)
                dve.wait_ge(ct_done.sem, ct_done.at(b, 2 * c + 2))
                dve.tensor_tensor(cs[32:64, c], ct[32:64], cs[32:64, c].bitcast(F32), ALU.subtract)\
                    .then_inc(cs_done.sem, 1)

            def expert_clip(b, r):
                e, t = divmod(r % NQ, KD)
                bank = psy if r % 2 == 0 else psg
                dve.wait_ge(p1_mm.sem, p1_mm.at(b, r + 1))
                if r >= NB:
                    dve.wait_ge(af_done.sem, af_done.at(b, r - NB + 1))
                dve.tensor_scalar(gate[:, r % NB], bank[:, 0], mbias[:, e, 0, t:t + 1], LIMIT,
                                  ALU.add, ALU.min).then_inc(gmin_done.sem, 1)
                dve.tensor_scalar(lin[:, r % NB], bank[:, 1], lin_lo[:, e, t:t + 1], lin_hi[:, e, t:t + 1],
                                  ALU.max, ALU.min).then_inc(lin_done.sem, 1)

            def expert_product(b, r, ahead):
                e, t = divmod(r % NQ, KD)
                dve.wait_ge(sc_done.sem, sc_done.at(b, r + 1))
                dve.wait_ge(lin_done.sem, lin_done.at(b, r + 1))
                if r >= NB:
                    dve.wait_ge(alo_done.sem, alo_done.at(b, r - NB + 1))
                elif r == 0:
                    dve.wait_ge(gy.sem, gy.at(ahead, NC))
                dve.scalar_tensor_tensor(af[:, r % NB], lin[:, r % NB], lin_one[:, e, t:t + 1],
                                         gate[:, r % NB], ALU.add, ALU.mult).then_inc(af_done.sem, 1)

            def expert_sum(b, c):
                dve.wait_ge(p2_mm.sem, p2_mm.at(b, (c + 1) * NQ))
                dve.wait_ge(moe_g.sem, moe_g.at(b, c))
                dve.tensor_scalar(sum16[:], psb[:], 1.0 / A_UP, None, ALU.mult).then_inc(moe_r.sem, 1)
                dve.wait_ge(moe_r.sem, moe_r.at(b, c + 1))
                dve.tensor_tensor(sum16[:], chunk(xb, c), sum16[:], ALU.add).then_inc(moe_s.sem, 1)

            def batch(b0, b1):
                for c in range(NC):
                    if b0 is not None:
                        l0_center(b0, c)
                    if b1 is not None:
                        head_center(b1, c)
                    if b0 is not None:
                        l0_scale(b0, c)
                    if b1 is not None:
                        head_norm(b1, c)
                        head_rest(b1, c)
                    for n in range(NS):
                        if b1 is not None:
                            state(b1, c, n)
                        if b0 is not None:
                            for task in tasks(n):
                                ffn_task(b0, c, task)
                    if b1 is not None:
                        states_add(b1, c)
                if b1 is not None:
                    for c in range(NC):
                        lf_center(b1, c)
                        lf_scale(b1, c)
                if b0 is not None:
                    wavelets_and_attention(b0, b1)
                else:
                    expert_norm(b1, 0)
                    expert_norm(b1, 1)
                    expert_gate(b1)
                    block_out(b1, 0)
                    expert_parts(b1, 0)
                    expert_parts(b1, 1)
                if b1 is not None:
                    block_out(b1, 1)
                if b0 is not None:
                    for c in range(NC):
                        lb_center(b0, c)
                        lb_scale(b0, c)
                if b1 is not None:
                    ahead = 0 if b0 is not None else b1
                    for r in range(Q + LAG):
                        if r == NQ + LAG_DOWN:
                            expert_sum(b1, 0)
                        if r < Q:
                            expert_clip(b1, r)
                        if r >= LAG:
                            expert_product(b1, r - LAG, ahead)
                    expert_sum(b1, 1)

            batch(0, None)
            next_turn(dve, "dve")
            with dve.Fori(0, B - 1):
                batch(0, -1)
                next_turn(dve, "dve")
            batch(None, -1)


_NAMES = ("x", "pack", "w1", "w2", "h1", "h2", "w3", "wd", "wbc", "wf1", "wf2", "mlp1_w", "mlp1_b", "mlp2_w",
          "mlp2_b", "gate_w", "gate_b")


def kernel(**inputs):
    import numpy as _np
    import concourse.bacc as _bacc
    from concourse import mybir as _mybir
    from concourse.bass_utils import run_bass_kernel_spmd as _run

    g = {k: _np.asarray(v) for k, v in inputs.items()}

    def columns(v):
        v = v.reshape(v.shape[0] // P, P, -1)
        return v.transpose(1, 0, 2).reshape(P, -1)

    def stationary(w):
        return w.T.reshape(-1, P, w.shape[0]).transpose(1, 0, 2)

    vectors = {
        "h_filter": g["L0_attn_h_filter"].T, "g_filter": g["L0_attn_g_filter"].T,
        "h_synth": g["L0_attn_h_synth"].T, "g_synth": g["L0_attn_g_synth"].T,
        "gamma": g["L0_attn_norm_gamma"], "beta": g["L0_attn_norm_beta"],
        "w1_s": g["L0_ffn_w1_s"], "w2_s": g["L0_ffn_w2_s"], "h1_s": g["L0_ffn_h1_s"],
        "h2_s": g["L0_ffn_h2_s"], "w3_s": g["L0_ffn_w3_s"], "ln1_g": g["L1_attn_ln1_g"],
        "ln1_b": g["L1_attn_ln1_b"], "bd": g["L1_attn_bd"], "A_log": g["L1_attn_A_log"],
        "D": g["L1_attn_D"], "ln2_g": g["L1_attn_ln2_g"], "ln2_b": g["L1_attn_ln2_b"],
        "b1": g["L1_attn_b1"], "b2": g["L1_attn_b2"], "norm_w": g["L1_ffn_norm_weight"],
        "bbc": _np.concatenate([g["L1_attn_bbc"]] * (P // 32)),
    }
    wbc = g["L1_attn_Wbc"]
    mlp1 = g["L1_ffn_mlp1_weight"].reshape(E, D, 2, KD, P)
    mlp2 = g["L1_ffn_mlp2_weight"].reshape(E, D, KD, P)
    arrays = {
        "x": g["L0_attn_x"].reshape(B, L, KD, P).transpose(0, 3, 2, 1),
        "pack": _np.concatenate([columns(vectors[k]) for k in PACK], axis=1),
        "w1": stationary(g["L0_ffn_w1_w"]), "w2": stationary(g["L0_ffn_w2_w"]),
        "h1": stationary(g["L0_ffn_h1_w"]), "h2": stationary(g["L0_ffn_h2_w"]),
        "w3": stationary(g["L0_ffn_w3_w"]), "wd": stationary(g["L1_attn_Wd"]),
        "wbc": stationary(_np.concatenate([wbc, wbc])),
        "wf1": stationary(g["L1_attn_W1"]), "wf2": stationary(g["L1_attn_W2"]),
        "mlp1_w": mlp1.transpose(4, 0, 3, 2, 1),
        "mlp1_b": g["L1_ffn_mlp1_bias"].reshape(E, KD, P, 2).transpose(2, 0, 3, 1),
        "mlp2_w": mlp2.transpose(3, 0, 2, 1),
        "mlp2_b": g["L1_ffn_mlp2_bias"],
        "gate_w": g["L1_ffn_gate_weight"].reshape(E, KD, P).transpose(2, 1, 0),
        "gate_b": g["L1_ffn_gate_bias"].reshape(1, E),
    }
    nc = _bacc.Bacc("TRN2", target_bir_lowering=False, num_devices=1)
    aps, feed = {}, {}
    for name in _NAMES:
        v = _np.ascontiguousarray(arrays[name])
        feed[f"in_{name}"] = v
        aps[name] = nc.dram_tensor(f"in_{name}", v.shape, _mybir.dt.from_np(v.dtype), kind="ExternalInput").ap()
    aps["out"] = nc.dram_tensor("out_0", (B, P, KD, L), F32, kind="ExternalOutput").ap()
    build(nc, aps)
    r = _run(nc, [feed], core_ids=[0])
    out = r.results[0]["out_0"]
    return out.transpose(0, 3, 2, 1).reshape(B, L, D)
```

```python
from contextlib import ExitStack

import concourse.bass as bass
from concourse import mybir

F32 = mybir.dt.float32
F32R = mybir.dt.float32r
F16 = mybir.dt.float16
BF16 = mybir.dt.bfloat16
ALU = mybir.AluOpType
ACT = mybir.ActivationFunctionType
AX_X = mybir.AxisListType.X

P = 128
B, L, D = 4, 1024, 256
KD = D // P
F = 1024
KF = F // P
N = 512
NC = L // N
NS = 16
E = 8
HEAD = 16
LN_EPS = 1e-5
ATTN_EPS = 1e-6
LIMIT = 7.0
ALPHA = 1.702
H_UP = 128.0
G_UP = 4.0
A_UP = 1024.0

PACK = {}
_at = 0
for _name, _width in (
    ("h_filter", 8), ("g_filter", 8), ("h_synth", 8), ("g_synth", 8), ("gamma", 2), ("beta", 2),
    ("w1_s", 8), ("w2_s", 8), ("h1_s", 8), ("h2_s", 8), ("w3_s", 2), ("ln1_g", 2), ("ln1_b", 2),
    ("bd", 2), ("A_log", 32), ("D", 2), ("ln2_g", 2), ("ln2_b", 2), ("b1", 8), ("b2", 2),
    ("norm_w", 2), ("bbc", 1),
):
    PACK[_name] = (_at, _at + _width)
    _at += _width
PACKED = _at


POOL_CONST = 14
DVE_CONST = 24
LB_STEPS = 3
LE_STEPS = 9
HEAD_STEPS = 4
LE_PARTS = HEAD_STEPS + 1
GATE_STEPS = 20
NJ = L // P
NQ = E * KD
NB = 3
LAG = 2
LAG_DOWN = 5
OUT_LAG = 6
LATE_AT = NQ + OUT_LAG + 3
GATE0_AT = 0
NEXT_AT, NEXT_CENTER_AT, NEXT_SQ_AT, NEXT_VAR_AT, NEXT_STD_AT, NEXT_SCALE_AT, NEXT_SPLIT_AT, NEXT_LOW_AT = \
    25, 26, 27, 28, 29, 30, 31, 32
LI_AT, LI_SQ_AT, LI_VAR_AT, LI_SCALE_AT, LI_SPLIT_AT, LI_LOW_AT = 4, 5, 6, 7, 8, 9
LF_VAR_AT, RMS_AT, RMS1_AT, LOGITS_AT, ATTN_AT, NUM_AT, TURN_AT, TURN1_AT = 2, 3, 4, 6, 7, 8, 9, 11


class Signal:

    def __init__(self, sem, layer, per, unit=1):
        self.sem, self.layer, self.per, self.unit = sem, layer, per, unit

    @property
    def batch(self):
        return self.per * self.unit

    @property
    def start(self):
        return (1 + self.layer) * self.batch

    def at(self, b, k):
        return (b + 1 + self.layer) * self.batch + k * self.unit


def build(nc, a):
    ctx = ExitStack()
    with ctx:
        def sb(name, shape, dt):
            return ctx.enter_context(nc.sbuf_tensor(name, shape, dt))

        w1 = sb("w1", [P, KD, F], F16)
        w2 = sb("w2", [P, KD, F], F16)
        h1w = sb("h1w", [P, KF, F], F16)
        h2w = sb("h2w", [P, KF, F], F16)
        w3 = sb("w3", [P, KF, D], F32R)
        wd = sb("wd", [P, KD, D], F32)
        wbc = sb("wbc", [P, KD, 64], F32)
        wf2 = sb("wf2", [P, KF, D], F32)
        xn = sb("xn", [P, KD, L + 2], F32)
        xp = sb("xp", [P, 2, KD, N], F16)
        gx = sb("gx", [P, KD, L], F32)
        x2 = sb("x2", [P, KD, L], F32)
        xb = sb("xb", [P, KD, L], BF16)
        so = sb("so", [P, KD, L], F32)
        pk = sb("pk", [P, PACKED], F32)
        ident = sb("ident", [P, P], F32)
        meanw = sb("meanw", [P, P], F32)
        headmask = sb("headmask", [P, P], F32)
        sel = sb("sel", [64, 32], F32R)
        synth = sb("synth", [P, 2, KD, 5], F32)
        aneg = sb("aneg", [P, KD, NS], F32)
        s_h = sb("s_h", [P, KF], F32)
        s_g1 = sb("s_g1", [P, KF], F32)
        s_g2 = sb("s_g2", [P, KF], F32)
        mbias16 = sb("mbias16", [P, E, 2, KD], BF16)
        mbias = sb("mbias", [P, E, 2, KD], F32)
        lin_lo = sb("lin_lo", [P, E, KD], F32)
        lin_hi = sb("lin_hi", [P, E, KD], F32)
        lin_one = sb("lin_one", [P, E, KD], F32)
        b2s = sb("b2s", [64, D], F32R)
        wgate = sb("wgate", [P, KD, E], BF16)
        gbias = sb("gbias", [1, E], BF16)
        ones16 = sb("ones16", [1, P], BF16)
        rank = sb("rank", [P, NJ, E], F32)
        eps = sb("eps", [P, 1], F32)
        carry = sb("carry", [P, KD, NS], F32)
        lg16 = sb("lg16", [P, NJ, E], BF16)
        lg = sb("lg", [P, NJ, E], F32)
        first = sb("first", [P, NJ, E], F32)
        second = sb("second", [P, NJ, E], F32)
        gtmp = sb("gtmp", [P, NJ, E], F32)
        gm1 = sb("gm1", [P, NJ], F32)
        gm2 = sb("gm2", [P, NJ], F32)
        gix = sb("gix", [P, NJ], F32)
        gex = sb("gex", [P, NJ], F32)
        gw1 = sb("gw1", [P, NJ], F32)
        gw2 = sb("gw2", [P, NJ], F32)
        comb = sb("comb", [P, NJ, 64], F32)

        R1, R2 = 51200, 51200

        def region(name, size):
            base = -(-nc.sbuf_base // 32) * 32
            sb(name, [P, size // 4], F32)

            def place(name, at, shape, dt):
                return nc.alloc_sbuf_tensor_at(name, shape, dt, offset=base + at)
            return place

        r1, r2 = region("region1", R1), region("region2", R2)
        hp = r1("hp", 0, [P, 2, KF, N], F16)
        g1p = r1("g1p", 16384, [P, 2, KF, N], F16)
        g2p = r1("g2p", 32768, [P, 2, 2, N], F32R)
        sa = r1("sa", 40960, [P, 2, N], F32)
        tf = r1("tf", 45056, [P, 2, N], F32)
        sq0_1 = r1("sq0_1", 40960, [P, KD, N], F32)
        rs0 = r1("rs0", 49152, [P, N], F32)
        l1b = r1("l1b", 0, [P, KD, N + 2], F32)
        h1b = r1("h1b", 4352, [P, KD, N + 2], F32)
        l2 = r1("l2", 8704, [P, KD, N // 2], F32)
        h2b = r1("h2b", 10752, [P, KD, N // 2 + 2], F32)
        q0 = r1("q0", 12928, [P, KD, N // 2], F32)
        qe = r1("qe", 14976, [P, KD, N // 2], F32)
        low2 = r1("low2", 17024, [P, KD, N // 2 + 2], F32)
        low1 = r1("low1", 19200, [P, KD, N + 2], F32)
        qt = r1("qt", 23424, [P, 2, D], F32)
        vt = r1("vt", 25472, [P, 2, D], F32)
        kvm = r1("kvm", 27520, [P, KD, P], F32)
        zm = r1("zm", 28544, [P, KD, P], F32)
        rden = r1("rden", 29568, [P, KD, N // 2], F32)
        zs = r1("zs", 31616, [P, KD], F32)
        y0 = r1("y0", 43008, [P, KD, L], F32)
        sqb = r1("sqb", 33792, [P, KD, N], F32)
        rsb = r1("rsb", 18432, [P, N], F32)
        xr = r1("xr", 38912, [P, KD, N], F32)
        gate = r1("gate", 0, [P, NB, N], F32)
        lin = r1("lin", 6144, [P, NB, N], F32)
        sum16 = r1("sum16", 20480, [P, KD, N], BF16)
        gate1 = r1("gate1", 33792, [P, KD, N], F32)
        cs = r1("cs", 23424, [64, NC, N], F32R)
        af = r1("af", 12288, [P, NB, N], F32)
        ap2 = r1("ap2", 27520, [P, NB, 2, N], F16)
        outc = r1("outc", 38912, [P, KD, N], F32)
        xn1_0 = r1("xn1_0", 43008, [P, KD, N], F32)
        sqm = r1("sqm", 40960, [P, KD, N], F32)
        rsm = r1("rsm", 45056, [P, N], F32)
        xrms = r1("xrms", 47104, [P, KD, N], F32)
        ct = r1("ct", 45056, [64, N], F32)
        sq2 = r1("sq2", 40960, [P, KD, N], F32)
        rs3 = r1("rs3", 49152, [P, N], F32)
        xc_0 = r2("xc_0", 10240, [P, KD, N], F32)
        zt = r2("zt", 43008, [P, KD, N], F32)
        sq1 = r2("sq1", 43008, [P, KD, N], F32)
        sq0_0 = r2("sq0_0", 43008, [P, KD, N], F32)
        v1 = r2("v1", 47104, [P, N], F32)
        bcf = r2("bcf", 47104, [64, N], F32)
        delta = [r2("delta_0", 6144, [P, KD, N], F32), r2("delta_1", 0, [P, KD, N], F32)]
        bcs = [r2("bcs_0", 49152, [64, N], F32R), r2("bcs_1", 4096, [64, N], F32R)]
        da = r2("da", 10240, [P, 4, KD, N], F32)
        u = r2("u", 26624, [P, 4, KD, N], F32)
        nrm = [r2("nrm_0", 6144, [P, KD, N], F32), r2("nrm_1", 0, [P, KD, N], F32)]
        hff = r2("hff", 10240, [P, 2, N], F32)
        cb = r2("cb", 0, [P, 2, N], F32)
        wf1 = r2("wf1", 43008, [P, KD, F], F32)
        nf = r2("nf", 14336, [P, NC, KD, N], BF16)
        mw1 = r2("mw1", 18432, [P, E, KD, 2, D], BF16)
        mw2 = r2("mw2", 34816, [P, E, KD, D], BF16)

        def ps(name):
            return ctx.enter_context(nc.psum_tensor(name, [P, 2, N], F32))

        psy, psb, psf, psg = ps("psy"), ps("psb"), ps("psf"), ps("psg")

        def col(name, k=0, w=1):
            lo, hi = PACK[name]
            return pk[:, lo + k:lo + k + w]

        def chunk(t, c):
            return t[:, :, c * N:(c + 1) * N]

        sq0 = [sq0_0, sq0_1]
        xc = [xc_0[:], chunk(gx, 1)]
        xn1 = [xn1_0[:], chunk(so, 1)]
        hb = [psf[:, 1], psy[:, 1]]
        lin_bank = [(psf[:, 1], psf[:, 1]), (psy[:, 0], psy[:, 0])]

        lf_bank = [psy[:, 0], psf[:, 0]]

        def both(t):
            return t.rearrange("p (o n) -> p o n", o=1).broadcast_to([P, KD, t.shape[-1]])

        def last8(t):
            return t.rearrange("p (j o) -> p j o", o=1).broadcast_to([P, NJ, E])

        signals_early, signals_late = [], []
        signals = signals_late
        layer = 0

        def sig(name, per, unit=1):
            s = Signal(ctx.enter_context(nc.semaphore(name)), layer, per, unit)
            signals.append(s)
            return s

        def one(name):
            return ctx.enter_context(nc.semaphore(name))

        packs_in = one("packs_in")
        w12_in = one("w12_in")
        h1_in = one("h1_in")
        h2_in = one("h2_in")
        w3_in = one("w3_in")
        wl1_in = one("wl1_in")
        b2_in = one("b2_in")
        pool_const = one("pool_const")
        dve_const = one("dve_const")
        act_const = one("act_const")
        b2s_zero = one("b2s_zero")
        x_in = [sig(f"x_in{c}", 1, 16) for c in range(NC)]
        li_mean = sig("li_mean", NC)
        li_cen = sig("li_cen", NC)
        li_sq = sig("li_sq", NC)
        li_var = sig("li_var", NC)
        li_ln = sig("li_ln", NC)
        li_rstd = sig("li_rstd", NC)
        li_xn = sig("li_xn", NC)
        li_hi = sig("li_hi", NC)
        li_lo = sig("li_lo", NC)
        signals = signals_early
        ab_mm = sig("ab_mm", NC * KF)
        silu_a = sig("silu_a", NC * KF)
        h_f = sig("h_f", NC * KF)
        h_hi = sig("h_hi", NC * KF)
        h_lo = sig("h_lo", NC * KF)
        g1_mm = sig("g1_mm", NC * KF)
        g1_f = sig("g1_f", NC * KF)
        g1_hi = sig("g1_hi", NC * KF)
        g1_lo = sig("g1_lo", NC * KF)
        g2_mm = sig("g2_mm", NC * KF)
        g2_f = sig("g2_f", NC * KF)
        g2_hi = sig("g2_hi", NC * KF)
        g2_lo = sig("g2_lo", NC * KF)
        w3_mm = sig("w3_mm", NC * KF)
        signals = signals_late
        gate0 = sig("gate0", NC)
        conv = sig("conv", 88)
        q_min = sig("q_min", 1)
        q_exp = sig("q_exp", 1)
        q_done = sig("q_done", 1)
        turned = sig("turned", 1)
        qt_done = sig("qt_done", 1)
        vt_done = sig("vt_done", 1)
        kv_mm = sig("kv_mm", 1)
        kv_masked = sig("kv_masked", 1)
        num_mm = sig("num_mm", 1)
        y_done = sig("y_done", 1)
        lb_mean = sig("lb_mean", NC)
        lb_cen = sig("lb_cen", NC)
        lb_sq = sig("lb_sq", NC)
        lb_var = sig("lb_var", NC)
        lb_ln = sig("lb_ln", NC)
        lb_rstd = sig("lb_rstd", NC)
        lb_step = sig("lb_step", LB_STEPS * NC)
        xr_in = sig("xr_in", NC, 16)
        gy = sig("gy", NC)
        x2n = sig("x2n", NC)
        layer = 1
        le_copy = sig("le_copy", NC)
        le_mean = sig("le_mean", NC)
        le_cen = sig("le_cen", NC)
        le_sq = sig("le_sq", NC)
        le_var = sig("le_var", NC)
        le_ln = sig("le_ln", 2 * NC)
        le_rstd = sig("le_rstd", NC)
        le_step = sig("le_step", LE_STEPS * NC)
        le_rstd1 = sig("le_rstd1", NC)
        le_xb = sig("le_xb", NC)
        dt_mm = sig("dt_mm", NC * KD)
        bc_mm = sig("bc_mm", NC)
        z_done = sig("z_done", NC * KD)
        z_abs = sig("z_abs", NC)
        z_exp = sig("z_exp", NC)
        z_ln = sig("z_ln", NC)
        head_done = sig("head_done", NC)
        signals = signals_early
        b_mm = sig("b_mm", NC * NS)
        c_mm = sig("c_mm", NC * NS)
        da_done = sig("da_done", NC * NS)
        u_done = sig("u_done", NC * NS)
        scan_done = sig("scan_done", NC * NS)
        carried = sig("carried", NS)
        cy_done = sig("cy_done", NC * NS)
        y_acc = sig("y_acc", NC * NS)
        lf_mean = sig("lf_mean", NC)
        lf_cen = sig("lf_cen", NC)
        lf_sq = sig("lf_sq", NC)
        lf_var = sig("lf_var", NC)
        lf_ln = sig("lf_ln", NC)
        lf_rstd = sig("lf_rstd", NC)
        lf_step = sig("lf_step", 2 * NC)
        signals = signals_late
        wf1_in = sig("wf1_in", 1, 16)
        f1_mm = sig("f1_mm", NC * KF)
        f1_done = sig("f1_done", NC * KF)
        f2_mm = sig("f2_mm", NC * KF)
        block_done = sig("block_done", NC)
        mw_in = sig("mw_in", 2, 16)
        m_sq = sig("m_sq", NC)
        m_ms = sig("m_ms", NC)
        m_rms = sig("m_rms", NC)
        m_ln = sig("m_ln", NC)
        m_step = sig("m_step", NC)
        nf_done = sig("nf_done", NC)
        gate_mm = sig("gate_mm", 1)
        gate_step = sig("gate_step", GATE_STEPS)
        gate_d = sig("gate_d", 1)
        gate_e = sig("gate_e", 1)
        comb_done = sig("comb_done", 1)
        comb_t = sig("comb_t", NC)
        ct_done = sig("ct_done", 2 * NC)
        cs_done = sig("cs_done", NC)
        cb_mm = sig("cb_mm", NC * E)
        cb_done = sig("cb_done", NC * E)
        Q = NC * NQ
        p1_mm = sig("p1_mm", Q)
        gmin_done = sig("gmin_done", Q)
        lin_done = sig("lin_done", Q)
        sg_done = sig("sg_done", Q)
        sc_done = sig("sc_done", Q)
        af_done = sig("af_done", Q)
        ahi_done = sig("ahi_done", Q)
        alo_done = sig("alo_done", Q)
        p2_mm = sig("p2_mm", Q)
        moe_r = sig("moe_r", NC)
        moe_s = sig("moe_s", NC)
        moe_g = sig("moe_g", NC)
        out_m = sig("out_m", NC)
        out_ready = sig("out_ready", NC)
        out_sent = sig("out_sent", NC, 16)

        arrived = one("arrived")
        released = {e: one(f"released_{e}") for e in ("pool", "act", "pe", "dve")}

        def next_turn(engine, name):
            engine.sem_inc(arrived, 1)
            engine.wait_ge(released[name], 1)
            engine.sem_inc(released[name], -1)

        block = ctx.enter_context(nc.Block())

        def xn_chunk(c):
            return xn[:, :, 1 + c * N:1 + (c + 1) * N]

        ends = [0]
        for products in (4 * KD, 2 * KF, 2 * KF + 2 * KD):
            for _ in range(KF):
                ends.append(ends[-1] + products)

        def tasks(step):
            lo, hi = (ends[-1] * s / NS for s in (step, step + 1))
            return [task for task in range(3 * KF) if lo <= ends[task] < hi]

        @block.sync
        def _(sp):
            for s in signals_early + signals_late:
                sp.sem_inc(s.sem, s.start)

            def load_x(b, row):
                for c in range(NC):
                    sp.wait_ge(y_done.sem, y_done.at(b - 1, 1))
                    sp.dma_start(xn_chunk(c), a["x"][row][:, :, c * N:(c + 1) * N]).then_inc(x_in[c].sem, 16)

            def load_hidden(b):
                sp.wait_ge(head_done.sem, head_done.at(b, NC))
                sp.wait_ge(c_mm.sem, c_mm.at(b, NS))
                sp.dma_start(wf1[:], a["wf1"]).then_inc(wf1_in.sem, 16)

            def load_experts(b):
                sp.wait_ge(y_acc.sem, y_acc.at(b, NC * NS))
                sp.dma_start(mw1[:], a["mlp1_w"]).then_inc(mw_in.sem, 16)
                sp.dma_start(mw2[:], a["mlp2_w"]).then_inc(mw_in.sem, 16)

            def load_residual(b, row):
                for c in range(NC):
                    sp.wait_ge(gate0.sem, gate0.at(b, NC))
                    sp.wait_ge(nf_done.sem, nf_done.at(b - 1, NC))
                    sp.wait_ge(x2n.sem, x2n.at(b, c))
                    sp.dma_start(xr[:], a["x"][row][:, :, c * N:(c + 1) * N]).then_inc(xr_in.sem, 16)

            def store_out(b, row):
                for c in range(NC):
                    sp.wait_ge(out_ready.sem, out_ready.at(b, c + 1))
                    sp.dma_start(a["out"][row][:, :, c * N:(c + 1) * N], outc[:]).then_inc(out_sent.sem, 16)

            sp.dma_start(pk[:], a["pack"]).then_inc(packs_in, 16)
            sp.dma_start(mbias16[:], a["mlp1_b"]).then_inc(packs_in, 16)
            sp.dma_start(wgate[:], a["gate_w"]).then_inc(packs_in, 16)
            sp.dma_start(gbias[:], a["gate_b"]).then_inc(packs_in, 16)
            load_x(0, 0)
            sp.wait_ge(h2_in, 16)
            sp.dma_start(wf2[:], a["wf2"]).then_inc(wl1_in, 16)
            sp.dma_start(wd[:], a["wd"]).then_inc(wl1_in, 16)
            sp.dma_start(wbc[:], a["wbc"]).then_inc(wl1_in, 16)

            def turn(row, last=False):
                load_hidden(-1)
                load_experts(-1)
                load_residual(0, row)
                if not last:
                    load_x(1, row + 1)
                sp.wait_ge(p1_mm.sem, p1_mm.at(-1, 1))
                sp.wait_ge(sg_done.sem, sg_done.at(-1, 1))
                sp.wait_ge(gmin_done.sem, gmin_done.at(-1, 1))
                sp.wait_ge(sc_done.sem, sc_done.at(-1, 1))
                for s in signals_early:
                    sp.sem_inc(s.sem, -s.batch)
                store_out(-1, row - 1)

            def take_down(group):
                sp.wait_ge(arrived, len(released))
                sp.sem_inc(arrived, -len(released))
                for s in group:
                    sp.sem_inc(s.sem, -s.batch)
                for s in released.values():
                    sp.sem_inc(s, 1)

            load_residual(0, 0)
            load_x(1, 1)
            take_down(signals_early + signals_late)
            with sp.Fori(0, B - 2) as i:
                turn(i + 1)
                take_down(signals_late)
            turn(B - 1, last=True)
            take_down(signals_late)
            load_hidden(-1)
            load_experts(-1)
            store_out(-1, B - 1)
            sp.wait_ge(out_sent.sem, out_sent.at(-1, NC))

        @block.gpsimd
        def _(pool):
            pool.dma_start(w1[:], a["w1"]).then_inc(w12_in, 16)
            pool.dma_start(w2[:], a["w2"]).then_inc(w12_in, 16)
            k = 0

            def const(ins):
                nonlocal k
                k += 1
                ins.then_inc(pool_const, 1)
                pool.wait_ge(pool_const, k)

            const(pool.memset(ident[:], 0.0))
            const(pool.affine_select(out=ident[:], in_=ident[:], compare_op=ALU.not_equal, fill=1.0,
                                     base=0, pattern=[[-1, P]], channel_multiplier=1))
            const(pool.memset(headmask[:], 1.0))
            hm = headmask[:].rearrange("p (h d) -> p h d", d=HEAD)
            const(pool.affine_select(out=hm, in_=hm, compare_op=ALU.is_ge, fill=0.0, base=0,
                                     pattern=[[-HEAD, P // HEAD], [0, HEAD]], channel_multiplier=1))
            const(pool.affine_select(out=hm, in_=hm, compare_op=ALU.is_ge, fill=0.0, base=HEAD - 1,
                                     pattern=[[HEAD, P // HEAD], [0, HEAD]], channel_multiplier=-1))
            for e in range(E):
                const(pool.memset(rank[:, :, e:e + 1], float(E - e)))
            const(pool.memset(comb[:], 0.0))
            assert k == POOL_CONST

            pool.wait_ge(x_in[0].sem, x_in[0].at(0, 1))
            pool.dma_start(h1w[:], a["h1"]).then_inc(h1_in, 16)
            pool.dma_start(w3[:], a["w3"]).then_inc(w3_in, 16)
            pool.dma_start(h2w[:], a["h2"]).then_inc(h2_in, 16)
            pool.wait_ge(b2s_zero, 1)
            pool.dma_start(b2s[0:E, :], a["mlp2_b"]).then_inc(b2_in, 16)
            pool.dma_start(b2s[32:32 + E, :], a["mlp2_b"]).then_inc(b2_in, 16)

            def l0_low(b, c):
                pool.wait_ge(li_hi.sem, li_hi.at(b, c + 1))
                pool.tensor_tensor(xp[:, 1], xn_chunk(c), xp[:, 0], ALU.subtract).then_inc(li_lo.sem, 1)

            def ffn_task(b, c, task):
                kind, m = divmod(task, KF)
                k = c * KF + m
                if kind == 0:
                    pool.wait_ge(h_hi.sem, h_hi.at(b, k + 1))
                    pool.tensor_tensor(hp[:, 1, m], tf[:, m % 2], hp[:, 0, m], ALU.subtract)\
                        .then_inc(h_lo.sem, 1)
                elif kind == 2:
                    pool.wait_ge(g2_hi.sem, g2_hi.at(b, k + 1))
                    pool.tensor_tensor(g2p[:, m % 2, 1], tf[:, m % 2], g2p[:, m % 2, 0].bitcast(F32),
                                       ALU.subtract).then_inc(g2_lo.sem, 1)

            def state_add(b, c, n):
                k = c * NS + n
                pool.wait_ge(cy_done.sem, cy_done.at(b, k + 1))
                pool.wait_ge(y_acc.sem, y_acc.at(b, k))
                out = chunk(gx, c) if n < NS - 1 else chunk(so, c)
                pool.tensor_tensor(out, chunk(gx, c), u[:, n % 4], ALU.add).then_inc(y_acc.sem, 1)

            def l0_out(b, c):
                pool.wait_ge(lb_step.sem, lb_step.at(b, LB_STEPS * (c + 1)))
                pool.tensor_tensor(chunk(gx, c), chunk(y0, c), chunk(gx, c), ALU.mult).then_inc(gy.sem, 1)
                pool.wait_ge(gy.sem, gy.at(b, c + 1))
                pool.wait_ge(xr_in.sem, xr_in.at(b, c + 1))
                pool.tensor_tensor(chunk(gx, c), chunk(gx, c), xr[:], ALU.add).then_inc(x2n.sem, 1)

            def expert_weighted(b, r):
                pool.wait_ge(sg_done.sem, sg_done.at(b, r + 1))
                pool.wait_ge(cb_done.sem, cb_done.at(b, r // KD + 1))
                pool.tensor_tensor(gate[:, r % NB], gate[:, r % NB], cb[:, r // KD % 2], ALU.mult)\
                    .then_inc(sc_done.sem, 1)

            def expert_low(b, r):
                pool.wait_ge(ahi_done.sem, ahi_done.at(b, r + 1))
                pool.tensor_tensor(ap2[:, r % NB, 1], af[:, r % NB], ap2[:, r % NB, 0], ALU.subtract)\
                    .then_inc(alo_done.sem, 1)

            def expert_out(b, c, ahead):
                pool.wait_ge(moe_g.sem, moe_g.at(b, c + 1))
                pool.wait_ge(block_done.sem, block_done.at(b, c + 1))
                pool.wait_ge(x2n.sem, x2n.at(ahead, NC))
                pool.wait_ge(out_sent.sem, out_sent.at(b, c))
                pool.tensor_tensor(outc[:], chunk(so, c), gate1[:], ALU.mult).then_inc(out_m.sem, 1)
                pool.wait_ge(out_m.sem, out_m.at(b, c + 1))
                pool.tensor_tensor(outc[:], outc[:], chunk(x2, c), ALU.add).then_inc(out_ready.sem, 1)

            def batch(b0, b1, last=False):
                for c in range(NC):
                    for n in range(NS):
                        if b0 is not None and c == 0 and n == LI_LOW_AT:
                            l0_low(b0, 1)
                        if b0 is not None:
                            for task in tasks(n):
                                ffn_task(b0, c, task)
                        if b1 is not None:
                            state_add(b1, c, n)
                if b1 is None:
                    for c in range(NC):
                        l0_out(b0, c)
                    l0_low(b0 + 1, 0)
                else:
                    ahead = 0 if b0 is not None else b1
                    for r in range(Q + LAG):
                        if r < Q:
                            expert_weighted(b1, r)
                        if r >= LAG:
                            expert_low(b1, r - LAG)
                        if b0 is not None:
                            for at, c in ((6, 0), (11, 1)):
                                if r == at:
                                    l0_out(b0, c)
                            if not last and r == NEXT_LOW_AT:
                                l0_low(b0 + 1, 0)
                        if r == NQ + OUT_LAG:
                            expert_out(b1, 0, ahead)
                    expert_out(b1, 1, ahead)

            l0_low(0, 0)
            batch(0, None)
            next_turn(pool, "pool")
            with pool.Fori(0, B - 2):
                batch(0, -1)
                next_turn(pool, "pool")
            batch(0, -1, last=True)
            next_turn(pool, "pool")
            batch(None, -1)

        @block.scalar
        def _(act):
            act.wait_ge(packs_in, 16 * 4)
            lo, hi = PACK["A_log"]
            act.activation(aneg[:], pk[:, lo:hi].rearrange("p (t n) -> p t n", t=KD), ACT.Exp)\
                .then_inc(act_const, 1)

            def split_input(b, c):
                act.wait_ge(li_xn.sem, li_xn.at(b, c + 1))
                if c >= 1:
                    act.wait_ge(ab_mm.sem, ab_mm.at(b, c * KF))
                act.activation(xp[:, 0], xn_chunk(c), ACT.Copy).then_inc(li_hi.sem, 1)

            def l0_square(b, c):
                act.wait_ge(li_cen.sem, li_cen.at(b, c + 1))
                if c == 0:
                    act.wait_ge(le_step.sem, le_step.at(b - 1, LE_STEPS - 1))
                    act.wait_ge(x2n.sem, x2n.at(b - 1, NC))
                else:
                    act.wait_ge(h_f.sem, h_f.at(b, c * KF))
                act.activation(sq0[c][:], xn_chunk(c), ACT.Square).then_inc(li_sq.sem, 1)

            def l0_std(b, c):
                act.wait_ge(li_var.sem, li_var.at(b, c + 1))
                act.activation(rs0[:], lin_bank[c][1], ACT.Ln, bias=eps[:]).then_inc(li_ln.sem, 1)
                act.wait_ge(li_ln.sem, li_ln.at(b, c + 1))
                act.activation(rs0[:], rs0[:], ACT.Exp, scale=-0.5).then_inc(li_rstd.sem, 1)

            def ffn_task(b, c, task):
                kind, m = divmod(task, KF)
                k = c * KF + m
                if kind == 0:
                    bank = psf if m % 2 == 0 else psy
                    if c == 0 and m == 0:
                        act.wait_ge(p2_mm.sem, p2_mm.at(b - 2, Q))
                        act.wait_ge(out_sent.sem, out_sent.at(b - 2, NC))
                        act.wait_ge(x2n.sem, x2n.at(b - 1, NC))
                        act.wait_ge(head_done.sem, head_done.at(b - 1, 1))
                    act.wait_ge(ab_mm.sem, ab_mm.at(b, k + 1))
                    act.wait_ge(h_f.sem, h_f.at(b, k - 1))
                    act.activation(sa[:, m % 2], bank[:, 0], ACT.Silu, scale=col("w1_s", m))\
                        .then_inc(silu_a.sem, 1)
                elif kind == 1:
                    act.wait_ge(g1_mm.sem, g1_mm.at(b, k + 1))
                    if m < 2:
                        act.wait_ge(h_lo.sem, h_lo.at(b, c * KF + KF))
                    else:
                        act.wait_ge(g1_lo.sem, g1_lo.at(b, k - 1))
                    act.activation(tf[:, m % 2], psf[:, m % 2], ACT.Gelu, scale=s_g1[:, m:m + 1])\
                        .then_inc(g1_f.sem, 1)
                else:
                    act.wait_ge(g2_mm.sem, g2_mm.at(b, k + 1))
                    if m < 2:
                        act.wait_ge(g1_lo.sem, g1_lo.at(b, c * KF + KF))
                    else:
                        act.wait_ge(g2_lo.sem, g2_lo.at(b, k - 1))
                    act.activation(tf[:, m % 2], psf[:, m % 2], ACT.Gelu, scale=s_g2[:, m:m + 1])\
                        .then_inc(g2_f.sem, 1)

            def ffn_high(b, c, task):
                kind, m = divmod(task, KF)
                k = c * KF + m
                if kind == 0:
                    act.wait_ge(h_f.sem, h_f.at(b, k + 1))
                    if m == 0:
                        act.wait_ge(g1_mm.sem, g1_mm.at(b, c * KF))
                    act.activation(hp[:, 0, m], tf[:, m % 2], ACT.Copy).then_inc(h_hi.sem, 1)
                elif kind == 1:
                    act.wait_ge(g1_f.sem, g1_f.at(b, k + 1))
                    if m == 0:
                        act.wait_ge(g2_mm.sem, g2_mm.at(b, c * KF))
                    act.activation(g1p[:, 0, m], tf[:, m % 2], ACT.Copy, scale=G_UP).then_inc(g1_hi.sem, 1)
                else:
                    act.wait_ge(g2_f.sem, g2_f.at(b, k + 1))
                    act.wait_ge(w3_mm.sem, w3_mm.at(b, k - 1))
                    act.activation(g2p[:, m % 2, 0], tf[:, m % 2], ACT.Copy).then_inc(g2_hi.sem, 1)

            def l0_gate(b, c):
                act.wait_ge(w3_mm.sem, w3_mm.at(b, (c + 1) * KF))
                act.wait_ge(y_acc.sem, y_acc.at(b - 1, (c + 1) * NS))
                for t in range(KD):
                    last = act.activation(gx[:, t, c * N:(c + 1) * N], psg[:, t], ACT.Silu,
                                          scale=col("w3_s", t))
                last.then_inc(gate0.sem, 1)

            def q_expo(b):
                act.wait_ge(q_min.sem, q_min.at(b, 1))
                act.activation(qe[:], qe[:], ACT.Exp).then_inc(q_exp.sem, 1)

            def turn_copy(b):
                act.wait_ge(turned.sem, turned.at(b, 1))
                act.activation(qt[:], psf[:, 0].rearrange("p (j c) -> p j c", j=2), ACT.Copy)\
                    .then_inc(qt_done.sem, 1)
                act.activation(vt[:], psf[:, 1].rearrange("p (j c) -> p j c", j=2), ACT.Copy)\
                    .then_inc(vt_done.sem, 1)

            def lb_square(b, c):
                act.wait_ge(lb_cen.sem, lb_cen.at(b, c + 1))
                act.wait_ge(lb_var.sem, lb_var.at(b, c))
                act.activation(sqb[:], chunk(y0, c), ACT.Square).then_inc(lb_sq.sem, 1)

            def lb_root(b, c):
                act.wait_ge(lb_var.sem, lb_var.at(b, c + 1))
                act.wait_ge(lb_step.sem, lb_step.at(b, LB_STEPS * c))
                act.activation(rsb[:], psf[:, 1], ACT.Ln, bias=eps[:]).then_inc(lb_ln.sem, 1)
                act.wait_ge(lb_ln.sem, lb_ln.at(b, c + 1))
                act.activation(rsb[:], rsb[:], ACT.Exp, scale=-0.5).then_inc(lb_rstd.sem, 1)

            def head_copy(b, c):
                act.wait_ge(x2n.sem, x2n.at(b, c + 1))
                act.wait_ge(out_ready.sem, out_ready.at(b - 1, c + 1))
                act.activation(chunk(x2, c), chunk(gx, c), ACT.Copy).then_inc(le_copy.sem, 1)

            def head_square(b, c):
                act.wait_ge(le_cen.sem, le_cen.at(b, c + 1))
                if c == 0:
                    act.wait_ge(f2_mm.sem, f2_mm.at(b - 1, NC * KF))
                else:
                    act.wait_ge(head_done.sem, head_done.at(b, c))
                act.activation(sq1[:], xc[c], ACT.Square).then_inc(le_sq.sem, 1)

            def head_root(b, c):
                act.wait_ge(le_var.sem, le_var.at(b, c + 1))
                act.activation(v1[:], hb[c], ACT.Ln, bias=eps[:]).then_inc(le_ln.sem, 1)
                act.wait_ge(le_ln.sem, le_ln.at(b, 2 * c + 1))
                act.activation(delta[c][:, 0], v1[:], ACT.Exp, scale=-0.5)
                act.activation(v1[:], v1[:], ACT.Exp, scale=-1.0).then_inc(le_rstd.sem, 1)

            def head_root1(b, c):
                act.wait_ge(le_step.sem, le_step.at(b, LE_STEPS * c + 1))
                act.activation(delta[c][:, 1], v1[:], ACT.Ln, bias=eps[:]).then_inc(le_ln.sem, 1)
                act.wait_ge(le_ln.sem, le_ln.at(b, 2 * c + 2))
                act.activation(delta[c][:, 1], delta[c][:, 1], ACT.Exp, scale=-0.5).then_inc(le_rstd1.sem, 1)

            def head_b16(b, c):
                act.wait_ge(le_step.sem, le_step.at(b, LE_STEPS * c + 2))
                act.wait_ge(moe_s.sem, moe_s.at(b - 1, c + 1))
                act.activation(chunk(xb, c), xc[c], ACT.Copy).then_inc(le_xb.sem, 1)

            def softplus(b, c):
                act.wait_ge(z_done.sem, z_done.at(b, KD * (c + 1)))
                act.activation(delta[c][:], zt[:], ACT.Abs).then_inc(z_abs.sem, 1)
                act.wait_ge(z_abs.sem, z_abs.at(b, c + 1))
                act.activation(delta[c][:], delta[c][:], ACT.Exp, scale=-1.0).then_inc(z_exp.sem, 1)
                act.wait_ge(z_exp.sem, z_exp.at(b, c + 1))
                act.activation(delta[c][:], delta[c][:], ACT.Ln, bias=1.0).then_inc(z_ln.sem, 1)

            def decay(b, c, n):
                k = c * NS + n
                if n == 0:
                    act.wait_ge(head_done.sem, head_done.at(b, c + 1))
                if k == 0:
                    act.wait_ge(p2_mm.sem, p2_mm.at(b - 1, Q))
                act.wait_ge(scan_done.sem, scan_done.at(b, k - 3))
                for t in range(KD):
                    last = act.activation(da[:, n % 4, t], delta[c][:, t], ACT.Exp, scale=aneg[:, t, n:n + 1])
                last.then_inc(da_done.sem, 1)

            def lf_square(b, c, beside):
                act.wait_ge(lf_cen.sem, lf_cen.at(b, c + 1))
                if c == 0:
                    act.wait_ge(out_sent.sem, out_sent.at(b - 1, NC))
                    if beside:
                        act.wait_ge(h_f.sem, h_f.at(b + 1, NC * KF))
                else:
                    act.wait_ge(lf_var.sem, lf_var.at(b, c))
                act.activation(sq2[:], nrm[c][:], ACT.Square).then_inc(lf_sq.sem, 1)

            def lf_root(b, c):
                act.wait_ge(lf_var.sem, lf_var.at(b, c + 1))
                act.wait_ge(lf_step.sem, lf_step.at(b, 2 * c))
                act.activation(rs3[:], lf_bank[c], ACT.Ln, bias=eps[:]).then_inc(lf_ln.sem, 1)
                act.wait_ge(lf_ln.sem, lf_ln.at(b, c + 1))
                act.activation(rs3[:], rs3[:], ACT.Exp, scale=-0.5).then_inc(lf_rstd.sem, 1)

            def hidden1(b, c, m):
                k = c * KF + m
                act.wait_ge(f1_mm.sem, f1_mm.at(b, k + 1))
                if k == 0:
                    act.wait_ge(scan_done.sem, scan_done.at(b, NC * NS))
                act.wait_ge(f2_mm.sem, f2_mm.at(b, k - 1))
                act.activation(hff[:, m % 2], psy[:, m % 2], ACT.Gelu, bias=col("b1", m))\
                    .then_inc(f1_done.sem, 1)

            def expert_square(b, c):
                if c == 0:
                    act.wait_ge(le_xb.sem, le_xb.at(b, NC))
                    act.wait_ge(lf_var.sem, lf_var.at(b, NC))
                else:
                    act.wait_ge(m_ms.sem, m_ms.at(b, c))
                act.activation(sqm[:], chunk(xb, c), ACT.Square).then_inc(m_sq.sem, 1)

            def expert_root(b, c):
                act.wait_ge(m_ms.sem, m_ms.at(b, c + 1))
                act.wait_ge(m_step.sem, m_step.at(b, c))
                act.activation(rsm[:], psg[:, 1], ACT.Ln, bias=eps[:]).then_inc(m_ln.sem, 1)
                act.wait_ge(m_ln.sem, m_ln.at(b, c + 1))
                act.activation(rsm[:], rsm[:], ACT.Exp, scale=-0.5).then_inc(m_rms.sem, 1)

            def gate_exp(b):
                act.wait_ge(gate_d.sem, gate_d.at(b, 1))
                act.activation(gex[:], gex[:], ACT.Exp).then_inc(gate_e.sem, 1)

            def gate_copy(b, k):
                act.wait_ge(cb_mm.sem, cb_mm.at(b, k + 1))
                if k >= 2:
                    act.wait_ge(sc_done.sem, sc_done.at(b, (k - 1) * KD))
                act.activation(cb[:, k % 2], psf[:, 0], ACT.Copy, scale=1.0 / ALPHA)\
                    .then_inc(cb_done.sem, 1)

            def expert_silu(b, r):
                act.wait_ge(gmin_done.sem, gmin_done.at(b, r + 1))
                act.activation(gate[:, r % NB], gate[:, r % NB], ACT.Silu, scale=ALPHA)\
                    .then_inc(sg_done.sem, 1)

            def expert_high(b, r):
                act.wait_ge(af_done.sem, af_done.at(b, r + 1))
                if r >= NB:
                    act.wait_ge(p2_mm.sem, p2_mm.at(b, r - NB + 1))
                act.activation(ap2[:, r % NB, 0], af[:, r % NB], ACT.Copy).then_inc(ahi_done.sem, 1)

            def expert_gate(b, c):
                act.wait_ge(moe_s.sem, moe_s.at(b, c + 1))
                if c >= 1:
                    act.wait_ge(out_m.sem, out_m.at(b, c))
                act.activation(gate1[:], sum16[:], ACT.Silu).then_inc(moe_g.sem, 1)

            def batch(b0, b1, last=False):
                for c in range(NC):
                    if b1 is not None:
                        decay(b1, c, 0)
                        decay(b1, c, 1)
                    for n in range(NS):
                        if b1 is not None and n % 2 == 0 and n + 2 < NS:
                            decay(b1, c, n + 2)
                            decay(b1, c, n + 3)
                        if b0 is not None and c == 0:
                            for at, piece in ((LI_SQ_AT, l0_square), (LI_VAR_AT, l0_std), (LI_SPLIT_AT, split_input)):
                                if n == at:
                                    piece(b0, 1)
                        if b1 is not None and c == 0:
                            for at, piece in ((4, head_copy), (6, head_square), (7, head_root), (9, head_root1),
                                              (9, head_b16), (12, softplus)):
                                if n == at:
                                    piece(b1, 1)
                        if b0 is not None and c == 1 and n == GATE0_AT:
                            l0_gate(b0, 0)
                        if b1 is not None and c == 1:
                            if n == 6:
                                lf_square(b1, 0, b0 is not None)
                            if n == 7:
                                lf_root(b1, 0)
                        if b0 is not None:
                            for task in tasks(n):
                                if task == KF:
                                    ffn_high(b0, c, task - 1)
                                ffn_task(b0, c, task)
                                if 1 <= task < KF:
                                    ffn_high(b0, c, task - 1)
                                elif task >= KF:
                                    ffn_high(b0, c, task)
                if b1 is not None:
                    lf_square(b1, 1, b0 is not None)
                if b0 is not None:
                    l0_gate(b0, 1)
                if b1 is None:
                    q_expo(b0)
                    turn_copy(b0)
                else:
                    for k in range(NC * KF):
                        if k == LF_VAR_AT:
                            lf_root(b1, 1)
                            expert_square(b1, 0)
                        if k == RMS_AT:
                            expert_root(b1, 0)
                            expert_square(b1, 1)
                        if k == RMS1_AT:
                            expert_root(b1, 1)
                        if b0 is not None and k == ATTN_AT:
                            q_expo(b0)
                            turn_copy(b0)
                        if k == NUM_AT:
                            gate_exp(b1)
                        hidden1(b1, *divmod(k, KF))
                if b1 is None:
                    for c in range(NC):
                        lb_square(b0, c)
                        lb_root(b0, c)
                if b1 is not None:
                    gate_copy(b1, 0)
                    for r in range(Q + LAG):
                        if r < Q:
                            expert_silu(b1, r)
                        if r >= LAG:
                            expert_high(b1, r - LAG)
                        if r % KD == 0 and r // KD + 1 < NC * E:
                            gate_copy(b1, r // KD + 1)
                        if b0 is not None:
                            for at, piece, c in ((2, lb_square, 0), (3, lb_root, 0), (6, lb_square, 1),
                                                 (8, lb_root, 1), (11, head_square, 0), (13, head_root, 0),
                                                 (15, head_root1, 0), (22, softplus, 0),
                                                 (LATE_AT, head_copy, 0), (LATE_AT, head_b16, 0)):
                                if r == at:
                                    piece(b0, c)
                        if b0 is not None and not last:
                            for at, piece in ((NEXT_SQ_AT, l0_square), (NEXT_STD_AT, l0_std),
                                              (NEXT_SPLIT_AT, split_input)):
                                if r == at:
                                    piece(b0 + 1, 0)
                        if r == NQ + LAG_DOWN + 1:
                            expert_gate(b1, 0)
                    expert_gate(b1, 1)
                else:
                    for piece in (head_square, head_root, head_root1, softplus, head_copy, head_b16):
                        piece(b0, 0)
                    for piece in (l0_square, l0_std, split_input):
                        piece(b0 + 1, 0)

            act.wait_ge(dve_const, DVE_CONST)
            l0_square(0, 0)
            l0_std(0, 0)
            split_input(0, 0)
            batch(0, None)
            next_turn(act, "act")
            with act.Fori(0, B - 2):
                batch(0, -1)
                next_turn(act, "act")
            batch(0, -1, last=True)
            next_turn(act, "act")
            batch(None, -1)

        @block.tensor
        def _(pe):
            def average(out, rhs):
                for k in range(KD):
                    last = pe.matmul(out, meanw[:], rhs[:, k], start=(k == 0), stop=(k == KD - 1))
                return last

            def l0_mean(b, c):
                pe.wait_ge(x_in[c].sem, x_in[c].at(b, 1))
                if c == 0:
                    pe.wait_ge(le_step.sem, le_step.at(b - 1, LE_PARTS))
                else:
                    pe.wait_ge(h_f.sem, h_f.at(b, c * KF))
                average(lin_bank[c][0], xn_chunk(c)).then_inc(li_mean.sem, 1)

            def l0_var(b, c):
                pe.wait_ge(li_sq.sem, li_sq.at(b, c + 1))
                average(lin_bank[c][1], sq0[c]).then_inc(li_var.sem, 1)

            def ffn_task(b, c, task):
                kind, m = divmod(task, KF)
                k = c * KF + m
                cols = slice(m * P, (m + 1) * P)
                if kind == 0:
                    bank = psf if m % 2 == 0 else psy
                    if m == 0 and c == 0:
                        pe.wait_ge(cb_done.sem, cb_done.at(b - 2, NC * E))
                    if m == 0:
                        pe.wait_ge(w12_in, 32)
                        pe.wait_ge(li_lo.sem, li_lo.at(b, c + 1))
                        pe.wait_ge(li_ln.sem, li_ln.at(b, c + 1))
                    elif m == 1 and c == 0:
                        pe.wait_ge(lin_done.sem, lin_done.at(b - 2, Q))
                    elif m == 1:
                        pe.wait_ge(head_done.sem, head_done.at(b - 1, NC))
                    if m >= 2:
                        pe.wait_ge(silu_a.sem, silu_a.at(b, k - 1))
                        pe.wait_ge(h_f.sem, h_f.at(b, k - 1))
                    for half, w in enumerate((w1, w2)):
                        for t in range(KD):
                            for part in range(2):
                                last = pe.matmul(bank[:, half], w[:, t, cols], xp[:, part, t],
                                                 start=(t == 0 and part == 0),
                                                 stop=(t == KD - 1 and part == 1))
                    last.then_inc(ab_mm.sem, 1)
                    return
                if kind == 1:
                    src, w, mm, free, parts = hp, h1w, g1_mm, g1_f, (h_hi, h_lo)
                else:
                    src, w, mm, free, parts = g1p, h2w, g2_mm, g2_f, (g1_hi, g1_lo)
                if m >= 2:
                    pe.wait_ge(free.sem, free.at(b, k - 1))
                elif m == 0:
                    pe.wait_ge(*((h1_in, 16) if kind == 1 else (h2_in, 16)))
                    before = h_f if kind == 1 else g1_f
                    pe.wait_ge(before.sem, before.at(b, c * KF + KF - 1))
                for part in range(2):
                    for t in range(KF):
                        if m == 0:
                            pe.wait_ge(parts[part].sem, parts[part].at(b, c * KF + t + 1))
                        last = pe.matmul(psf[:, m % 2], w[:, t, cols], src[:, part, t],
                                         start=(t == 0 and part == 0), stop=(t == KF - 1 and part == 1))
                last.then_inc(mm.sem, 1)
                if kind == 2 and m >= 1:
                    project(b, c, m - 1)

            def project(b, c, m):
                k = c * KF + m
                pe.wait_ge(g2_hi.sem, g2_hi.at(b, k + 1))
                pe.wait_ge(g2_lo.sem, g2_lo.at(b, k + 1))
                if k == 0:
                    pe.wait_ge(w3_in, 16)
                    pe.wait_ge(kv_masked.sem, kv_masked.at(b - 1, 1))
                    pe.wait_ge(lin_done.sem, lin_done.at(b - 2, Q))
                elif m == 0:
                    pe.wait_ge(gate0.sem, gate0.at(b, c))
                for t in range(KD):
                    for part in range(2):
                        last = pe.matmul(psg[:, t], w3[:, m, t * P:(t + 1) * P], g2p[:, m % 2, part],
                                         start=(m == 0 and part == 0), stop=(m == KF - 1 and part == 1))
                last.then_inc(w3_mm.sem, 1)

            def attention_turn(b):
                pe.wait_ge(q_done.sem, q_done.at(b, 1))
                pe.wait_ge(g2_f.sem, g2_f.at(b, NC * KF))
                pe.wait_ge(lf_ln.sem, lf_ln.at(b - 1, NC))
                for half, src in enumerate((q0, l2)):
                    for j in range(2):
                        for t in range(KD):
                            last = pe.transpose(psf[:, half, (j * KD + t) * P:(j * KD + t + 1) * P],
                                                src[:, t, j * P:(j + 1) * P], ident[:])
                last.then_inc(turned.sem, 1)

            def attention_kv(b):
                pe.wait_ge(qt_done.sem, qt_done.at(b, 1))
                pe.wait_ge(vt_done.sem, vt_done.at(b, 1))
                pe.wait_ge(gate0.sem, gate0.at(b, NC))
                for t in range(KD):
                    for j in range(2):
                        last = pe.matmul(psg[:, 0, t * P:(t + 1) * P], qt[:, j, t * P:(t + 1) * P],
                                         vt[:, j, t * P:(t + 1) * P], start=(j == 0), stop=(j == 1))
                last.then_inc(kv_mm.sem, 1)

            def attention_num(b):
                pe.wait_ge(kv_masked.sem, kv_masked.at(b, 1))
                for half, w in enumerate((kvm, zm)):
                    for t in range(KD):
                        last = pe.matmul(psf[:, half, t * N // 2:(t + 1) * N // 2], w[:, t], q0[:, t],
                                         start=True, stop=True)
                last.then_inc(num_mm.sem, 1)

            def lb_average(b, c):
                pe.wait_ge(y_done.sem, y_done.at(b, 1))
                pe.wait_ge(lb_ln.sem, lb_ln.at(b, c))
                average(psf[:, 1], chunk(y0, c)).then_inc(lb_mean.sem, 1)

            def lb_variance(b, c):
                pe.wait_ge(lb_sq.sem, lb_sq.at(b, c + 1))
                average(psf[:, 1], sqb).then_inc(lb_var.sem, 1)

            def head_mean(b, c):
                pe.wait_ge(x2n.sem, x2n.at(b, c + 1))
                if c == 0:
                    pe.wait_ge(lb_ln.sem, lb_ln.at(b, NC))
                else:
                    pe.wait_ge(lin_done.sem, lin_done.at(b - 1, Q))
                average(hb[c], chunk(gx, c)).then_inc(le_mean.sem, 1)

            def head_var(b, c):
                pe.wait_ge(le_sq.sem, le_sq.at(b, c + 1))
                average(hb[c], sq1).then_inc(le_var.sem, 1)

            def head_delta(b, c, t):
                if t == 0:
                    pe.wait_ge(le_step.sem, le_step.at(b, LE_STEPS * c + HEAD_STEPS))
                else:
                    pe.wait_ge(z_done.sem, z_done.at(b, c * KD + t))
                for k in range(KD):
                    last = pe.matmul(hb[c], wd[:, k, t * P:(t + 1) * P], xn1[c][:, k],
                                     start=(k == 0), stop=(k == KD - 1))
                last.then_inc(dt_mm.sem, 1)

            def head_delta0(b, c):
                head_delta(b, c, 0)

            def head_delta1(b, c):
                head_delta(b, c, 1)

            def head_bc(b, c):
                pe.wait_ge(z_done.sem, z_done.at(b, (c + 1) * KD))
                for k in range(KD):
                    last = pe.matmul(hb[c][0:64], wbc[:, k], xn1[c][:, k], start=(k == 0), stop=(k == KD - 1))
                last.then_inc(bc_mm.sem, 1)

            def spread_bc(b, c, n):
                k = c * NS + n
                if n == 0:
                    pe.wait_ge(head_done.sem, head_done.at(b, c + 1))
                if k == 0:
                    pe.wait_ge(moe_r.sem, moe_r.at(b - 1, NC))
                else:
                    pe.wait_ge(u_done.sem, u_done.at(b, k))
                pe.matmul(psb[:, 0], sel[:, n:n + 1].broadcast_to([64, P]), bcs[c][:], start=True, stop=True)\
                    .then_inc(b_mm.sem, 1)
                if n == 0 and c == 0:
                    pe.wait_ge(moe_r.sem, moe_r.at(b - 1, NC))
                else:
                    pe.wait_ge(cy_done.sem, cy_done.at(b, k))
                pe.matmul(psb[:, 1], sel[:, NS + n:NS + n + 1].broadcast_to([64, P]), bcs[c][:],
                          start=True, stop=True).then_inc(c_mm.sem, 1)

            def lf_average(b, c, beside):
                pe.wait_ge(y_acc.sem, y_acc.at(b, (c + 1) * NS))
                if c == 0:
                    pe.wait_ge(head_done.sem, head_done.at(b, NC))
                    if beside:
                        pe.wait_ge(h_f.sem, h_f.at(b + 1, NC * KF))
                elif beside:
                    pe.wait_ge(g2_f.sem, g2_f.at(b + 1, NC * KF))
                average(lf_bank[c], chunk(so, c)).then_inc(lf_mean.sem, 1)

            def lf_variance(b, c):
                pe.wait_ge(lf_sq.sem, lf_sq.at(b, c + 1))
                average(lf_bank[c], sq2).then_inc(lf_var.sem, 1)

            def hidden1(b, c, m):
                k = c * KF + m
                if k == 0:
                    pe.wait_ge(wf1_in.sem, wf1_in.at(b, 1))
                if m == 0:
                    pe.wait_ge(lf_step.sem, lf_step.at(b, 2 * (c + 1)))
                if k >= 2:
                    pe.wait_ge(f1_done.sem, f1_done.at(b, k - 1))
                for t in range(KD):
                    last = pe.matmul(psy[:, m % 2], wf1[:, t, m * P:(m + 1) * P], nrm[c][:, t],
                                     start=(t == 0), stop=(t == KD - 1))
                last.then_inc(f1_mm.sem, 1)

            def hidden2(b, c, m):
                k = c * KF + m
                pe.wait_ge(f1_done.sem, f1_done.at(b, k + 1))
                if m == 0:
                    pe.wait_ge(cy_done.sem, cy_done.at(b, NC * NS))
                    pe.wait_ge(block_done.sem, block_done.at(b, c))
                for t in range(KD):
                    last = pe.matmul(psb[:, t], wf2[:, m, t * P:(t + 1) * P], hff[:, m % 2],
                                     start=(m == 0), stop=(m == KF - 1))
                last.then_inc(f2_mm.sem, 1)

            def expert_mean(b, c, ahead):
                pe.wait_ge(m_sq.sem, m_sq.at(b, c + 1))
                if c == 0:
                    pe.wait_ge(gate0.sem, gate0.at(ahead, NC))
                else:
                    pe.wait_ge(m_ln.sem, m_ln.at(b, c))
                average(psg[:, 1], sqm).then_inc(m_ms.sem, 1)

            def expert_logits(b):
                pe.wait_ge(m_ln.sem, m_ln.at(b, NC))
                pe.wait_ge(nf_done.sem, nf_done.at(b, NC))
                for j in range(NJ):
                    out = psg[:, 1, j * E:(j + 1) * E]
                    c, at = divmod(j * P, N)
                    for t in range(KD):
                        pe.matmul(out, nf[:, c, t, at:at + P], wgate[:, t], start=(t == 0), stop=False)
                    last = pe.matmul(out, ones16[:], gbias[:], start=False, stop=True)
                last.then_inc(gate_mm.sem, 1)

            def expert_turn(b, c):
                pe.wait_ge(comb_done.sem, comb_done.at(b, 1))
                if c >= 1:
                    pe.wait_ge(ct_done.sem, ct_done.at(b, 2 * c - 1))
                for j in range(N // P):
                    last = pe.transpose(psg[0:64, 1, j * P:(j + 1) * P], comb[:, c * N // P + j], ident[:])
                last.then_inc(comb_t.sem, 1)

            def expert_spread(b, k, ahead):
                if k == 0:
                    pe.wait_ge(cs_done.sem, cs_done.at(b, NC))
                    pe.wait_ge(y_done.sem, y_done.at(ahead, 1))
                else:
                    pe.wait_ge(cb_done.sem, cb_done.at(b, k))
                c, e = divmod(k, E)
                pe.matmul(psf[:, 0], sel[:, e:e + 1].broadcast_to([64, P]), cs[:, c],
                          start=True, stop=True).then_inc(cb_mm.sem, 1)

            def expert_up(b, r, ahead):
                c, q = divmod(r, NQ)
                e, t = divmod(q, KD)
                bank = psy if r % 2 == 0 else psg
                if r == 0:
                    pe.wait_ge(mw_in.sem, mw_in.at(b, 2))
                    pe.wait_ge(f1_done.sem, f1_done.at(b, NC * KF))
                elif r == 1:
                    pe.wait_ge(kv_masked.sem, kv_masked.at(ahead, 1))
                    pe.wait_ge(ct_done.sem, ct_done.at(b, 2 * NC))
                else:
                    pe.wait_ge(lin_done.sem, lin_done.at(b, r - 1))
                for half in range(2):
                    for kk in range(KD):
                        last = pe.matmul(bank[:, half], mw1[:, e, kk, half, t * P:(t + 1) * P], nf[:, c, kk],
                                         start=(kk == 0), stop=(kk == KD - 1))
                last.then_inc(p1_mm.sem, 1)

            def expert_down(b, r):
                c, q = divmod(r, NQ)
                e, t = divmod(q, KD)
                if q == 0:
                    if c == 0:
                        pe.wait_ge(block_done.sem, block_done.at(b, NC))
                    else:
                        pe.wait_ge(moe_r.sem, moe_r.at(b, c))
                    for h in range(KD):
                        pe.matmul(psb[:, h], b2s[:, h * P:(h + 1) * P], cs[:, c], start=True, stop=False)
                pe.wait_ge(alo_done.sem, alo_done.at(b, r + 1))
                for h in range(KD):
                    for part in range(2):
                        last = pe.matmul(psb[:, h], mw2[:, e, t, h * P:(h + 1) * P], ap2[:, r % NB, part],
                                         start=False, stop=(q == NQ - 1 and part == 1))
                last.then_inc(p2_mm.sem, 1)

            def batch(b0, b1, last=False):
                for c in range(NC):
                    for n in range(NS):
                        if b1 is not None:
                            spread_bc(b1, c, n)
                        if b0 is not None and c == 0:
                            for at, piece in ((LI_AT, l0_mean), (LI_VAR_AT, l0_var)):
                                if n == at:
                                    piece(b0, 1)
                        if b1 is not None and c == 0:
                            for at, piece in ((5, head_mean), (7, head_var), (10, head_delta0), (11, head_delta1),
                                              (12, head_bc)):
                                if n == at:
                                    piece(b1, 1)
                        if b1 is not None and c == 1:
                            if n == 4:
                                lf_average(b1, 0, b0 is not None)
                            if n == 7:
                                lf_variance(b1, 0)
                        if b0 is not None:
                            for task in tasks(n):
                                ffn_task(b0, c, task)
                    if b0 is not None:
                        project(b0, c, KF - 1)
                ahead = 0 if b0 is not None else b1
                if b1 is not None:
                    lf_average(b1, 1, b0 is not None)
                    for k in range(NC * KF + 1):
                        if k == LF_VAR_AT:
                            lf_variance(b1, 1)
                        if k == RMS_AT:
                            expert_mean(b1, 0, ahead)
                        if k == RMS1_AT:
                            expert_mean(b1, 1, ahead)
                        if k == LOGITS_AT:
                            expert_logits(b1)
                        if b0 is not None and k == ATTN_AT:
                            attention_turn(b0)
                            attention_kv(b0)
                        if b0 is not None and k == NUM_AT:
                            attention_num(b0)
                        if k == TURN_AT:
                            expert_turn(b1, 0)
                        if k == TURN1_AT:
                            expert_turn(b1, 1)
                        if k < NC * KF:
                            hidden1(b1, *divmod(k, KF))
                        if k >= 1:
                            hidden2(b1, *divmod(k - 1, KF))
                elif b0 is not None:
                    attention_turn(b0)
                    attention_kv(b0)
                    attention_num(b0)
                if b1 is None:
                    for c in range(NC):
                        lb_average(b0, c)
                        lb_variance(b0, c)
                if b1 is not None:
                    expert_spread(b1, 0, ahead)
                    for r in range(Q + LAG_DOWN):
                        if r < Q:
                            expert_up(b1, r, ahead)
                        if r % KD == 0 and r // KD + 1 < NC * E:
                            expert_spread(b1, r // KD + 1, ahead)
                        if r >= LAG_DOWN:
                            expert_down(b1, r - LAG_DOWN)
                        if b0 is not None:
                            for at, piece, c in ((0, lb_average, 0), (3, lb_variance, 0), (5, lb_average, 1),
                                                 (8, lb_variance, 1), (11, head_mean, 0), (13, head_var, 0),
                                                 (18, head_delta0, 0), (20, head_delta1, 0), (22, head_bc, 0)):
                                if r == at:
                                    piece(b0, c)
                        if b0 is not None and not last:
                            for at, piece in ((NEXT_AT, l0_mean), (NEXT_VAR_AT, l0_var)):
                                if r == at:
                                    piece(b0 + 1, 0)
                else:
                    for piece in (head_mean, head_var, head_delta0, head_delta1, head_bc):
                        piece(b0, 0)
                    l0_mean(b0 + 1, 0)
                    l0_var(b0 + 1, 0)

            pe.wait_ge(dve_const, DVE_CONST)
            pe.wait_ge(pool_const, POOL_CONST)
            l0_mean(0, 0)
            l0_var(0, 0)
            batch(0, None)
            pe.wait_ge(wl1_in, 48)
            pe.wait_ge(packs_in, 64)
            pe.wait_ge(b2_in, 32)
            next_turn(pe, "pe")
            with pe.Fori(0, B - 2):
                batch(0, -1)
                next_turn(pe, "pe")
            batch(0, -1, last=True)
            next_turn(pe, "pe")
            batch(None, -1)

        @block.vector
        def _(dve):
            k = 0

            def const(ins):
                nonlocal k
                k += 1
                ins.then_inc(dve_const, 1)

            dve.memset(b2s[:].bitcast(F32), 0.0).then_inc(b2s_zero, 1)
            const(dve.memset(meanw[:], 1.0 / D))
            const(dve.memset(eps[:], LN_EPS))
            const(dve.memset(ones16[:], 1.0))
            for side in (0, L + 1):
                const(dve.memset(xn[:, :, side:side + 1], 0.0))
            dve.wait_ge(pool_const, POOL_CONST)
            const(dve.tensor_tensor(sel[:], ident[0:64, 0:32], ident[0:64, 32:64], ALU.add))
            dve.wait_ge(packs_in, 64)
            for j, name in enumerate(("h_synth", "g_synth")):
                lo, hi = PACK[name]
                f = pk[:, lo:hi].rearrange("p (t k) -> p t k", k=4)
                const(dve.tensor_copy(synth[:, j, :, 0:1], f[:, :, 0:1]))
                const(dve.tensor_tensor(synth[:, j, :, 1:2], f[:, :, 1:2], f[:, :, 2:3], ALU.add))
                const(dve.tensor_copy(synth[:, j, :, 2:3], f[:, :, 3:4]))
                const(dve.tensor_tensor(synth[:, j, :, 3:4], f[:, :, 0:1], f[:, :, 1:2], ALU.add))
                const(dve.tensor_tensor(synth[:, j, :, 4:5], f[:, :, 2:3], f[:, :, 3:4], ALU.add))
            const(dve.tensor_scalar(s_h[:], col("w2_s", 0, KF), H_UP, None, ALU.mult))
            const(dve.tensor_scalar(s_g1[:], col("h1_s", 0, KF), 1.0 / H_UP, None, ALU.mult))
            const(dve.tensor_scalar(s_g2[:], col("h2_s", 0, KF), 1.0 / G_UP, None, ALU.mult))
            const(dve.tensor_copy(mbias[:], mbias16[:]))
            dve.wait_ge(dve_const, k)
            blin = mbias[:, :, 1]
            const(dve.tensor_scalar(lin_lo[:], blin, -1.0, -LIMIT, ALU.mult, ALU.add))
            const(dve.tensor_scalar(lin_hi[:], blin, -1.0, LIMIT, ALU.mult, ALU.add))
            const(dve.tensor_scalar(lin_one[:], blin, 1.0, None, ALU.add))
            dve.wait_ge(act_const, 1)
            const(dve.tensor_scalar(aneg[:], aneg[:], -1.0, None, ALU.mult))
            dve.wait_ge(dve_const, k)
            assert k == DVE_CONST

            def l0_center(b, c):
                dve.wait_ge(li_mean.sem, li_mean.at(b, c + 1))
                dve.tensor_tensor(xn_chunk(c), xn_chunk(c), both(lin_bank[c][0]), ALU.subtract)\
                    .then_inc(li_cen.sem, 1)

            def l0_scale(b, c):
                dve.wait_ge(li_rstd.sem, li_rstd.at(b, c + 1))
                dve.tensor_tensor(xn_chunk(c), xn_chunk(c), both(rs0[:]), ALU.mult).then_inc(li_xn.sem, 1)

            def ffn_task(b, c, task):
                kind, m = divmod(task, KF)
                k = c * KF + m
                if kind == 0:
                    bank = psf if m % 2 == 0 else psy
                    dve.wait_ge(silu_a.sem, silu_a.at(b, k + 1))
                    if m >= 2:
                        dve.wait_ge(h_lo.sem, h_lo.at(b, k - 1))
                    elif c >= 1:
                        dve.wait_ge(g2_lo.sem, g2_lo.at(b, c * KF))
                    else:
                        dve.wait_ge(x2n.sem, x2n.at(b - 1, NC))
                    dve.scalar_tensor_tensor(tf[:, m % 2], bank[:, 1], s_h[:, m:m + 1], sa[:, m % 2],
                                             ALU.mult, ALU.mult).then_inc(h_f.sem, 1)
                elif kind == 1:
                    dve.wait_ge(g1_hi.sem, g1_hi.at(b, k + 1))
                    dve.scalar_tensor_tensor(g1p[:, 1, m], tf[:, m % 2], G_UP, g1p[:, 0, m],
                                             ALU.mult, ALU.subtract).then_inc(g1_lo.sem, 1)

            def wavelets_and_attention(b, b1):
                n = 0

                def step(ins):
                    nonlocal n
                    n += 1
                    ins.then_inc(conv.sem, 1)

                def settle(back):
                    dve.wait_ge(conv.sem, conv.at(b, n - back))

                def filters(terms, lag):
                    depth = max(len(t) for _, t, _ in terms)
                    for j in range(depth):
                        for out, views, base in terms:
                            if j >= len(views):
                                continue
                            view, scalar = views[j]
                            if n:
                                settle(0 if len(terms) < 2 else lag)
                            if j == 0 and base is None:
                                step(dve.tensor_scalar(out, view, scalar, None, ALU.mult))
                            else:
                                step(dve.scalar_tensor_tensor(out, view, scalar, out if j else base,
                                                              ALU.mult, ALU.add))

                def taps(name, t):
                    lo, _ = PACK[name]
                    return [pk[:, lo + 4 * t + j:lo + 4 * t + j + 1] for j in range(4)]

                def analysis(src, width, low, high, tiles=range(KD)):
                    terms = []
                    for t in tiles:
                        for name, out in (("h_filter", low), ("g_filter", high)):
                            f = taps(name, t)
                            views = [(src[:, t, j:j + width - 1:2], f[j]) for j in range(4)]
                            terms.append((out(t), views, None))
                    filters(terms, len(terms) - 1)

                dve.wait_ge(g2_mm.sem, g2_mm.at(b, NC * KF))
                half, quarter = L // 2, L // 4
                for buf, width in ((l1b, half), (h1b, half), (h2b, quarter), (low2, quarter), (low1, half)):
                    for side in (0, width + 1):
                        step(dve.memset(buf[:, :, side:side + 1], 0.0))
                for t in range(KD):
                    analysis(xn, L, lambda t: l1b[:, t, 1:half + 1], lambda t: h1b[:, t, 1:half + 1], [t])
                    if b1 is not None and t == 0:
                        lf_scale(b1, 1)
                if b1 is not None:
                    expert_norm(b1, 0)
                    expert_norm(b1, 1)
                settle(0)
                analysis(l1b, half, lambda t: l2[:, t, :], lambda t: h2b[:, t, 1:quarter + 1])
                settle(0)
                dve.tensor_scalar(qe[:], l2[:], 0.0, None, ALU.min).then_inc(q_min.sem, 1)
                dve.wait_ge(q_exp.sem, q_exp.at(b, 1))
                dve.scalar_tensor_tensor(q0[:], l2[:], 0.0, qe[:], ALU.max, ALU.add).then_inc(q_done.sem, 1)
                dve.wait_ge(q_done.sem, q_done.at(b, 1))
                step(dve.tensor_reduce(zs[:], q0[:], AX_X, ALU.add))
                settle(0)
                for t in range(KD):
                    step(dve.tensor_scalar(zm[:, t], headmask[:], zs[:, t:t + 1], None, ALU.mult))
                if b1 is not None:
                    expert_gate(b1)
                dve.wait_ge(kv_mm.sem, kv_mm.at(b, 1))
                settle(0)
                dve.tensor_tensor(kvm[:], psg[:, 0, 0:KD * P].rearrange("p (t n) -> p t n", t=KD),
                                  headmask[:].rearrange("p (o n) -> p o n", o=1).broadcast_to([P, KD, P]),
                                  ALU.mult).then_inc(kv_masked.sem, 1)
                dve.wait_ge(num_mm.sem, num_mm.at(b, 1))
                step(dve.tensor_scalar(rden[:], psf[:, 1].rearrange("p (t n) -> p t n", t=KD), ATTN_EPS,
                                       None, ALU.add))
                settle(0)
                step(dve.reciprocal(rden[:], rden[:]))
                settle(0)
                step(dve.tensor_tensor(low2[:, :, 1:quarter + 1],
                                       psf[:, 0].rearrange("p (t n) -> p t n", t=KD), rden[:], ALU.mult))
                settle(0)

                def synthesis(low, high, width, out, base):
                    terms = []
                    for t in range(KD):
                        for odd in range(2):
                            views = []
                            for j, src in enumerate((low, high)):
                                f = [synth[:, j, t, i:i + 1] for i in range(5)]
                                if odd:
                                    views += [(src[:, t, 1:width + 1], f[3]), (src[:, t, 2:width + 2], f[4])]
                                else:
                                    views += [(src[:, t, i:width + i], f[i]) for i in range(3)]
                            terms.append((out(t, odd), views, base(t, odd) if base else None))
                    filters(terms, 1)

                if b1 is not None:
                    block_out(b1, 0)
                synthesis(low2, h2b, quarter, lambda t, odd: low1[:, t, 1 + odd:half + odd:2], None)
                settle(0)
                if b1 is not None:
                    expert_parts(b1, 0)
                    expert_parts(b1, 1)
                if b1 is not None:
                    dve.wait_ge(cs_done.sem, cs_done.at(b1, NC))
                synthesis(low1, h1b, half, lambda t, odd: y0[:, t, odd:L - 1 + odd:2],
                          lambda t, odd: xn[:, t, 1 + odd:L + odd:2])
                assert n == conv.per
                settle(0)
                dve.memset(zs[:], 0.0).then_inc(y_done.sem, 1)

            def lb_center(b, c):
                dve.wait_ge(lb_mean.sem, lb_mean.at(b, c + 1))
                dve.tensor_tensor(chunk(y0, c), chunk(y0, c), both(psf[:, 1]), ALU.subtract)\
                    .then_inc(lb_cen.sem, 1)

            def lb_scale(b, c):
                dve.wait_ge(lb_rstd.sem, lb_rstd.at(b, c + 1))
                dve.tensor_tensor(chunk(y0, c), chunk(y0, c), both(rsb[:]), ALU.mult).then_inc(lb_step.sem, 1)
                dve.wait_ge(lb_step.sem, lb_step.at(b, LB_STEPS * c + 1))
                for t in range(KD):
                    part = y0[:, t, c * N:(c + 1) * N]
                    dve.tensor_scalar(part, part, col("gamma", t), col("beta", t), ALU.mult, ALU.add)\
                        .then_inc(lb_step.sem, 1)

            def head_center(b, c):
                dve.wait_ge(le_mean.sem, le_mean.at(b, c + 1))
                if c == 1:
                    dve.wait_ge(le_copy.sem, le_copy.at(b, c + 1))
                dve.tensor_tensor(xc[c], chunk(gx, c), both(hb[c]), ALU.subtract).then_inc(le_cen.sem, 1)

            def head_step(b, c, at, ins):
                ins.then_inc(le_step.sem, 1)
                dve.wait_ge(le_step.sem, le_step.at(b, LE_STEPS * c + at))

            def head_norm(b, c):
                dve.wait_ge(le_rstd.sem, le_rstd.at(b, c + 1))
                head_step(b, c, 1, dve.tensor_tensor(v1[:], hb[c], v1[:], ALU.mult))
                head_step(b, c, 2, dve.tensor_tensor(xc[c], xc[c], both(delta[c][:, 0]), ALU.mult))

            def head_norm1(b, c):
                dve.wait_ge(le_rstd1.sem, le_rstd1.at(b, c + 1))
                if c == 0:
                    dve.wait_ge(x2n.sem, x2n.at(b, NC))
                head_step(b, c, 3, dve.tensor_tensor(xn1[c], xc[c], both(delta[c][:, 1]), ALU.mult))
                for t in range(KD):
                    last = dve.tensor_scalar(xn1[c][:, t], xn1[c][:, t], col("ln1_g", t), col("ln1_b", t),
                                             ALU.mult, ALU.add)
                head_step(b, c, HEAD_STEPS, last)

            def head_z(b, c, t):
                dve.wait_ge(dt_mm.sem, dt_mm.at(b, c * KD + t + 1))
                dve.tensor_scalar(zt[:, t], hb[c], col("bd", t), None, ALU.add).then_inc(z_done.sem, 1)

            def head_z0(b, c):
                head_z(b, c, 0)

            def head_z1(b, c):
                head_z(b, c, 1)

            def head_parts(b, c):
                dve.wait_ge(bc_mm.sem, bc_mm.at(b, c + 1))
                head_step(b, c, LE_PARTS, dve.tensor_scalar(bcf[:], hb[c][0:64], col("bbc")[0:64], None, ALU.add))
                head_step(b, c, 6, dve.tensor_copy(bcs[c][:], bcf[:]))
                head_step(b, c, 7, dve.tensor_tensor(bcs[c][32:64], bcf[32:64], bcs[c][32:64].bitcast(F32),
                                                     ALU.subtract))

            def head_softplus(b, c):
                dve.wait_ge(z_ln.sem, z_ln.at(b, c + 1))
                head_step(b, c, 8, dve.scalar_tensor_tensor(delta[c][:], zt[:], 0.0, delta[c][:],
                                                            ALU.max, ALU.add))

            def head_late(b, c):
                dve.wait_ge(le_xb.sem, le_xb.at(b, c + 1))
                dve.wait_ge(le_copy.sem, le_copy.at(b, c + 1))
                for t in range(KD):
                    last = dve.scalar_tensor_tensor(gx[:, t, c * N:(c + 1) * N], xn1[c][:, t], col("D", t),
                                                    xc[c][:, t], ALU.mult, ALU.add)
                head_step(b, c, LE_STEPS, last)
                dve.tensor_tensor(chunk(so, c), delta[c][:], xn1[c], ALU.mult).then_inc(head_done.sem, 1)

            def state_input(b, c, n):
                k = c * NS + n
                s = n % 4
                dve.wait_ge(b_mm.sem, b_mm.at(b, k + 1))
                if k >= 4:
                    dve.wait_ge(y_acc.sem, y_acc.at(b, k - 3))
                dve.tensor_tensor(u[:, s], chunk(so, c), both(psb[:, 0]), ALU.mult).then_inc(u_done.sem, 1)

            def state_scan(b, c, n):
                k = c * NS + n
                s = n % 4
                dve.wait_ge(u_done.sem, u_done.at(b, k + 1))
                dve.wait_ge(da_done.sem, da_done.at(b, k + 1))
                for t in range(KD):
                    last = dve.tensor_tensor_scan(u[:, s, t], da[:, s, t], u[:, s, t],
                                                  0.0 if c == 0 else carry[:, t, n:n + 1],
                                                  ALU.mult, ALU.add)
                last.then_inc(scan_done.sem, 1)

            def state_output(b, c, n):
                k = c * NS + n
                s = n % 4
                dve.wait_ge(scan_done.sem, scan_done.at(b, k + 1))
                if c + 1 < NC:
                    dve.tensor_copy(carry[:, :, n:n + 1], u[:, s, :, N - 1:N]).then_inc(carried.sem, 1)
                    dve.wait_ge(carried.sem, carried.at(b, n + 1))
                dve.wait_ge(c_mm.sem, c_mm.at(b, k + 1))
                dve.tensor_tensor(u[:, s], u[:, s], both(psb[:, 1]), ALU.mult).then_inc(cy_done.sem, 1)

            def lf_center(b, c):
                dve.wait_ge(lf_mean.sem, lf_mean.at(b, c + 1))
                if c == 0:
                    dve.wait_ge(da_done.sem, da_done.at(b, NS))
                else:
                    dve.wait_ge(da_done.sem, da_done.at(b, NC * NS))
                dve.tensor_tensor(nrm[c][:], chunk(so, c), both(lf_bank[c]), ALU.subtract)\
                    .then_inc(lf_cen.sem, 1)

            def lf_scale(b, c):
                dve.wait_ge(lf_rstd.sem, lf_rstd.at(b, c + 1))
                dve.tensor_tensor(nrm[c][:], nrm[c][:], both(rs3[:]), ALU.mult).then_inc(lf_step.sem, 1)
                dve.wait_ge(lf_step.sem, lf_step.at(b, 2 * c + 1))
                for t in range(KD):
                    last = dve.tensor_scalar(nrm[c][:, t], nrm[c][:, t], col("ln2_g", t), col("ln2_b", t),
                                             ALU.mult, ALU.add)
                last.then_inc(lf_step.sem, 1)

            def block_out(b, c):
                dve.wait_ge(f2_mm.sem, f2_mm.at(b, (c + 1) * KF))
                for t in range(KD):
                    part = so[:, t, c * N:(c + 1) * N]
                    last = dve.scalar_tensor_tensor(part, psb[:, t], col("b2", t), part, ALU.add, ALU.add)
                last.then_inc(block_done.sem, 1)

            def expert_norm(b, c):
                dve.wait_ge(m_rms.sem, m_rms.at(b, c + 1))
                dve.wait_ge(nf_done.sem, nf_done.at(b, c))
                dve.tensor_tensor(xrms[:], chunk(xb, c), both(rsm[:]), ALU.mult).then_inc(m_step.sem, 1)
                dve.wait_ge(m_step.sem, m_step.at(b, c + 1))
                for t in range(KD):
                    last = dve.tensor_scalar(nf[:, c, t], xrms[:, t], col("norm_w", t), None, ALU.mult)
                last.then_inc(nf_done.sem, 1)

            def expert_gate(b):
                at = 0

                def step(ins):
                    nonlocal at
                    at += 1
                    ins.then_inc(gate_step.sem, 1)
                    dve.wait_ge(gate_step.sem, gate_step.at(b, at))

                dve.wait_ge(gate_mm.sem, gate_mm.at(b, 1))
                step(dve.tensor_copy(lg16[:], psg[:, 1, 0:NJ * E].rearrange("p (j e) -> p j e", e=E)))
                step(dve.tensor_copy(lg[:], lg16[:]))
                for largest, chosen in ((gm1, first), (gm2, second)):
                    step(dve.tensor_reduce(largest[:], lg[:], AX_X, ALU.max))
                    step(dve.tensor_tensor(gtmp[:], lg[:], last8(largest[:]), ALU.is_equal))
                    step(dve.tensor_tensor(gtmp[:], gtmp[:], rank[:], ALU.mult))
                    step(dve.tensor_reduce(gix[:], gtmp[:], AX_X, ALU.max))
                    step(dve.tensor_tensor(chosen[:], gtmp[:], last8(gix[:]), ALU.is_equal))
                    if chosen is first:
                        step(dve.scalar_tensor_tensor(lg[:], first[:], -3e38, lg[:], ALU.mult, ALU.add))
                dve.tensor_tensor(gex[:], gm2[:], gm1[:], ALU.subtract).then_inc(gate_d.sem, 1)
                dve.wait_ge(gate_e.sem, gate_e.at(b, 1))
                step(dve.tensor_scalar(gw1[:], gex[:], 1.0, None, ALU.add))
                step(dve.reciprocal(gw1[:], gw1[:]))
                step(dve.tensor_scalar(gw1[:], gw1[:], A_UP, None, ALU.mult))
                step(dve.tensor_tensor(gw2[:], gex[:], gw1[:], ALU.mult))
                step(dve.tensor_tensor(first[:], first[:], last8(gw1[:]), ALU.mult))
                step(dve.tensor_tensor(second[:], second[:], last8(gw2[:]), ALU.mult))
                step(dve.tensor_tensor(comb[:, :, 0:E], first[:], second[:], ALU.add))
                assert at == GATE_STEPS
                dve.tensor_copy(comb[:, :, 32:32 + E], comb[:, :, 0:E]).then_inc(comb_done.sem, 1)

            def expert_parts(b, c):
                dve.wait_ge(comb_t.sem, comb_t.at(b, c + 1))
                dve.wait_ge(cs_done.sem, cs_done.at(b, c))
                dve.tensor_copy(ct[:], psg[0:64, 1]).then_inc(ct_done.sem, 1)
                dve.wait_ge(ct_done.sem, ct_done.at(b, 2 * c + 1))
                dve.tensor_copy(cs[:, c], ct[:]).then_inc(ct_done.sem, 1)
                dve.wait_ge(ct_done.sem, ct_done.at(b, 2 * c + 2))
                dve.tensor_tensor(cs[32:64, c], ct[32:64], cs[32:64, c].bitcast(F32), ALU.subtract)\
                    .then_inc(cs_done.sem, 1)

            def expert_clip(b, r):
                e, t = divmod(r % NQ, KD)
                bank = psy if r % 2 == 0 else psg
                dve.wait_ge(p1_mm.sem, p1_mm.at(b, r + 1))
                if r >= NB:
                    dve.wait_ge(af_done.sem, af_done.at(b, r - NB + 1))
                dve.tensor_scalar(gate[:, r % NB], bank[:, 0], mbias[:, e, 0, t:t + 1], LIMIT,
                                  ALU.add, ALU.min).then_inc(gmin_done.sem, 1)
                dve.tensor_scalar(lin[:, r % NB], bank[:, 1], lin_lo[:, e, t:t + 1], lin_hi[:, e, t:t + 1],
                                  ALU.max, ALU.min).then_inc(lin_done.sem, 1)

            def expert_product(b, r):
                e, t = divmod(r % NQ, KD)
                dve.wait_ge(sc_done.sem, sc_done.at(b, r + 1))
                dve.wait_ge(lin_done.sem, lin_done.at(b, r + 1))
                if r >= NB:
                    dve.wait_ge(alo_done.sem, alo_done.at(b, r - NB + 1))
                dve.scalar_tensor_tensor(af[:, r % NB], lin[:, r % NB], lin_one[:, e, t:t + 1],
                                         gate[:, r % NB], ALU.add, ALU.mult).then_inc(af_done.sem, 1)

            def expert_sum(b, c):
                dve.wait_ge(p2_mm.sem, p2_mm.at(b, (c + 1) * NQ))
                dve.wait_ge(moe_g.sem, moe_g.at(b, c))
                dve.tensor_scalar(sum16[:], psb[:], 1.0 / A_UP, None, ALU.mult).then_inc(moe_r.sem, 1)
                dve.wait_ge(moe_r.sem, moe_r.at(b, c + 1))
                dve.tensor_tensor(sum16[:], chunk(xb, c), sum16[:], ALU.add).then_inc(moe_s.sem, 1)

            def batch(b0, b1, last=False):
                for c in range(NC):
                    for n in range(NS):
                        late = [t - 1 for t in tasks(n) if t >= 1] if b0 is not None else []
                        if b1 is not None:
                            state_input(b1, c, n)
                        for task in late[:1]:
                            if task < KF:
                                ffn_task(b0, c, task)
                        if b1 is not None:
                            state_scan(b1, c, n)
                        for task in late[1:2]:
                            if task < KF:
                                ffn_task(b0, c, task)
                        if b1 is not None:
                            state_output(b1, c, n)
                        if b1 is not None and c == 1:
                            if n == 5:
                                lf_center(b1, 0)
                            if n == 8:
                                lf_scale(b1, 0)
                        if b0 is not None and c == 0:
                            for at, piece in ((LI_AT, l0_center), (LI_SCALE_AT, l0_scale)):
                                if n == at:
                                    piece(b0, 1)
                        if b1 is not None and c == 0:
                            for at, piece in ((5, head_center), (8, head_norm), (9, head_norm1), (10, head_z0),
                                              (11, head_z1), (12, head_parts), (13, head_softplus),
                                              (14, head_late)):
                                if n == at:
                                    piece(b1, 1)
                        for i, task in enumerate(late):
                            if i >= 2 or task >= KF:
                                ffn_task(b0, c, task)
                if b1 is not None:
                    lf_center(b1, 1)
                if b0 is not None:
                    wavelets_and_attention(b0, b1)
                else:
                    lf_scale(b1, 1)
                    expert_norm(b1, 0)
                    expert_norm(b1, 1)
                    expert_gate(b1)
                    block_out(b1, 0)
                    expert_parts(b1, 0)
                    expert_parts(b1, 1)
                if b1 is not None:
                    block_out(b1, 1)
                if b1 is None:
                    for c in range(NC):
                        lb_center(b0, c)
                        lb_scale(b0, c)
                if b1 is not None:
                    for r in range(Q + LAG):
                        if r == NQ + LAG_DOWN:
                            expert_sum(b1, 0)
                        if r < Q:
                            expert_clip(b1, r)
                        if r >= LAG:
                            expert_product(b1, r - LAG)
                        if b0 is not None:
                            for at, piece, c in ((1, lb_center, 0), (5, lb_scale, 0), (6, lb_center, 1),
                                                 (10, lb_scale, 1), (11, head_center, 0), (15, head_norm, 0),
                                                 (17, head_norm1, 0), (19, head_z0, 0), (21, head_z1, 0),
                                                 (23, head_parts, 0), (25, head_softplus, 0),
                                                 (LATE_AT + 1, head_late, 0)):
                                if r == at:
                                    piece(b0, c)
                        if b0 is not None and not last:
                            for at, piece in ((NEXT_CENTER_AT, l0_center), (NEXT_SCALE_AT, l0_scale)):
                                if r == at:
                                    piece(b0 + 1, 0)
                    expert_sum(b1, 1)
                else:
                    for piece in (head_center, head_norm, head_norm1, head_z0, head_z1, head_parts,
                                  head_softplus, head_late):
                        piece(b0, 0)
                    l0_center(b0 + 1, 0)
                    l0_scale(b0 + 1, 0)

            l0_center(0, 0)
            l0_scale(0, 0)
            batch(0, None)
            next_turn(dve, "dve")
            with dve.Fori(0, B - 2):
                batch(0, -1)
                next_turn(dve, "dve")
            batch(0, -1, last=True)
            next_turn(dve, "dve")
            batch(None, -1)


_NAMES = ("x", "pack", "w1", "w2", "h1", "h2", "w3", "wd", "wbc", "wf1", "wf2", "mlp1_w", "mlp1_b", "mlp2_w",
          "mlp2_b", "gate_w", "gate_b")


def kernel(**inputs):
    import numpy as _np
    import concourse.bacc as _bacc
    from concourse import mybir as _mybir
    from concourse.bass_utils import run_bass_kernel_spmd as _run

    g = {k: _np.asarray(v) for k, v in inputs.items()}

    def columns(v):
        v = v.reshape(v.shape[0] // P, P, -1)
        return v.transpose(1, 0, 2).reshape(P, -1)

    def stationary(w):
        return w.T.reshape(-1, P, w.shape[0]).transpose(1, 0, 2)

    vectors = {
        "h_filter": g["L0_attn_h_filter"].T, "g_filter": g["L0_attn_g_filter"].T,
        "h_synth": g["L0_attn_h_synth"].T, "g_synth": g["L0_attn_g_synth"].T,
        "gamma": g["L0_attn_norm_gamma"], "beta": g["L0_attn_norm_beta"],
        "w1_s": g["L0_ffn_w1_s"], "w2_s": g["L0_ffn_w2_s"], "h1_s": g["L0_ffn_h1_s"],
        "h2_s": g["L0_ffn_h2_s"], "w3_s": g["L0_ffn_w3_s"], "ln1_g": g["L1_attn_ln1_g"],
        "ln1_b": g["L1_attn_ln1_b"], "bd": g["L1_attn_bd"], "A_log": g["L1_attn_A_log"],
        "D": g["L1_attn_D"], "ln2_g": g["L1_attn_ln2_g"], "ln2_b": g["L1_attn_ln2_b"],
        "b1": g["L1_attn_b1"], "b2": g["L1_attn_b2"], "norm_w": g["L1_ffn_norm_weight"],
        "bbc": _np.concatenate([g["L1_attn_bbc"]] * (P // 32)),
    }
    wbc = g["L1_attn_Wbc"]
    mlp1 = g["L1_ffn_mlp1_weight"].reshape(E, D, 2, KD, P)
    mlp2 = g["L1_ffn_mlp2_weight"].reshape(E, D, KD, P)
    arrays = {
        "x": g["L0_attn_x"].reshape(B, L, KD, P).transpose(0, 3, 2, 1),
        "pack": _np.concatenate([columns(vectors[k]) for k in PACK], axis=1),
        "w1": stationary(g["L0_ffn_w1_w"]), "w2": stationary(g["L0_ffn_w2_w"]),
        "h1": stationary(g["L0_ffn_h1_w"]), "h2": stationary(g["L0_ffn_h2_w"]),
        "w3": stationary(g["L0_ffn_w3_w"]), "wd": stationary(g["L1_attn_Wd"]),
        "wbc": stationary(_np.concatenate([wbc, wbc])),
        "wf1": stationary(g["L1_attn_W1"]), "wf2": stationary(g["L1_attn_W2"]),
        "mlp1_w": mlp1.transpose(4, 0, 3, 2, 1),
        "mlp1_b": g["L1_ffn_mlp1_bias"].reshape(E, KD, P, 2).transpose(2, 0, 3, 1),
        "mlp2_w": mlp2.transpose(3, 0, 2, 1),
        "mlp2_b": g["L1_ffn_mlp2_bias"],
        "gate_w": g["L1_ffn_gate_weight"].reshape(E, KD, P).transpose(2, 1, 0),
        "gate_b": g["L1_ffn_gate_bias"].reshape(1, E),
    }
    nc = _bacc.Bacc("TRN2", target_bir_lowering=False, num_devices=1)
    aps, feed = {}, {}
    for name in _NAMES:
        v = _np.ascontiguousarray(arrays[name])
        feed[f"in_{name}"] = v
        aps[name] = nc.dram_tensor(f"in_{name}", v.shape, _mybir.dt.from_np(v.dtype), kind="ExternalInput").ap()
    aps["out"] = nc.dram_tensor("out_0", (B, P, KD, L), F32, kind="ExternalOutput").ap()
    build(nc, aps)
    r = _run(nc, [feed], core_ids=[0])
    out = r.results[0]["out_0"]
    return out.transpose(0, 3, 2, 1).reshape(B, L, D)
```
